# Optimizing a Trainium2 kernel written in Bass

```python
import numpy as np
import jax
import jax.numpy as jnp

def _softmax(x, axis=-1):
    return jax.nn.softmax(x, axis=axis)

def _gelu(x):
    return jax.nn.gelu(x, approximate=True)

def _silu(x):
    return jax.nn.silu(x)

def _sigmoid(x):
    return jax.nn.sigmoid(x)

def _layernorm(x, axis=-1, eps=1e-05):
    m = jnp.mean(x, axis=axis, keepdims=True)
    v = jnp.var(x, axis=axis, keepdims=True)
    return (x - m) / jnp.sqrt(v + eps)

def _scatter_add(tgt, idx, src, axis=0):
    return tgt.at[idx].add(src)

def _segment_sum(src, seg, n):
    return jax.ops.segment_sum(src, seg, n)
kernel_name = 'mk_gnn_preln_d4_gnn_r8_4640ee'

def setup_inputs(seed: int=0):
    np.random.seed(seed)
    _w = jnp.asarray

    def _rec_inputs():
        import jax
        import jax.numpy as jnp
        _gk = jax.random.key(seed)
        x = -0.0003713 + 1 * jax.random.normal(jax.random.fold_in(_gk, 1), (12500, 128), jnp.float32)
        src = jax.random.randint(jax.random.fold_in(_gk, 2), (200000,), 0, 12500, jnp.int32)
        dst = jnp.minimum((12500 * jax.random.uniform(jax.random.fold_in(_gk, 3), (200000,)) ** 2.0).astype(jnp.int32), 99999)
        _o = jnp.argsort(dst, stable=True)
        src = src[_o]
        dst = dst[_o]
        edge_attr_32 = 0.000189758 + 1.00013 * jax.random.normal(jax.random.fold_in(_gk, 12), (200000, 32), jnp.float32)
        edge_attr_8 = jax.random.uniform(jax.random.fold_in(_gk, 13), (200000, 8), jnp.float32, 0.0, 1)
        edge_type_460 = jax.random.randint(jax.random.fold_in(_gk, 15), (200000,), 0, 460, jnp.int32)
        return (x, src, dst, edge_attr_32, edge_attr_8, edge_type_460)
    x, src, dst, edge_attr_32, edge_attr_8, edge_type_460 = _rec_inputs()

    def _L0_gnn_setup():
        import jax, jax.numpy as jnp
        import numpy as np
        N_NODES = 12500
        N_EDGES = 200000
        IN_DIM = 128
        OUT_DIM = 128
        EDGE_DIM = 32
        EPS = 1e-05

        def _layernorm(h, gamma, beta):
            mu = jnp.mean(h, axis=-1, keepdims=True)
            var = jnp.var(h, axis=-1, keepdims=True)
            return (h - mu) * jax.lax.rsqrt(var + EPS) * gamma + beta
        key = jax.random.key(seed)
        ks = jax.random.split(key, 10)
        hid = OUT_DIM * 2
        x = jax.random.normal(ks[0], (N_NODES, IN_DIM), dtype=jnp.float32)
        edge_index = jax.random.randint(ks[1], (2, N_EDGES), 0, N_NODES, dtype=jnp.int64)
        edge_attr = jax.random.normal(ks[2], (N_EDGES, EDGE_DIM), dtype=jnp.float32)
        W1 = jax.random.normal(ks[3], (IN_DIM + EDGE_DIM, hid), dtype=jnp.float32) / np.sqrt(IN_DIM + EDGE_DIM)
        b1 = jnp.zeros((hid,), jnp.float32)
        g1 = jnp.ones((hid,), jnp.float32)
        be1 = jnp.zeros((hid,), jnp.float32)
        W2 = jax.random.normal(ks[4], (hid, OUT_DIM), dtype=jnp.float32) / np.sqrt(hid)
        b2 = jnp.zeros((OUT_DIM,), jnp.float32)
        Wu = jax.random.normal(ks[5], (IN_DIM + OUT_DIM, OUT_DIM), dtype=jnp.float32) / np.sqrt(IN_DIM + OUT_DIM)
        bu = jnp.zeros((OUT_DIM,), jnp.float32)
        gu = jnp.ones((OUT_DIM,), jnp.float32)
        beu = jnp.zeros((OUT_DIM,), jnp.float32)
        return {'x': x, 'edge_index': edge_index, 'edge_attr': edge_attr, 'W1': W1, 'b1': b1, 'g1': g1, 'be1': be1, 'W2': W2, 'b2': b2, 'Wu': Wu, 'bu': bu, 'gu': gu, 'beu': beu}
    _L0_gnn_all = _L0_gnn_setup()
    _L0_gnn_in = {k: v for k, v in _L0_gnn_all.items() if k in ('W1', 'b1', 'g1', 'be1', 'W2', 'b2', 'Wu', 'bu', 'gu', 'beu')}
    del _L0_gnn_all

    def _L1_gnn_setup():
        import jax, jax.numpy as jnp
        import numpy as np
        RRELU_SLOPE = 11.0 / 48.0
        key = jax.random.key(seed)
        ks = jax.random.split(key, 7)
        N, R, H, E, L = (6250, 460, 128, 100000, 2)
        scale = 1.0 / np.sqrt(H)
        return {'ent_emb': jax.random.normal(ks[0], (N, H), jnp.float32), 'rel_emb': jax.random.normal(ks[1], (R, H), jnp.float32), 'w_neighbor': jax.random.normal(ks[2], (L, H, H), jnp.float32) * scale, 'w_loop': jax.random.normal(ks[3], (L, H, H), jnp.float32) * scale, 'src': jax.random.randint(ks[4], (E,), 0, N, jnp.int64), 'dst': jax.random.randint(ks[5], (E,), 0, N, jnp.int64), 'etype': jax.random.randint(ks[6], (E,), 0, R, jnp.int64)}
    _L1_gnn_all = _L1_gnn_setup()
    _L1_gnn_in = {k: v for k, v in _L1_gnn_all.items() if k in ('rel_emb', 'w_neighbor', 'w_loop')}
    del _L1_gnn_all

    def _L2_gnn_setup():
        import jax, jax.numpy as jnp
        import numpy as np
        N_NODES = 12500
        N_EDGES = 200000
        D_FEAT = 128
        D_OUT = 128
        ETYPE_DIM = 8
        key = jax.random.key(seed)
        k1, k2, k3, k4, k5, k6 = jax.random.split(key, 6)
        h = jax.random.normal(k1, (N_NODES, D_FEAT), dtype=jnp.float32)
        edge_types = jax.random.uniform(k2, (N_EDGES, ETYPE_DIM), dtype=jnp.float32)
        w_attn = jax.random.normal(k3, (ETYPE_DIM, 1), dtype=jnp.float32) * (1.0 / np.sqrt(ETYPE_DIM))
        W_lin = jax.random.normal(k4, (D_OUT, D_FEAT), dtype=jnp.float32) * (1.0 / np.sqrt(D_FEAT))
        src = jax.random.randint(k5, (N_EDGES,), 0, N_NODES, dtype=jnp.int64)
        dst = jax.random.randint(k6, (N_EDGES,), 0, N_NODES, dtype=jnp.int64)
        return {'h': h, 'edge_types': edge_types, 'w_attn': w_attn, 'W_lin': W_lin, 'src': src, 'dst': dst}
    _L2_gnn_all = _L2_gnn_setup()
    _L2_gnn_in = {k: v for k, v in _L2_gnn_all.items() if k in ('w_attn', 'W_lin')}
    del _L2_gnn_all

    def _L3_gnn_setup():
        import jax, jax.numpy as jnp
        import numpy as np
        N = 12500
        E = 100000
        D_IN, D_H, D_OUT = (128, 128, 128)
        key = jax.random.key(seed)
        ks = jax.random.split(key, 8)
        x = jax.random.normal(ks[0], (N, D_IN), dtype=jnp.float32)
        edge_index = jax.random.randint(ks[1], (2, E), 0, N, dtype=jnp.int64)
        s = 1.0 / np.sqrt(D_IN)
        W1 = jax.random.uniform(ks[2], (D_H, D_IN), minval=-s, maxval=s, dtype=jnp.float32)
        b1 = jax.random.uniform(ks[3], (D_H,), minval=-s, maxval=s, dtype=jnp.float32)
        sh = 1.0 / np.sqrt(D_H)
        W2 = jax.random.uniform(ks[4], (D_H, D_H), minval=-sh, maxval=sh, dtype=jnp.float32)
        b2 = jax.random.uniform(ks[5], (D_H,), minval=-sh, maxval=sh, dtype=jnp.float32)
        W3 = jax.random.uniform(ks[6], (D_OUT, D_H), minval=-sh, maxval=sh, dtype=jnp.float32)
        b3 = jax.random.uniform(ks[7], (D_OUT,), minval=-sh, maxval=sh, dtype=jnp.float32)
        return {'x': x, 'edge_index': edge_index, 'W1': W1, 'b1': b1, 'W2': W2, 'b2': b2, 'W3': W3, 'b3': b3}
    _L3_gnn_all = _L3_gnn_setup()
    _L3_gnn_in = {k: v for k, v in _L3_gnn_all.items() if k in ('W1', 'b1', 'W2', 'b2', 'W3', 'b3')}
    del _L3_gnn_all
    return {'x': x, 'src': src, 'dst': dst, 'edge_attr_32': edge_attr_32, 'edge_attr_8': edge_attr_8, 'edge_type_460': edge_type_460, 'L0_gnn_W1': _L0_gnn_in['W1'], 'L0_gnn_b1': _L0_gnn_in['b1'], 'L0_gnn_g1': _L0_gnn_in['g1'], 'L0_gnn_be1': _L0_gnn_in['be1'], 'L0_gnn_W2': _L0_gnn_in['W2'], 'L0_gnn_b2': _L0_gnn_in['b2'], 'L0_gnn_Wu': _L0_gnn_in['Wu'], 'L0_gnn_bu': _L0_gnn_in['bu'], 'L0_gnn_gu': _L0_gnn_in['gu'], 'L0_gnn_beu': _L0_gnn_in['beu'], 'L1_gnn_rel_emb': _L1_gnn_in['rel_emb'], 'L1_gnn_w_neighbor': _L1_gnn_in['w_neighbor'], 'L1_gnn_w_loop': _L1_gnn_in['w_loop'], 'L2_gnn_w_attn': _L2_gnn_in['w_attn'], 'L2_gnn_W_lin': _L2_gnn_in['W_lin'], 'L3_gnn_W1': _L3_gnn_in['W1'], 'L3_gnn_b1': _L3_gnn_in['b1'], 'L3_gnn_W2': _L3_gnn_in['W2'], 'L3_gnn_b2': _L3_gnn_in['b2'], 'L3_gnn_W3': _L3_gnn_in['W3'], 'L3_gnn_b3': _L3_gnn_in['b3']}

def reference(x, src, dst, edge_attr_32, edge_attr_8, edge_type_460, L0_gnn_W1, L0_gnn_b1, L0_gnn_g1, L0_gnn_be1, L0_gnn_W2, L0_gnn_b2, L0_gnn_Wu, L0_gnn_bu, L0_gnn_gu, L0_gnn_beu, L1_gnn_rel_emb, L1_gnn_w_neighbor, L1_gnn_w_loop, L2_gnn_w_attn, L2_gnn_W_lin, L3_gnn_W1, L3_gnn_b1, L3_gnn_W2, L3_gnn_b2, L3_gnn_W3, L3_gnn_b3):
    import jax
    import jax.numpy as jnp

    def _L0_gnn_ref(x, edge_index, edge_attr, W1, b1, g1, be1, W2, b2, Wu, bu, gu, beu):
        import jax, jax.numpy as jnp
        import numpy as np
        N_NODES = 12500
        N_EDGES = 200000
        IN_DIM = 128
        OUT_DIM = 128
        EDGE_DIM = 32
        EPS = 1e-05

        def _layernorm(h, gamma, beta):
            mu = jnp.mean(h, axis=-1, keepdims=True)
            var = jnp.var(h, axis=-1, keepdims=True)
            return (h - mu) * jax.lax.rsqrt(var + EPS) * gamma + beta
        row, col = (edge_index[0], edge_index[1])
        msg_in = jnp.concatenate([x[row], edge_attr], axis=-1)
        h = msg_in @ W1 + b1
        h = jax.nn.gelu(_layernorm(h, g1, be1), approximate=False)
        msg = h @ W2 + b2
        agg = jax.ops.segment_sum(msg, col, num_segments=x.shape[0])
        u = jnp.concatenate([x, agg], axis=-1) @ Wu + bu
        u = jax.nn.gelu(_layernorm(u, gu, beu), approximate=False)
        return u + x

    def _L1_gnn_ref(ent_emb, rel_emb, w_neighbor, w_loop, src, dst, etype):
        import jax, jax.numpy as jnp
        import numpy as np
        RRELU_SLOPE = 11.0 / 48.0
        n = ent_emb.shape[0]
        n_layers = w_neighbor.shape[0]
        deg = jax.ops.segment_sum(jnp.ones(dst.shape, ent_emb.dtype), dst, num_segments=n)
        norm = jnp.where(deg > 0, 1.0 / jnp.maximum(deg, 1.0), 0.0)[:, None]
        h = ent_emb
        for i in range(n_layers):
            msg = (h[src] + rel_emb[etype]) @ w_neighbor[i]
            agg = jax.ops.segment_sum(msg, dst, num_segments=n) * norm
            pre = agg + h @ w_loop[i]
            h = jnp.where(pre >= 0, pre, RRELU_SLOPE * pre)
        return h

    def _L2_gnn_ref(h, edge_types, w_attn, W_lin, src, dst):
        import jax, jax.numpy as jnp
        import numpy as np
        N_NODES = 12500
        N_EDGES = 200000
        D_FEAT = 128
        D_OUT = 128
        ETYPE_DIM = 8
        N = h.shape[0]
        e_type_tanh = jnp.tanh(edge_types @ w_attn)
        sum_tanh = jax.ops.segment_sum(e_type_tanh, dst, num_segments=N)
        e_type_w = sum_tanh / N
        beta = jax.nn.softmax(e_type_w, axis=1)
        msg_sum = jax.ops.segment_sum(h[src], dst, num_segments=N)
        h_agg = beta * msg_sum
        return h_agg @ W_lin.T

    def _L3_gnn_ref(x, edge_index, W1, b1, W2, b2, W3, b3):
        import jax, jax.numpy as jnp
        import numpy as np
        N = 12500
        E = 100000
        D_IN, D_H, D_OUT = (128, 128, 128)
        row, col = (edge_index[0], edge_index[1])
        n = x.shape[0]
        deg = jnp.clip(jax.ops.segment_sum(jnp.ones_like(row, dtype=x.dtype), row, num_segments=n), 1.0)

        def mp(h):
            agg = jax.ops.segment_sum(h[col], row, num_segments=n)
            return jax.nn.relu(agg / deg[:, None])
        h = mp(x @ W1.T + b1)
        h = mp(h @ W2.T + b2)
        return h @ W3.T + b3
    edge_index = jnp.stack([src, dst])
    h = jnp.maximum(_layernorm(x, axis=-1), 0.0)
    x = x + _L0_gnn_ref(h, edge_index, edge_attr_32, L0_gnn_W1, L0_gnn_b1, L0_gnn_g1, L0_gnn_be1, L0_gnn_W2, L0_gnn_b2, L0_gnn_Wu, L0_gnn_bu, L0_gnn_gu, L0_gnn_beu)
    h = jnp.maximum(_layernorm(x, axis=-1), 0.0)
    x = x + _L1_gnn_ref(h, L1_gnn_rel_emb, L1_gnn_w_neighbor, L1_gnn_w_loop, src, dst, edge_type_460)
    h = jnp.maximum(_layernorm(x, axis=-1), 0.0)
    x = x + _L2_gnn_ref(h, edge_attr_8, L2_gnn_w_attn, L2_gnn_W_lin, src, dst)
    h = jnp.maximum(_layernorm(x, axis=-1), 0.0)
    x = x + _L3_gnn_ref(h, edge_index, L3_gnn_W1, L3_gnn_b1, L3_gnn_W2, L3_gnn_b2, L3_gnn_W3, L3_gnn_b3)
    return x

_drawn_inputs = setup_inputs


def setup_inputs(seed=0):
    import zlib

    import numpy as np

    out = dict(_drawn_inputs(seed))
    spreads = {'L0_gnn_b1': (0.0, 0.1),
     'L0_gnn_g1': (1.0, 0.2),
     'L0_gnn_be1': (0.0, 0.1),
     'L0_gnn_b2': (0.0, 0.1),
     'L0_gnn_bu': (0.0, 0.663),
     'L0_gnn_gu': (1.0, 0.2),
     'L0_gnn_beu': (0.0, 0.1)}
    factors = {'edge_attr_32': 2.728,
     'L3_gnn_W1': 8.0,
     'L3_gnn_b1': 8.0,
     'L3_gnn_W2': 8.0,
     'L3_gnn_b2': 8.0,
     'L3_gnn_W3': 8.0,
     'L3_gnn_b3': 8.0}
    for name, (base, spread) in spreads.items():
        noise = np.random.default_rng([zlib.crc32(name.encode()), seed]).standard_normal(out[name].shape)
        drawn = base * np.exp(spread * noise) if base else spread * noise
        out[name] = jnp.asarray(drawn.astype(out[name].dtype))
    for name, factor in factors.items():
        out[name] = (out[name] * factor).astype(out[name].dtype)
    return out
```

```python
from contextlib import ExitStack

import concourse.bass as bass
from concourse import mybir

P = 128
N = 12500
E = 200000
D = 128
HID = 256
ED = 32
NB = -(-N // P)
NPAD = NB * P
W = 8
C = -(-E // (P * W)) * W
CT = C // W
LAST = E - (P - 1) * C
T = -(-(E // P + NB) // (2 * W)) * 2 * W
TT = T // W
ROWS = T + W
RD = 4 + ED
RS = 2
ACCW = (NB + 1) * P
B = 7
NT = NB // B
BW = B * D
TRASH = P - 1
EPS = 1e-5
SLOPE = 11.0 / 48.0

assert NB % B == 0 and LAST % W == 0 and LAST > 0 and CT % 2 == 0 and TT % 2 == 0
assert T >= (E + NB * (P - 1)) // P + 1 and ROWS - T >= (P * C - E) // P + 2

F32 = mybir.dt.float32
BF16 = mybir.dt.bfloat16
I32 = mybir.dt.int32
ALU = mybir.AluOpType
ACT = mybir.ActivationFunctionType
AX = mybir.AxisListType.X

STAGES = 99


def build(nc, A, out):
    ctx = ExitStack()
    with ctx:
        def sb(name, shape, dt=F32):
            return ctx.enter_context(nc.sbuf_tensor(name, shape, dt))

        def sem(name):
            return ctx.enter_context(nc.semaphore(name))

        def dram(name, shape, dt=F32):
            return nc.dram_tensor(name, shape, dt).ap()

        rec_d = dram("rec_d", [P * ROWS, RD])
        rec_s = dram("rec_s", [P * ROWS, RS])
        tab_p = dram("tab_p", [NPAD, HID])
        x_pad = dram("x_pad", [NPAD, D])
        x1, x2, x3 = (dram(f"x{k}_rows", [NPAD, D]) for k in (1, 2, 3))
        h1, h2, h4, g1t, g2t = (dram(n, [NPAD, D]) for n in ("h1_rows", "h2_rows", "h4_rows", "l3a_rows", "l3b_rows"))

        acc = sb("acc", [P, 2 * ACCW])
        acc2 = acc[:, :].rearrange("p (a n) -> p a n", a=2)
        idx_d = sb("idx_d", [P, T + W], I32)
        ety_d = sb("ety_d", [P, T + W], I32)
        loc_d = sb("loc_d", [P, T])
        idx_s = sb("idx_s", [P, T + W], I32)
        loc_s = sb("loc_s", [P, T])
        off_d = sb("off_d", [32, T], I32)
        off_s = sb("off_s", [32, T], I32)
        work = sb("work", [P, 10000])

        consts = sb("consts", [P, 4 * P])
        ident, iota, lower, mask = (consts[:, k * P:(k + 1) * P] for k in range(4))
        cbf = sb("cbf", [P, 5 * P], BF16)
        ident_b, iota_b, lower_b, mask_b, rest_b = (cbf[:, k * P:(k + 1) * P] for k in range(5))
        ones_b = sb("ones_b", [P, P], BF16)
        w1a = sb("w1a", [P, HID])
        w1b = sb("w1b", [ED, HID])
        rows256 = sb("rows256", [P, 3, HID])
        rows128 = sb("rows128", [P, 6, D])
        b2col = sb("b2col", [P, 1])
        attn = sb("attn", [P, W])
        w2 = sb("w2", [P, 2, D])
        wu = sb("wu", [P, 2, D])
        wn = sb("wn", [P, 2, D])
        wl = sb("wl", [P, 2, D])
        lin = sb("lin", [P, 4, D])
        linT = sb("linT", [P, 4, D])
        w2u = sb("w2u", [P, 2, D])
        vrow = sb("vrow", [P, D])
        deg_d = sb("deg_d", [P, P])
        deg_s = sb("deg_s", [P, P])
        beta = sb("beta", [P, P])
        norm_d = sb("norm_d", [P, P])
        small = sb("small", [P, 64])

        pair = [ctx.enter_context(nc.psum_tensor(f"pair{k}", [P, 1024], F32)) for k in range(4)]

        def acc_view(at, n):
            return acc[:, at:at + n]
        src_i, dst_i, ety_i, blk_d, lod, blk_s, los, tanh_c = (acc_view(k * C, C) for k in range(8))
        src_i, dst_i, ety_i = (v.bitcast(I32) for v in (src_i, dst_i, ety_i))
        FILL = ROWS // 8
        fill_d = acc_view(8 * C, FILL * RD)
        fill_s = acc_view(8 * C + FILL * RD, FILL * RS)
        trow = acc_view(8 * C + FILL * (RD + RS), T)
        tcol_i = fill_d[:, 0:C].bitcast(I32)

        at = [0]

        def ws(n, dt=F32):
            v = work[:, at[0]:at[0] + n]
            at[0] += n
            return v if dt == F32 else v.bitcast(dt)

        oh = [ws(W // 2 * P // 2, BF16) for _ in range(2)]
        ohl = [ws(W // 2 * P // 2, BF16) for _ in range(2)]
        oht = [ws(W // 2 * P) for _ in range(2)]
        ohf = [ws(W // 2 * P) for _ in range(2)]
        prod = ohf
        cnt = ws(W * P)
        base = ws(W * P)
        base_i = ws(W * P, I32)
        part = [ws(W * P // 2, BF16) for _ in range(3)]
        cmp_b = ws(T // 2, BF16)
        ping = [ws(P) for _ in range(2)]
        assert at[0] <= 10000
        pay_d = [oht[k][:, 0:W * RD] for k in range(2)]
        pay_s = [oht[k][:, W * RD:W * (RD + RS)] for k in range(2)]
        pos = small[:, 0:8]
        pos_i = [small[:, 8 * k:8 * k + 8].bitcast(I32) for k in (1, 2, 3)]
        row_i = [small[:, 8 * k:8 * k + 8].bitcast(I32) for k in (4, 5)]
        chunk8 = cnt
        at[0] = 0
        ring = ws(W * HID)
        ring3 = ring.rearrange("p (k f) -> p k f", k=W)
        ring128 = ring[:, 0:W * D].rearrange("p (k f) -> p k f", k=W)
        sel = [ws(W // 2 * P) for _ in range(2)]
        recs = [ws(W * RD) for _ in range(2)]
        eaT = ws(W // 2 * P)
        zs = [ws(W // 2 * HID) for _ in range(1)][0]
        zn = [ws(W // 2 * HID) for _ in range(2)]
        sq = ws(HID)
        assert at[0] <= 10000
        idx_r = [small[:, 8 * k:8 * k + 8].bitcast(I32) for k in (0, 1)]
        ssq = small[:, 16:20]
        at[0] = 0
        X, H, HT, TMP, TM2 = (ws(BW) for _ in range(5))
        AG = ws(2 * BW)
        OUT = ws(B * HID)
        assert at[0] <= 10000
        st1, st2, st3 = small[:, 32:39], small[:, 40:47], small[:, 48:55]

        def cols(ap, k, n=P):
            return ap[:, k * n:(k + 1) * n]

        weights_in = sem("weights_in")
        edges_in = sem("edges_in")
        ea8_in = sem("ea8_in")
        fill_ready = sem("fill_ready")
        fills_done = sem("fills_done")
        dve_step = sem("dve_step")
        act_step = sem("act_step")
        tanh_dot = sem("tanh_dot")
        tanh_ready = sem("tanh_ready")
        onehots_ready = sem("onehots_ready")
        counted = sem("counted")
        cmp_ready = sem("cmp_ready")
        blocks_in_psum = sem("blocks_in_psum")
        blocks_read = sem("blocks_read")
        seeds_ready = sem("seeds_ready")
        rank_onehots = sem("rank_onehots")
        ranks_in_psum = sem("ranks_in_psum")
        ranks_read = sem("ranks_read")
        carried = sem("carried")
        payload_cleared = sem("payload_cleared")
        payload_ready = sem("payload_ready")
        ea_in = [sem(f"ea_in{k}") for k in range(2)]
        scattered = [sem(f"scattered{k}") for k in range(2)]
        pool_turn = sem("pool_turn")
        sp_turn = sem("sp_turn")
        regrouped = sem("regrouped")
        columns_ready = sem("columns_ready")
        w_psum = sem("w_psum")
        w_ready = sem("w_ready")
        beta_ready = sem("beta_ready")
        beta_exp = sem("beta_exp")
        idx_copied = sem("idx_copied")
        gathered = [sem(f"gathered{k}") for k in range(W)]
        sel_ready = sem("sel_ready")
        sums_in_psum = sem("sums_in_psum")
        sums_added = sem("sums_added")
        acc_ready = sem("acc_ready")
        recs_in = [sem(f"recs_in{k}") for k in range(2)]
        eaT_in_psum = sem("eaT_in_psum")
        eaT_ready = sem("eaT_ready")
        edge_part = sem("edge_part")
        z_ready = sem("z_ready")
        squares = sem("squares")
        z_scaled = sem("z_scaled")
        gelu_ready = sem("gelu_ready")
        rows_loaded = sem("rows_loaded")
        h_ready = sem("h_ready")
        hT_in_psum = sem("hT_in_psum")
        hT_ready = sem("hT_ready")
        sums_copied = sem("sums_copied")
        product = sem("product")
        product2 = sem("product2")
        pre_gelu = sem("pre_gelu")
        post_gelu = sem("post_gelu")
        result_ready = sem("result_ready")
        rows_stored = sem("rows_stored")

        def wait(eng, s, value):
            if not (isinstance(value, int) and value <= 0):
                eng.wait_ge(s, value)

        class Chain:

            def __init__(self, eng, s):
                self.eng, self.s, self.done, self.k, self.at = eng, s, 0, 0, 0

            def turn(self, i, per):
                self.at, self.k, self.per = self.done + i * per, 0, per

            def link(self, ins):
                self.k += 1
                ins.then_inc(self.s, 1)
                self.eng.wait_ge(self.s, self.at + self.k)

            def end(self):
                assert self.k == self.per, (self.k, self.per)

            def over(self, turns):
                self.done += turns * self.per

            def straight(self, ins):
                self.done += 1
                ins.then_inc(self.s, 1)
                self.eng.wait_ge(self.s, self.done)

        def loop(eng, n, body, peel_first=False, peel_last=False):
            lo, hi = int(peel_first), n - int(peel_last)
            if peel_first:
                body(0)
            with eng.Fori(lo, hi) as i:
                body(i)
            if peel_last:
                body(n - 1)

        PASSES = [(A["L1_gnn_rel_emb"], ety_d, loc_d, off_d), (h1, idx_d, loc_d, off_d),
                  (h2, idx_d, loc_d, off_d), (h4, idx_d, loc_d, off_d),
                  (g1t, idx_s, loc_s, off_s), (g2t, idx_s, loc_s, off_s)]
        STORES = [2, 2, 1, 2, 2, 1, 1]
        LOADS = [1, 1, 1, 2, 1, 0, 1]

        def stored(n, j=0):
            extra = 16 * STORES[n] * j if not isinstance(j, int) or j else 0
            return 16 * NT * sum(STORES[:n]) + extra

        def loaded(n, j=0):
            return 16 * NT * sum(LOADS[:n]) + (NX if n > 0 else 0) + 16 * LOADS[n] * j
        NX = 16

        def table_done(n):
            return stored(n + 1)

        block = ctx.enter_context(nc.Block())

        @block.sync
        def _(sp):
            def row(name):
                return A[name].rearrange("(a f) -> a f", a=1)

            loads = [(consts[:, :], A["shape_consts"]), (w1a[:, :], A["L0_gnn_W1"][0:D, :]),
                     (w1b[:, :], A["L0_gnn_W1"][D:D + ED, :]),
                     (b2col[:, :], A["L0_gnn_b2"].rearrange("(f a) -> f a", a=1)),
                     (attn[:, :], A["L2_gnn_w_attn"].rearrange("k a -> a k").to_broadcast([P, W])),
                     (w2[:, :, :], A["L0_gnn_W2"].rearrange("(a p) f -> p a f", a=2)),
                     (wu[:, :, :], A["L0_gnn_Wu"].rearrange("(a p) f -> p a f", a=2)),
                     (wn[:, :, :], A["L1_gnn_w_neighbor"].rearrange("a p f -> p a f")),
                     (wl[:, :, :], A["L1_gnn_w_loop"].rearrange("a p f -> p a f")),
                     (trow, A["tile_numbers"].to_broadcast([P, T]))]
            loads += [(rows256[:, k, :], row(n).to_broadcast([P, HID]))
                      for k, n in enumerate(("L0_gnn_b1", "L0_gnn_g1", "L0_gnn_be1"))]
            loads += [(rows128[:, k, :], row(n).to_broadcast([P, D])) for k, n in enumerate(
                ("L0_gnn_bu", "L0_gnn_gu", "L0_gnn_beu", "L3_gnn_b1", "L3_gnn_b2", "L3_gnn_b3"))]
            loads += [(lin[:, k, :], A[n]) for k, n in enumerate(
                ("L2_gnn_W_lin", "L3_gnn_W1", "L3_gnn_W2", "L3_gnn_W3"))]
            for dst, src in loads:
                with nc.allow_non_contiguous_dma(reason="a column of 128 biases"):
                    sp.dma_start(dst, src).then_inc(weights_in, 16)
            assert len(loads) == 23
            sp.wait_ge(fill_ready, 1)
            for v, name in ((src_i, "src"), (dst_i, "dst"), (ety_i, "edge_type_460")):
                sp.dma_start(v[0:P - 1, :], A[name][0:(P - 1) * C].rearrange("(p c) -> p c", c=C)).then_inc(edges_in, 16)
                sp.dma_start(v[P - 1:P, 0:LAST], A[name][(P - 1) * C:E].rearrange("(a c) -> a c", a=1)).then_inc(edges_in, 16)
            sp.wait_ge(fill_ready, 2)
            fd = rec_d.rearrange("(p r) w -> p (r w)", p=P)
            fs = rec_s.rearrange("(p r) w -> p (r w)", p=P)
            for k in range(8):
                sp.dma_start(fd[:, k * FILL * RD:(k + 1) * FILL * RD], fill_d).then_inc(fills_done, 16)
                sp.dma_start(fs[:, k * FILL * RS:(k + 1) * FILL * RS], fill_s).then_inc(fills_done, 16)
            for q in range(NE8):
                if q:
                    sp.wait_ge(tanh_dot, q)
                n = CE8
                c0 = q * n
                sp.dma_start(chunk8[0:P - 1, 0:n * W], A["edge_attr_8"][0:(P - 1) * C, :].rearrange("(p c) k -> p (c k)", c=C)[:, c0 * W:(c0 + n) * W]).then_inc(ea8_in, 16)
                m = max(0, min(LAST - c0, n))
                if m:
                    a0 = (P - 1) * C + c0
                    sp.dma_start(chunk8[P - 1:P, 0:m * W], A["edge_attr_8"][a0:a0 + m, :].rearrange("(a c) k -> a (c k)", a=1)).then_inc(ea8_in, 16)
                else:
                    sp.dma_start(chunk8[P - 1:P, 0:W], A["edge_attr_8"][0:1, :]).then_inc(ea8_in, 16)

            ea = A["edge_attr_32"]
            top, mid = 112, P - 1
            ea_top = ea[0:top * C, :].rearrange("(p c) f -> p c f", c=C)
            ea_mid = ea[top * C:mid * C, :].rearrange("(p c) f -> p c f", c=C)
            ea_low = ea[mid * C:E, :].rearrange("(a c) f -> a c f", a=1)

            def feed(j, low):
                for k in range(2):
                    c0 = (2 * j + k) * W
                    wait(sp, scattered[k], 16 * W * j)
                    v = pay_d[k].rearrange("p (c w) -> p c w", c=W)
                    sp.dma_start(v[0:top, :, 4:RD], ea_top[:, bass.ds(c0, W), :]).then_inc(ea_in[k], 16)
                    sp.dma_start(v[top:mid, :, 4:RD], ea_mid[:, bass.ds(c0, W), :]).then_inc(ea_in[k], 16)
                    if low:
                        sp.dma_start(v[mid:P, :, 4:RD], ea_low[:, bass.ds(c0, W), :]).then_inc(ea_in[k], 16)
            sp.wait_ge(payload_cleared, 1)
            feed(0, True)
            with sp.Fori(1, LAST // W // 2) as j:
                feed(j, True)
            with sp.Fori(LAST // W // 2, CT // 2) as j:
                feed(j, False)

            for k in range(2):
                sp.wait_ge(scattered[k], 16 * W * CT // 2)
            rd = rec_d.rearrange("(p r) w -> p (r w)", p=P)
            for q in range(NRB):
                if q:
                    sp.wait_ge(columns_ready, q)
                sp.dma_start(fill_d[:, 0:T // NRB * RD], rd[:, q * (T // NRB) * RD:(q + 1) * (T // NRB) * RD]).then_inc(regrouped, 16)
            for k in range(2):
                sp.wait_ge(scattered[k], 16 * W * CT)
            sp.wait_ge(columns_ready, NRB)
            sp.dma_start(fill_d[:, 0:T * RS], rec_s.rearrange("(p r) w -> p (r w)", p=P)[:, 0:T * RS]).then_inc(regrouped, 16)

            def node_rows(t, j):
                return t[bass.ds(j * B * P, B * P), :].rearrange("(b p) f -> p b f", p=P)

            def seven(v):
                return v.rearrange("p (b f) -> p b f", b=B)

            FULL = B - 1
            NR = N - (NB - 1) * P

            def stage(n, load, store):
                def body(j):
                    if n > 0 or not (isinstance(j, int) and j == 0):
                        wait(sp, rows_stored, stored(n, j))
                        sp.sem_inc(sp_turn)
                    load(j)
                    store(j)
                loop(sp, NT, body, peel_first=n == 0, peel_last=n in (0, 6))

            def load_x(src):
                return lambda j: sp.dma_start(seven(X), node_rows(src, j)).then_inc(rows_loaded, 16)

            def load0(j):
                if isinstance(j, int) and j == NT - 1:
                    r0 = j * B * P
                    sp.dma_start(seven(X)[:, 0:FULL, :], A["x"][r0:r0 + FULL * P, :].rearrange("(b p) f -> p b f", p=P)).then_inc(rows_loaded, 16)
                    sp.dma_start(seven(X)[0:NR, FULL, :], A["x"][r0 + FULL * P:N, :]).then_inc(rows_loaded, 16)
                else:
                    sp.dma_start(seven(X), node_rows(A["x"], j)).then_inc(rows_loaded, 16)

            def store0(j):
                sp.wait_ge(rows_loaded, (16 + 16 * j) if not (isinstance(j, int) and j == NT - 1) else 16 * NT + NX)
                sp.dma_start(node_rows(x_pad, j), seven(X)).then_inc(rows_stored, 16)
                sp.wait_ge(result_ready, 1 + j)
                sp.dma_start(node_rows(tab_p, j), seven(OUT)).then_inc(rows_stored, 16)
            sp.wait_ge(columns_ready, NRB + 1)
            sp.wait_ge(carried, 4 * CT)
            stage(0, load0, store0)

            rdt = rec_d.rearrange("(p r) w -> p (r w)", p=P)

            def edge_recs(j):
                for k in range(2):
                    t = 2 * j + k
                    wait(sp, eaT_in_psum, 2 * t - 2)
                    sp.dma_start(recs[k], rdt[:, bass.ds(t * (W * RD), W * RD)]).then_inc(recs_in[k], 16)
            sp.wait_ge(rows_stored, stored(1))
            loop(sp, TT // 2, edge_recs, peel_first=True)
            if STAGES < 2:
                return

            def results(n, first, second=None):
                m = 2 if second is not None else 1

                def body(j):
                    base_r = RES[n]
                    sp.wait_ge(result_ready, base_r + 1 + m * j)
                    sp.dma_start(node_rows(first[0], j), seven(first[1])).then_inc(rows_stored, 16)
                    if second is not None:
                        sp.wait_ge(result_ready, base_r + 2 + m * j)
                        sp.dma_start(node_rows(second[0], j), seven(second[1])).then_inc(rows_stored, 16)
                return body

            sp.wait_ge(sums_added, 2 * TT)
            stage(1, load_x(x_pad), results(1, (x1, TM2), (h1, H)))

            def load_h(src, second=None):
                def body(j):
                    sp.dma_start(seven(H), node_rows(src, j)).then_inc(rows_loaded, 16)
                    if second is not None:
                        sp.dma_start(seven(X), node_rows(second, j)).then_inc(rows_loaded, 16)
                return body
            sp.wait_ge(sums_added, 6 * TT)
            stage(2, load_h(h1), results(2, (h2, TM2)))
            sp.wait_ge(sums_added, 8 * TT)
            stage(3, load_h(h2, x1), results(3, (x2, TM2), (h4, HT)))
            sp.wait_ge(sums_added, 10 * TT)
            stage(4, load_x(x2), results(4, (x3, TM2), (g1t, TMP)))
            sp.wait_ge(sums_added, 12 * TT)
            stage(5, lambda j: None, results(5, (g2t, TM2)))
            sp.wait_ge(sums_added, 14 * TT)

            def last_rows(j):
                sp.wait_ge(result_ready, RES[6] + 1 + j)
                if isinstance(j, int):
                    r0 = j * B * P
                    sp.dma_start(out[r0:r0 + FULL * P, :].rearrange("(b p) f -> p b f", p=P), seven(TM2)[:, 0:FULL, :]).then_inc(rows_stored, 16)
                    sp.dma_start(out[r0 + FULL * P:N, :], seven(TM2)[0:NR, FULL, :]).then_inc(rows_stored, 16)
                else:
                    sp.dma_start(node_rows(out, j), seven(TM2)).then_inc(rows_stored, 16)
            stage(6, load_x(x3), last_rows)
            sp.wait_ge(rows_stored, stored(7) + 16)

        @block.gpsimd
        def _(pool):
            def admitted():
                pool.sem_inc(pool_turn)

            pool.wait_ge(fills_done, 16 * 16)

            def scatter(j, rec, pay, words, first, dst):
                for k in range(2):
                    wait(pool, payload_ready, first + 2 * j + k + 1)
                    if dst:
                        wait(pool, ea_in[k], dst(j))
                    admitted()
                    v = pay[k].rearrange("p (c w) -> p c w", c=W)
                    for c in range(W):
                        pool.indirect_dma_start(
                            out=rec[:, :], out_offset=bass.IndirectOffsetOnAxis(ap=row_i[k][:, c:c + 1], axis=0),
                            in_=v[:, c, :], in_offset=None).then_inc(scattered[k], 16)
            lowj = LAST // W // 2
            loop(pool, lowj, lambda j: scatter(j, rec_d, pay_d, RD, 0, lambda j: 48 * (j + 1)))
            with pool.Fori(lowj, CT // 2) as j:
                scatter(j, rec_d, pay_d, RD, 0, lambda j: 48 * lowj + 32 * (j - lowj + 1))
            loop(pool, CT // 2, lambda j: scatter(j, rec_s, pay_s, RS, CT, None))

            def gathers(n, table, idx, dst):
                g0 = 2 * TT * n

                def copy(i, k):
                    pool.tensor_copy(idx_r[k], idx[:, bass.ds(i * W, W)]).then_inc(idx_copied, 1)
                wait(pool, idx_copied, n * (TT + 1))
                copy(0, 0)

                def turn2(j):
                    for k in range(2):
                        i = 2 * j + k
                        for h in range(2):
                            wait(pool, sums_in_psum, g0 + 2 * i + h - 1)
                            if h == 1:
                                admitted()
                                copy(i + 1, 1 - k)
                            else:
                                wait(pool, idx_copied, n * (TT + 1) + i + 1)
                                admitted()
                            for c in range(4 * h, 4 * h + 4):
                                pool.indirect_dma_start(
                                    out=dst[:, c, :], out_offset=None, in_=table[:, :],
                                    in_offset=bass.IndirectOffsetOnAxis(ap=idx_r[k][:, c:c + 1], axis=0)).then_inc(gathered[c], 16)
                loop(pool, TT // 2, turn2, peel_first=True)
            pool.wait_ge(rows_stored, table_done(0))
            gathers(0, tab_p, idx_d, ring3)
            if STAGES < 2:
                return
            for n, (table, idx, _, _) in enumerate(PASSES):
                pool.wait_ge(rows_stored, table_done(1 if n < 2 else n))
                if n == 1:
                    pool.wait_ge(sums_in_psum, 4 * TT)
                gathers(n + 1, table, idx, ring128)

        @block.scalar
        def _(act):
            act.wait_ge(tanh_dot, NE8)
            nc.scalar.activation(tanh_c, tanh_c, ACT.Tanh).then_inc(tanh_ready, 1)
            act.wait_ge(beta_ready, 1)
            nc.scalar.activation(beta[:, 0:NB], beta[:, 0:NB], ACT.Exp).then_inc(beta_exp, 1)
            act.wait_ge(w_psum, 1)
            nc.scalar.copy(linT[:, :, :].rearrange("p a f -> p (a f)"), pair[3][:, 0:4 * D]).then_inc(w_ready, 1)
            act.wait_ge(columns_ready, NRB + 1)
            nc.scalar.copy(TMP[:, 0:2 * D], pair[3][:, 512:512 + 2 * D]).then_inc(w_ready, 1)
            act.wait_ge(w_psum, 2)
            nc.scalar.copy(w2u[:, :, :].rearrange("p a f -> p (a f)"), pair[2][:, 0:2 * D]).then_inc(w_ready, 1)
            nc.scalar.copy(vrow[:, :], pair[2][:, 2 * D:3 * D]).then_inc(w_ready, 1)

            def transposed(at, j):
                act.wait_ge(hT_in_psum, at + 1 + j)
                nc.scalar.copy(HT, pair[0][:, 0:BW]).then_inc(hT_ready, 1)

            def sums(at, j, halves, func=ACT.Copy):
                v = acc2[:, 2 - halves:2, bass.ds(j * BW, BW)]
                nc.scalar.activation(AG[:, 0:halves * BW].rearrange("p (a n) -> p a n", a=halves), v, func).then_inc(sums_copied, 1)

            loop(act, NT, lambda j: transposed(0, j), peel_first=True)

            def tile4(j):
                for k in range(2):
                    for h in range(2):
                        q = 4 * j + 2 * k + h
                        act.wait_ge(eaT_in_psum, q + 1)
                        wait(act, edge_part, q)
                        nc.scalar.copy(eaT[0:ED, :], pair[3][0:ED, 0:4 * P]).then_inc(eaT_ready, 1)
                        act.wait_ge(z_ready, q + 1)
                        for c in range(4):
                            last = nc.scalar.activation(sq, cols(zs, c, HID), ACT.Square, accum_out=ssq[:, c:c + 1])
                            last.then_inc(act_step, 1)
                            act.wait_ge(act_step, 4 * q + c + 1)
                        act.sem_inc(squares)
                        act.wait_ge(z_scaled, q + 1)
                        nc.scalar.activation(zn[h], zn[h], ACT.Gelu).then_inc(gelu_ready, 1)
            act.wait_ge(rows_stored, stored(1))
            loop(act, TT // 2, tile4, peel_first=True)
            if STAGES < 2:
                return

            def stage1(j):
                wait(act, rows_stored, stored(1, j))
                sums(1, j, 2)
                transposed(NT, j)
                act.wait_ge(pre_gelu, 1 + j)
                nc.scalar.activation(TMP, TMP, ACT.Gelu).then_inc(post_gelu, 1)
            act.wait_ge(sums_added, 2 * TT)
            loop(act, NT, stage1)
            for n, at_h in ((2, 2 * NT), (3, 3 * NT)):
                act.wait_ge(sums_added, (2 + 2 * n) * TT)

                def stage23(j):
                    wait(act, rows_stored, stored(n, j))
                    sums(n, j, 1)
                    transposed(at_h, j)
                loop(act, NT, stage23)
            act.wait_ge(sums_added, 10 * TT)

            def stage4(j):
                wait(act, rows_stored, stored(4, j))
                sums(4, j, 1)
                transposed(4 * NT, j)
            loop(act, NT, stage4)
            for n in (5, 6):
                act.wait_ge(sums_added, (2 + 2 * n) * TT)

                def stage56(j):
                    wait(act, rows_stored, stored(n, j))
                    sums(n, j, 1, ACT.Relu)
                loop(act, NT, stage56)

        @block.tensor
        def _(pe):
            mm = nc.tensor.matmul

            def count(g, weighted):
                g0 = 2 * CT * g

                def body(i):
                    for h in range(2):
                        first = isinstance(i, int) and i == 0
                        pe.wait_ge(onehots_ready, g0 + 2 * i + h + 1)
                        last = mm(pair[0][:, 512 * h:512 * h + 512], ones_b[:, :], oh[h], start=first, stop=False, skip_group_check=True)
                        for c in range(4):
                            last = mm(pair[1][:, 0:P], cols(ohl[h], c), cols(oh[h], c), start=first and h == 0 and c == 0, stop=False, skip_group_check=True)
                        if weighted:
                            for c in range(4):
                                last = mm(pair[1][:, 512:512 + P], cols(oht[h], c), cols(ohf[h], c), start=first and h == 0 and c == 0, stop=False, skip_group_check=True)
                        last.then_inc(counted, 1)
                loop(pe, CT, body, peel_first=True)

            def block_numbers(g):
                pe.wait_ge(cmp_ready, g + 1)
                n = T // 4
                for q in range(4):
                    last = mm(pair[2 + q // 2][0:32, 512 * (q % 2):512 * (q % 2) + n], mask_b[:, 0:32], cmp_b[:, q * n:(q + 1) * n], start=True, stop=True)
                last.then_inc(blocks_in_psum, 1)

            def ranks(g):
                g0 = 2 * CT * g
                pe.wait_ge(seeds_ready, g + 1)
                for h in range(2):
                    for s in range(3):
                        mm(pair[0][:, 512 * h:512 * h + 512], ident_b, part[s][:, 512 * h:512 * h + 512], start=s == 0, stop=False, skip_group_check=True)

                def body(i):
                    for h in range(2):
                        pe.wait_ge(rank_onehots, g0 + 2 * i + h + 1)
                        mm(pair[0][:, 512 * h:512 * h + 512], lower_b, oh[h], start=False, stop=False, skip_group_check=True).then_inc(ranks_in_psum, 1)
                    for h in range(2):
                        pe.wait_ge(ranks_read, g0 + 2 * i + h + 1)
                        mm(pair[0][:, 512 * h:512 * h + 512], rest_b, oh[h], start=False, stop=False, skip_group_check=True).then_inc(carried, 1)
                loop(pe, CT, body)

            for g in range(2):
                count(g, g == 0)
                block_numbers(g)
                ranks(g)

            pe.wait_ge(weights_in, 16 * 23)
            pe.wait_ge(blocks_read, 2)
            for k in range(4):
                nc.tensor.transpose(pair[3][:, k * D:(k + 1) * D], lin[:, k, :], ident)
            for k in range(2):
                last = nc.tensor.transpose(pair[3][:, 512 + k * D:512 + (k + 1) * D], w2[:, k, :], ident)
            last.then_inc(w_psum, 1)
            pe.wait_ge(w_ready, 2)
            for k in range(2):
                mm(pair[2][:, k * D:(k + 1) * D], TMP[:, k * D:(k + 1) * D], wu[:, 1, :], start=True, stop=True)
            pe.wait_ge(seeds_ready, 3)
            mm(pair[2][:, 2 * D:3 * D], TMP[:, 2 * D:3 * D], wu[:, 1, :], start=True, stop=True).then_inc(w_psum, 1)

            def transposes(at, j, src=H):
                pe.wait_ge(h_ready, at + 1 + j)
                for b in range(B):
                    last = nc.tensor.transpose(pair[0][:, b * D:(b + 1) * D], cols(src, b), ident)
                last.then_inc(hT_in_psum, 1)

            def times(dst, terms, done, width=D):
                for b in range(B):
                    o = dst(b)
                    for t, (lhs, rhs) in enumerate(terms):
                        last = mm(o, cols(lhs, b), rhs, start=t == 0, stop=t == len(terms) - 1)
                last.then_inc(done, 1)

            def wide(b):
                return pair[1 + b // 4][:, (b % 4) * HID:(b % 4 + 1) * HID]

            def narrow(k):
                return lambda b: pair[k][:, b * D:(b + 1) * D]

            def stage0(j):
                transposes(0, j)
                pe.wait_ge(hT_ready, 1 + j)
                times(wide, [(HT, w1a[:, :])], product)
            pe.wait_ge(w_ready, 4)
            loop(pe, NT, stage0, peel_first=True)

            def tile4(j):
                for k in range(2):
                    t = 2 * j + k
                    for h in range(2):
                        q = 2 * t + h
                        if h == 0:
                            pe.wait_ge(recs_in[k], 16 * (j + 1))
                        wait(pe, eaT_ready, q)
                        r = recs[k].rearrange("p (c w) -> p c w", c=W)
                        for c in range(4):
                            last = nc.tensor.transpose(pair[3][0:ED, c * P:(c + 1) * P], r[:, 4 * h + c, 4:RD], ident)
                        last.then_inc(eaT_in_psum, 1)
                        pe.wait_ge(eaT_ready, q + 1)
                        wait(pe, z_ready, q)
                        for c in range(4):
                            last = mm(pair[2][:, c * HID:(c + 1) * HID], eaT[0:ED, c * P:(c + 1) * P], w1b[:, :], start=True, stop=True)
                        last.then_inc(edge_part, 1)
                        pe.wait_ge(gelu_ready, q + 1)
                        pe.wait_ge(sel_ready, q + 1)
                        wait(pe, sums_added, q - 1)
                        for a in range(2):
                            for c in range(4):
                                last = mm(pair[h][:, a * 512 + c * P:a * 512 + (c + 1) * P], zn[h][:, c * HID + a * P:c * HID + (a + 1) * P],
                                          cols(sel[h], c), start=True, stop=True)
                        last.then_inc(sums_in_psum, 1)
            pe.wait_ge(rows_stored, stored(1))
            loop(pe, TT // 2, tile4, peel_first=True)
            if STAGES < 2:
                return

            def passes(n):
                g0 = 2 * TT * n

                def turn(i):
                    for h in range(2):
                        for c in range(4 * h, 4 * h + 4):
                            pe.wait_ge(gathered[c], 16 * (TT * n + i + 1))
                        pe.wait_ge(sel_ready, g0 + 2 * i + h + 1)
                        wait(pe, sums_added, g0 + 2 * i + h - 1)
                        for c in range(4):
                            last = mm(pair[h][:, c * P:(c + 1) * P], ring128[:, 4 * h + c, :], cols(sel[h], c), start=True, stop=True)
                        last.then_inc(sums_in_psum, 1)
                loop(pe, TT, turn)

            def stage1(j):
                transposes(NT, j)
                pe.wait_ge(hT_ready, NT + 1 + j)
                pe.wait_ge(sums_copied, 1 + j)
                times(narrow(1), [(HT, wu[:, 0, :]), (AG[:, 0:BW], w2u[:, 0, :]), (AG[:, BW:2 * BW], w2u[:, 1, :])], product)
            loop(pe, NT, stage1)
            passes(1)
            passes(2)
            for n in (2, 3):
                def stage23(j):
                    pe.wait_ge(rows_loaded, loaded(n, j + 1))
                    pe.wait_ge(sums_copied, (n - 1) * NT + 1 + j)
                    times(narrow(1), [(AG[:, 0:BW], wn[:, n - 2, :])], product)
                    for b in range(B):
                        last = nc.tensor.transpose(pair[0][:, b * D:(b + 1) * D], cols(H, b), ident)
                    last.then_inc(hT_in_psum, 1)
                    pe.wait_ge(hT_ready, n * NT + 1 + j)
                    times(narrow(2), [(HT, wl[:, n - 2, :])], product2)
                loop(pe, NT, stage23)
                passes(n + 1)

            def stage4(j):
                pe.wait_ge(sums_copied, 3 * NT + 1 + j)
                times(narrow(1), [(AG[:, 0:BW], linT[:, 0, :])], product)
                transposes(2 * NT, j)
                pe.wait_ge(hT_ready, 4 * NT + 1 + j)
                times(narrow(2), [(HT, linT[:, 1, :])], product2)
            loop(pe, NT, stage4)
            passes(5)
            for n in (5, 6):
                def stage56(j):
                    pe.wait_ge(sums_copied, (n - 1) * NT + 1 + j)
                    times(narrow(1), [(AG[:, 0:BW], linT[:, n - 3, :])], product)
                loop(pe, NT, stage56)
                if n == 5:
                    passes(6)

        @block.vector
        def _(dve):
            v = nc.vector
            ch = Chain(dve, dve_step)
            link, straight = ch.link, ch.straight

            v.memset(src_i, TRASH * P)
            v.memset(dst_i, TRASH * P)
            v.memset(ety_i, 0)
            v.memset(chunk8, 0.0)
            v.memset(ones_b[:, :], 1.0)
            v.memset(idx_d[:, T:T + W], 0)
            v.memset(ety_d[:, T:T + W], 0)
            v.memset(idx_s[:, T:T + W], 0)
            v.memset(oht[0], 0.0)
            v.memset(oht[1], 0.0).then_inc(fill_ready, 1)
            straight(v.memset(fill_d, 0.0))
            straight(v.memset(fill_s, 0.0))
            v.memset(fill_d.rearrange("p (r w) -> p r w", w=RD)[:, :, 1], -1.0)
            v.memset(fill_s.rearrange("p (r w) -> p r w", w=RS)[:, :, 1], -1.0).then_inc(fill_ready, 1)
            dve.wait_ge(weights_in, 16 * 23)
            v.tensor_copy(cbf[:, 0:4 * P], consts[:, :])
            straight(v.tensor_scalar(rest_b, lower, -1.0, 1.0, ALU.mult, ALU.add))
            for w in (w1a[:, :], w1b[:, :], rows256[:, 0, :]):
                s = small[0:w.shape[0], 0:1]
                straight(v.tensor_reduce(s, w, AX, ALU.add))
                straight(v.tensor_scalar(s, s, -1.0 / HID, None, ALU.mult))
                straight(v.tensor_scalar(w, w, s, None, ALU.add))
            dve.wait_ge(edges_in, 16 * 6)
            dve.wait_ge(fills_done, 16 * 16)
            for ids, blk, place in ((dst_i, blk_d, lod), (src_i, blk_s, los)):
                straight(v.tensor_scalar(tcol_i, ids, 7, None, ALU.arith_shift_right))
                straight(v.tensor_copy(blk, tcol_i))
                straight(v.tensor_scalar(tcol_i, ids, P - 1, None, ALU.bitwise_and))
                straight(v.tensor_copy(place, tcol_i))
            attn_b = attn[:, :].rearrange("p (a k) -> p a k", a=1).to_broadcast([P, CE8, W])
            for q in range(NE8):
                dve.wait_ge(ea8_in, 32 * (q + 1))
                m3 = chunk8[:, 0:CE8 * W].rearrange("p (c k) -> p c k", k=W)
                straight(v.tensor_tensor(m3, m3, attn_b, ALU.mult))
                v.tensor_reduce(tanh_c[:, q * CE8:(q + 1) * CE8], m3, AX, ALU.add).then_inc(tanh_dot, 1)

            def onehot(h, i, blk):
                for c in range(4):
                    last = v.tensor_scalar(cols(oh[h], c), iota_b, blk[:, bass.ds(i * W + 4 * h + c, 1)], None, ALU.is_equal)
                return last

            def count(g, blk, place, weighted):
                g0 = 2 * CT * g
                wait(dve, carried, g0)

                def body(i):
                    for h in range(2):
                        wait(dve, counted, g0 + 2 * (i - 1) + h + 1)
                        onehot(h, i, blk)
                        for c in range(4):
                            at = bass.ds(i * W + 4 * h + c, 1)
                            last = v.tensor_scalar(cols(ohl[h], c), iota_b, place[:, at], None, ALU.is_equal)
                            if weighted:
                                v.tensor_scalar(cols(ohf[h], c), iota, blk[:, at], None, ALU.is_equal)
                                last = v.tensor_scalar(cols(oht[h], c), iota, place[:, at], tanh_c[:, at], ALU.is_equal, ALU.mult)
                        last.then_inc(onehots_ready, 1)
                loop(dve, CT, body, peel_first=True)

            def plan(g, deg, off):
                dve.wait_ge(counted, 2 * CT * (g + 1))
                straight(v.tensor_copy(cnt, pair[0][:, :]))
                straight(v.tensor_copy(deg[:, :], pair[1][:, 0:P]))
                total = ping[0]
                straight(v.tensor_reduce(total, cnt.rearrange("p (k b) -> p b k", k=W), AX, ALU.add))
                ti = base_i[:, 0:P]
                straight(v.tensor_copy(ti, total))
                straight(v.tensor_scalar(ti, ti, P - 1, None, ALU.add))
                straight(v.tensor_scalar(ti, ti, 7, None, ALU.arith_shift_right))
                tiles = cols(base, 1)
                straight(v.tensor_copy(tiles, ti))
                straight(v.memset(tiles[:, NB:P], 0.0))
                straight(v.tensor_copy(ping[0], tiles))
                a = 0
                for s in (1, 2, 4, 8, 16, 32, 64):
                    straight(v.tensor_copy(ping[1 - a][:, 0:s], ping[a][:, 0:s]))
                    straight(v.tensor_tensor(ping[1 - a][:, s:P], ping[a][:, s:P], ping[a][:, 0:P - s], ALU.add))
                    a = 1 - a
                ends, spare = ping[a], ping[1 - a]
                straight(v.tensor_tensor(spare, ends, ident, ALU.mult))
                straight(v.tensor_reduce(small[:, 0:1], spare, AX, ALU.add))
                v.tensor_scalar(cmp_b, trow, small[:, 0:1], None, ALU.is_ge).then_inc(cmp_ready, 1)
                straight(v.tensor_tensor(spare, ends, tiles, ALU.subtract))
                straight(v.tensor_scalar(cols(base, 0), spare, float(P), None, ALU.mult))
                straight(v.memset(cols(base, 0)[:, TRASH:P], float(T * P)))
                for k in range(1, W):
                    straight(v.tensor_tensor(cols(base, k), cols(base, k - 1), cols(cnt, k - 1), ALU.add))
                straight(v.tensor_copy(base_i, base))
                ci = cnt.bitcast(I32)
                for s, bits in enumerate((0xFF, 0xFF00, 0xFF0000)):
                    straight(v.tensor_scalar(ci, base_i, bits, None, ALU.bitwise_and))
                    straight(v.tensor_copy(part[s], ci))
                dve.sem_inc(seeds_ready)
                dve.wait_ge(blocks_in_psum, g + 1)
                n = T // 4
                for q in range(4):
                    last = v.tensor_scalar(off[:, q * n:(q + 1) * n], pair[2 + q // 2][0:32, 512 * (q % 2):512 * (q % 2) + n], float(P), None, ALU.mult)
                last.then_inc(blocks_read, 1)

            def ranks(g, blk, pay, fields, words):
                g0 = 2 * CT * g

                def body(j):
                    for k in range(2):
                        i = 2 * j + k
                        ch.turn(i, 7)
                        for h in range(2):
                            wait(dve, carried, g0 + 2 * (i - 1) + h + 1)
                            onehot(h, i, blk).then_inc(rank_onehots, 1)
                        for h in range(2):
                            dve.wait_ge(ranks_in_psum, g0 + 2 * i + h + 1)
                            v.tensor_tensor(prod[h], oh[h], pair[0][:, 512 * h:512 * h + 512], ALU.mult).then_inc(ranks_read, 1)
                        for h in range(2):
                            dve.wait_ge(ranks_read, g0 + 2 * i + h + 1)
                            link(v.tensor_reduce(pos[:, 4 * h:4 * h + 4], prod[h].rearrange("p (c b) -> p c b", c=4), AX, ALU.add))
                        link(v.tensor_copy(pos_i[0], pos))
                        link(v.tensor_scalar(pos_i[1], pos_i[0], P - 1, None, ALU.bitwise_and))
                        link(v.tensor_scalar(pos_i[2], pos_i[0], 7, None, ALU.arith_shift_right))
                        wait(dve, scattered[k], 16 * W * (CT // 2 * g + j))
                        link(v.scalar_tensor_tensor(out=row_i[k], in0=pos_i[1], scalar=float(ROWS), in1=pos_i[2], op0=ALU.mult, op1=ALU.add))
                        pv = pay[k].rearrange("p (c w) -> p c w", c=W)
                        for w, field in fields:
                            last = v.tensor_copy(pv[:, :, w].bitcast(field.dtype), field[:, bass.ds(i * W, W)])
                        link(last)
                        ch.end()
                        dve.sem_inc(payload_ready)
                loop(dve, CT // 2, body, peel_first=True)
                ch.over(CT)

            dve.wait_ge(tanh_ready, 1)
            count(0, blk_d, lod, True)
            plan(0, deg_d, off_d)
            straight(v.tensor_scalar(beta[:, 0:NB], pair[1][:, 512:512 + NB], 1.0 / N, None, ALU.mult))
            one = beta[:, 0:NB].rearrange("p (b a) -> p b a", a=1)
            straight(v.tensor_reduce(norm_d[:, 0:NB], one, AX, ALU.max))
            v.tensor_tensor(beta[:, 0:NB], beta[:, 0:NB], norm_d[:, 0:NB], ALU.subtract).then_inc(beta_ready, 1)
            dve.wait_ge(beta_exp, 1)
            straight(v.tensor_reduce(norm_d[:, 0:NB], one, AX, ALU.add))
            straight(v.reciprocal(norm_d[:, 0:NB], norm_d[:, 0:NB]))
            straight(v.tensor_tensor(beta[:, 0:NB], beta[:, 0:NB], norm_d[:, 0:NB], ALU.mult))
            v.memset(oht[0], 0.0)
            straight(v.memset(oht[1], 0.0))
            dve.sem_inc(payload_cleared)
            ranks(0, blk_d, pay_d, [(0, src_i), (1, lod), (2, ety_i)], RD)
            count(1, blk_s, los, False)
            plan(1, deg_s, off_s)
            ranks(1, blk_s, pay_s, [(0, dst_i), (1, los)], RS)

            straight(v.tensor_scalar(beta[:, NB:P], beta[:, 0:P - NB], 0.0, None, ALU.mult))
            straight(v.tensor_scalar(norm_d[:, :], deg_d[:, :], 1.0, None, ALU.max))
            straight(v.reciprocal(norm_d[:, :], norm_d[:, :]))
            straight(v.tensor_scalar(cnt[:, 0:P], deg_d[:, :], 0.0, None, ALU.is_gt))
            straight(v.tensor_tensor(norm_d[:, :], norm_d[:, :], cnt[:, 0:P], ALU.mult))
            straight(v.tensor_scalar(deg_s[:, :], deg_s[:, :], 1.0, None, ALU.max))
            straight(v.reciprocal(deg_s[:, :], deg_s[:, :]))

            n = T // NRB
            for q in range(NRB):
                dve.wait_ge(regrouped, 16 * (q + 1))
                r = fill_d[:, 0:n * RD].rearrange("p (t w) -> p t w", w=RD)
                at = slice(q * n, (q + 1) * n)
                v.tensor_copy(idx_d[:, at], r[:, :, 0].bitcast(I32))
                v.tensor_copy(loc_d[:, at], r[:, :, 1])
                v.tensor_copy(ety_d[:, at], r[:, :, 2].bitcast(I32)).then_inc(columns_ready, 1)
            dve.wait_ge(regrouped, 16 * (NRB + 1))
            r = fill_d[:, 0:T * RS].rearrange("p (t w) -> p t w", w=RS)
            v.tensor_copy(idx_s[:, 0:T], r[:, :, 0].bitcast(I32))
            v.tensor_copy(loc_s[:, :], r[:, :, 1]).then_inc(columns_ready, 1)

            dve.wait_ge(w_ready, 2)
            v.tensor_scalar(TMP[:, 2 * D:3 * D], ident, 0.0, b2col[:, 0:1], ALU.mult, ALU.add).then_inc(seeds_ready, 1)
            dve.wait_ge(w_ready, 4)

            def three(x):
                return x.rearrange("p (b f) -> p b f", b=B)

            def per_block(s):
                return s.rearrange("p (b a) -> p b a", a=1).to_broadcast([P, B, D])

            def every(row, width=D):
                return row.rearrange("p (a f) -> p a f", a=1).to_broadcast([P, B, width])

            def rsqrt(y, x, t):
                link(v.tensor_scalar(t.bitcast(I32), x.bitcast(I32), 1, None, ALU.arith_shift_right))
                link(v.tensor_scalar(y.bitcast(I32), t.bitcast(I32), -1.0, float(0x5F3759DF), ALU.mult, ALU.add))
                for _ in range(3):
                    link(v.scalar_tensor_tensor(out=t, in0=y, scalar=-0.5, in1=y, op0=ALU.mult, op1=ALU.mult))
                    link(v.tensor_tensor(t, t, x, ALU.mult))
                    link(v.scalar_tensor_tensor(out=y, in0=t, scalar=1.5, in1=y, op0=ALU.add, op1=ALU.mult))
            RSQ = 11
            LN = 7 + RSQ

            def normalise(src, dst, tmp):
                link(v.tensor_reduce(st1, three(src), AX, ALU.add))
                link(v.tensor_scalar(st1, st1, 1.0 / D, None, ALU.mult))
                link(v.tensor_tensor(three(dst), three(src), per_block(st1), ALU.subtract))
                link(v.tensor_tensor(tmp, dst, dst, ALU.mult))
                link(v.tensor_reduce(st2, three(tmp), AX, ALU.add))
                link(v.tensor_scalar(st2, st2, 1.0 / D, EPS, ALU.mult, ALU.add))
                rsqrt(st3, st2, st1)
                link(v.tensor_tensor(three(dst), three(dst), per_block(st3), ALU.mult))

            def stage0(j):
                ch.turn(j, LN)
                dve.wait_ge(rows_loaded, 16 + 16 * j if not (isinstance(j, int) and j == NT - 1) else 16 * NT + NX)
                normalise(X, H, TMP)
                v.tensor_scalar(H, H, 0.0, None, ALU.max).then_inc(h_ready, 1)
                ch.end()
                dve.wait_ge(product, 1 + j)
                o = OUT.rearrange("p (b f) -> p b f", b=B)
                b1 = rows256[:, 0:1, :]
                v.tensor_tensor(o[:, 0:4, :], pair[1][:, :].rearrange("p (b f) -> p b f", b=4), b1.to_broadcast([P, 4, HID]), ALU.add)
                v.tensor_tensor(o[:, 4:7, :], pair[2][:, 0:3 * HID].rearrange("p (b f) -> p b f", b=3), b1.to_broadcast([P, 3, HID]), ALU.add).then_inc(result_ready, 1)
            loop(dve, NT, stage0, peel_first=True, peel_last=True)
            ch.over(NT)

            straight(v.memset(acc[:, :], 0.0))
            dve.wait_ge(rows_stored, stored(1))
            offs = [dve.alloc_register(f"off{k}") for k in range(W)]

            def choose(h, i, loc):
                for c in range(4):
                    last = v.tensor_scalar(cols(sel[h], c), iota, loc[:, bass.ds(i * W + 4 * h + c, 1)], None, ALU.is_equal)
                last.then_inc(sel_ready, 1)

            def add_sums(h, at_col, psum, halves):
                for c in range(4):
                    o = dve.snap(offs[4 * h + c], min_val=0, max_val=NB * P)
                    if halves == 2:
                        dst = acc2[:, :, bass.ds(o, P)]
                        srcv = psum.rearrange("p (a c n) -> p a c n", a=2, c=4)[:, :, c, :]
                    else:
                        dst = acc[:, bass.ds(ACCW + o, P)]
                        srcv = cols(psum, c)
                    link(v.tensor_tensor(dst, dst, srcv, ALU.add))

            def tile8(i):
                dve.load(offs, off_d[0:1, bass.ds(i * W, W)])
                ch.turn(i, 2 * (1 + RSQ + 2 + 4))
                for h in range(2):
                    q = 2 * i + h
                    wait(dve, sums_in_psum, q - 1)
                    choose(h, i, loc_d)
                    for c in range(4 * h, 4 * h + 4):
                        dve.wait_ge(gathered[c], 16 * (i + 1))
                    dve.wait_ge(edge_part, q + 1)
                    wait(dve, squares, q)
                    for c in range(2):
                        last = v.tensor_tensor(cols(zs, c, 2 * HID), cols(pair[2], c, 2 * HID), cols(ring, 2 * h + c, 2 * HID), ALU.add)
                    last.then_inc(z_ready, 1)
                    dve.wait_ge(squares, q + 1)
                    link(v.tensor_scalar(st1[:, 0:4], ssq, 1.0 / HID, EPS, ALU.mult, ALU.add))
                    rsqrt(st2[:, 0:4], st1[:, 0:4], st3[:, 0:4])
                    for c in range(4):
                        last = v.scalar_tensor_tensor(out=cols(zn[h], c, HID), in0=cols(zs, c, HID), scalar=st2[:, c:c + 1], in1=rows256[:, 1, :], op0=ALU.mult, op1=ALU.mult)
                    link(last)
                    z4 = zn[h].rearrange("p (c f) -> p c f", c=4)
                    link(v.tensor_tensor(z4, z4, rows256[:, 2:3, :].to_broadcast([P, 4, HID]), ALU.add))
                    dve.sem_inc(z_scaled)
                    dve.wait_ge(sums_in_psum, q + 1)
                    add_sums(h, 0, pair[h][:, :], 2)
                    dve.sem_inc(sums_added)
                ch.end()
            loop(dve, TT, tile8, peel_first=True)
            ch.over(TT)
            if STAGES < 2:
                return

            def stage1(j):
                ch.turn(j, 3 * LN + 6)
                dve.wait_ge(rows_loaded, loaded(1, j + 1))
                normalise(X, H, TMP)
                v.tensor_scalar(H, H, 0.0, None, ALU.max).then_inc(h_ready, 1)
                dve.wait_ge(product, NT + 1 + j)
                dve.wait_ge(h_ready, NT + 1 + j)
                for b in range(B):
                    last = v.scalar_tensor_tensor(out=cols(TM2, b), in0=vrow[:, :], scalar=deg_d[:, bass.ds(j * B + b, 1)], in1=pair[1][:, b * D:(b + 1) * D], op0=ALU.mult, op1=ALU.add)
                link(last)
                link(v.tensor_tensor(three(TM2), three(TM2), every(rows128[:, 0, :]), ALU.add))
                normalise(TM2, TMP, TM2)
                link(v.tensor_tensor(three(TMP), three(TMP), every(rows128[:, 1, :]), ALU.mult))
                link(v.tensor_tensor(three(TMP), three(TMP), every(rows128[:, 2, :]), ALU.add))
                dve.sem_inc(pre_gelu)
                dve.wait_ge(post_gelu, 1 + j)
                link(v.tensor_tensor(TM2, TMP, H, ALU.add))
                link(v.tensor_tensor(TM2, TM2, X, ALU.add))
                dve.sem_inc(result_ready)
                normalise(TM2, H, TMP)
                v.tensor_scalar(H, H, 0.0, None, ALU.max).then_inc(result_ready, 1)
                ch.end()
            loop(dve, NT, stage1)
            ch.over(NT)

            def tiles(n, loc, off, start):
                g0 = 2 * TT * n
                if start is None:
                    straight(v.memset(acc[:, ACCW:2 * ACCW], 0.0))
                else:
                    straight(v.tensor_copy(acc[:, ACCW:2 * ACCW], start))

                def turn(i):
                    dve.load(offs, off[0:1, bass.ds(i * W, W)])
                    ch.turn(i, 8)
                    for h in range(2):
                        dve.wait_ge(sums_in_psum, g0 + 2 * i + h - 1)
                        choose(h, i, loc)
                    for h in range(2):
                        dve.wait_ge(sums_in_psum, g0 + 2 * i + h + 1)
                        add_sums(h, ACCW, pair[h][:, 0:512], 1)
                        dve.sem_inc(sums_added)
                    ch.end()
                loop(dve, TT, turn)
                ch.over(TT)

            dve.wait_ge(rows_stored, stored(2))
            dve.wait_ge(sums_copied, NT)
            tiles(1, loc_d, off_d, None)
            straight(v.tensor_copy(acc[:, 0:ACCW], acc[:, ACCW:2 * ACCW]))
            tiles(2, loc_d, off_d, acc[:, 0:ACCW])

            for n in (2, 3):
                def stage23(j):
                    ch.turn(j, 2 if n == 2 else 3 + LN)
                    dve.wait_ge(product, n * NT + 1 + j)
                    dve.wait_ge(product2, (n - 2) * NT + 1 + j)
                    link(v.tensor_copy(TMP, pair[2][:, 0:BW]))
                    for b in range(B):
                        last = v.scalar_tensor_tensor(out=cols(TMP, b), in0=pair[1][:, b * D:(b + 1) * D], scalar=norm_d[:, bass.ds(j * B + b, 1)], in1=cols(TMP, b), op0=ALU.mult, op1=ALU.add)
                    link(last)
                    if n == 2:
                        v.scalar_tensor_tensor(out=TM2, in0=TMP, scalar=SLOPE, in1=TMP, op0=ALU.mult, op1=ALU.max).then_inc(result_ready, 1)
                    else:
                        link(v.scalar_tensor_tensor(out=TM2, in0=TMP, scalar=SLOPE, in1=TMP, op0=ALU.mult, op1=ALU.max))
                        v.tensor_tensor(TM2, TM2, X, ALU.add).then_inc(result_ready, 1)
                        dve.wait_ge(result_ready, RES[3] + 1 + 2 * j)
                        normalise(TM2, HT, TMP)
                        v.tensor_scalar(HT, HT, 0.0, None, ALU.max).then_inc(result_ready, 1)
                    ch.end()
                if n == 3:
                    dve.wait_ge(rows_loaded, loaded(2, NT))
                loop(dve, NT, stage23)
                ch.over(NT)
                dve.wait_ge(rows_stored, stored(n + 1))
                dve.wait_ge(sums_copied, n * NT)
                tiles(n + 1, loc_d, off_d, acc[:, 0:ACCW] if n == 2 else None)

            def stage4(j):
                ch.turn(j, LN)
                dve.wait_ge(rows_loaded, loaded(4, j + 1))
                dve.wait_ge(product, 4 * NT + 1 + j)
                for b in range(B):
                    last = v.scalar_tensor_tensor(out=cols(TM2, b), in0=pair[1][:, b * D:(b + 1) * D], scalar=beta[:, bass.ds(j * B + b, 1)], in1=cols(X, b), op0=ALU.mult, op1=ALU.add)
                last.then_inc(result_ready, 1)
                dve.wait_ge(result_ready, RES[4] + 1 + 2 * j)
                normalise(TM2, H, TMP)
                v.tensor_scalar(H, H, 0.0, None, ALU.max).then_inc(h_ready, 1)
                dve.wait_ge(product2, 2 * NT + 1 + j)
                v.tensor_tensor(three(TMP), pair[2][:, 0:BW].rearrange("p (b f) -> p b f", b=B), every(rows128[:, 3, :]), ALU.add).then_inc(result_ready, 1)
                ch.end()
            loop(dve, NT, stage4)
            ch.over(NT)
            dve.wait_ge(rows_stored, stored(5))
            tiles(5, loc_s, off_s, None)
            for n in (5, 6):
                def stage56(j):
                    ch.turn(j, n - 5)
                    if n == 6:
                        dve.wait_ge(rows_loaded, loaded(6, j + 1))
                    dve.wait_ge(product, n * NT + 1 + j)
                    for b in range(B):
                        last = v.scalar_tensor_tensor(out=cols(TM2, b), in0=pair[1][:, b * D:(b + 1) * D], scalar=deg_s[:, bass.ds(j * B + b, 1)], in1=rows128[:, n - 1, :], op0=ALU.mult, op1=ALU.add)
                    if n == 6:
                        link(last)
                        last = v.tensor_tensor(TM2, TM2, X, ALU.add)
                    last.then_inc(result_ready, 1)
                    ch.end()
                loop(dve, NT, stage56, peel_last=n == 6)
                ch.over(NT)
                if n == 5:
                    dve.wait_ge(rows_stored, stored(6))
                    dve.wait_ge(sums_copied, 5 * NT)
                    tiles(6, loc_s, off_s, None)


CE8 = 112
NE8 = C // CE8
NRB = 8
RES = [0, NT, 3 * NT, 4 * NT, 6 * NT, 8 * NT, 9 * NT]
assert C % CE8 == 0 and T % NRB == 0 and CE8 * W <= W * P

_INS = ['x', 'src', 'dst', 'edge_attr_32', 'edge_attr_8', 'edge_type_460', 'L0_gnn_W1', 'L0_gnn_b1', 'L0_gnn_g1',
        'L0_gnn_be1', 'L0_gnn_W2', 'L0_gnn_b2', 'L0_gnn_Wu', 'L0_gnn_bu', 'L0_gnn_gu', 'L0_gnn_beu',
        'L1_gnn_rel_emb', 'L1_gnn_w_neighbor', 'L1_gnn_w_loop', 'L2_gnn_w_attn', 'L2_gnn_W_lin', 'L3_gnn_W1',
        'L3_gnn_b1', 'L3_gnn_W2', 'L3_gnn_b2', 'L3_gnn_W3', 'L3_gnn_b3']


def kernel(**inputs):
    import numpy as _np
    import concourse.bacc as _bacc
    from concourse import mybir as _mybir
    from concourse.bass_utils import run_bass_kernel_spmd as _run

    nc = _bacc.Bacc("TRN2", target_bir_lowering=False, num_devices=1)
    arrays, aps = {}, {}
    given = {name: _np.ascontiguousarray(inputs[name]) for name in _INS}
    k = _np.arange(P)
    given["shape_consts"] = _np.concatenate(
        [k[:, None] == k, _np.broadcast_to(k, (P, P)), k[:, None] < k, _np.broadcast_to(k[:, None] < NB, (P, P))],
        axis=1).astype(_np.float32)
    given["tile_numbers"] = _np.arange(T, dtype=_np.float32)[None, :]
    for name, a in given.items():
        arrays[f"in_{name}_dram"] = a
        aps[name] = nc.dram_tensor(f"in_{name}_dram", a.shape, _mybir.dt.from_np(a.dtype), kind="ExternalInput").ap()
    out = nc.dram_tensor("out_0_dram", (N, D), F32, kind="ExternalOutput").ap()
    build(nc, aps, out)
    r = _run(nc, [arrays], core_ids=[0])
    return r.results[0]["out_0_dram"]
```

```python
from contextlib import ExitStack

import concourse.bass as bass
from concourse import mybir

P = 128
N = 12500
E = 200000
D = 128
HID = 256
ED = 32
NB = -(-N // P)
NPAD = NB * P
W = 8
C = -(-E // (P * W)) * W
CT = C // W
LAST = E - (P - 1) * C
T = -(-(E // P + NB) // (2 * W)) * 2 * W
TT = T // W
ROWS = T + W
RD = 4 + ED
RS = 2
ACCW = (NB + 1) * P
B = 7
NT = NB // B
BW = B * D
TRASH = P - 1
EPS = 1e-5
SLOPE = 11.0 / 48.0

assert NB % B == 0 and LAST % W == 0 and LAST > 0 and CT % 2 == 0 and TT % 2 == 0
assert T >= (E + NB * (P - 1)) // P + 1 and ROWS - T >= (P * C - E) // P + 2

F32 = mybir.dt.float32
BF16 = mybir.dt.bfloat16
I32 = mybir.dt.int32
ALU = mybir.AluOpType
ACT = mybir.ActivationFunctionType
AX = mybir.AxisListType.X


def build(nc, A, out):
    ctx = ExitStack()
    with ctx:
        def sb(name, shape, dt=F32):
            return ctx.enter_context(nc.sbuf_tensor(name, shape, dt))

        def sem(name):
            return ctx.enter_context(nc.semaphore(name))

        def dram(name, shape, dt=F32):
            return nc.dram_tensor(name, shape, dt).ap()

        rec_d = dram("rec_d", [P * ROWS, RD])
        rec_s = dram("rec_s", [P * ROWS, RS])
        rel_sums = dram("rel_sums", [P, ACCW])
        tab_p = dram("tab_p", [NPAD, HID])
        x_pad = dram("x_pad", [NPAD, D])
        x1, x2, x3 = (dram(f"x{k}_rows", [NPAD, D]) for k in (1, 2, 3))
        h1, h2, h4, g1t, g2t = (dram(n, [NPAD, D]) for n in ("h1_rows", "h2_rows", "h4_rows", "l3a_rows", "l3b_rows"))

        acc = sb("acc", [P, 2 * ACCW])
        acc2 = acc[:, :].rearrange("p (a n) -> p a n", a=2)
        idx = sb("idx", [P, T + W], I32)
        ety = sb("ety", [P, T + W], I32)
        loc = sb("loc", [P, T])
        off = sb("off", [32, T], I32)
        off_s = sb("off_s", [32, T], I32)
        work = sb("work", [P, 11000])

        consts = sb("consts", [P, 4 * P])
        ident, iota, lower, mask = (consts[:, k * P:(k + 1) * P] for k in range(4))
        cbf = sb("cbf", [P, 5 * P], BF16)
        ident_b, iota_b, lower_b, mask_b, rest_b = (cbf[:, k * P:(k + 1) * P] for k in range(5))
        ones_b = sb("ones_b", [P, P], BF16)
        w1a = sb("w1a", [P, HID])
        w1b = sb("w1b", [ED, HID])
        rows256 = sb("rows256", [P, 3, HID])
        rows128 = sb("rows128", [P, 6, D])
        b2col = sb("b2col", [P, 1])
        attn = sb("attn", [P, W])
        w2 = sb("w2", [P, 2, D])
        wu = sb("wu", [P, 2, D])
        wn = sb("wn", [P, 2, D])
        wl = sb("wl", [P, 2, D])
        lin = sb("lin", [P, 4, D])
        linT = sb("linT", [P, 4, D])
        w2u = sb("w2u", [P, 2, D])
        vrow = sb("vrow", [P, D])
        deg = sb("deg", [P, P])
        node_sums = sb("node_sums", [P, 2 * P])
        beta = sb("beta", [P, P])
        norm_d = sb("norm_d", [P, P])
        small = sb("small", [P, 64])

        pair = [ctx.enter_context(nc.psum_tensor(f"pair{k}", [P, 1024], F32)) for k in range(4)]

        def acc_view(at, n):
            return acc[:, at:at + n]
        src_i, dst_i, ety_i, blk_d, lod, blk_s, los, tanh_c = (acc_view(k * C, C) for k in range(8))
        src_i, dst_i, ety_i = (v.bitcast(I32) for v in (src_i, dst_i, ety_i))
        FILL = ROWS // 8
        fill_d = acc_view(8 * C, FILL * RD)
        fill_s = acc_view(8 * C + FILL * RD, FILL * RS)
        trow = acc_view(8 * C + FILL * (RD + RS), T)
        tcol_i = fill_d[:, 0:C].bitcast(I32)

        at = [0]

        def ws(n, dt=F32):
            v = work[:, at[0]:at[0] + n]
            at[0] += n
            return v if dt == F32 else v.bitcast(dt)

        oh = [ws(W // 2 * P // 2, BF16) for _ in range(2)]
        prod = [ws(W // 2 * P) for _ in range(2)]
        pay_d = [ws(W * RD) for _ in range(2)]
        pay_s = [ws(W * RS) for _ in range(2)]
        cnt = ws(W * P)
        base = ws(W * P)
        base_i = ws(W * P, I32)
        part = [ws(W * P // 2, BF16) for _ in range(3)]
        cmp_b = ws(T // 2, BF16)
        ping = [ws(P) for _ in range(2)]
        assert at[0] <= 11000
        pos = small[:, 0:8]
        pos_i = [small[:, 8 * k:8 * k + 8].bitcast(I32) for k in (1, 2, 3)]
        row_i = [small[:, 8 * k:8 * k + 8].bitcast(I32) for k in (4, 5)]
        chunk8 = cnt
        at[0] = 0
        ring = ws(W * HID)
        ring3 = ring.rearrange("p (k f) -> p k f", k=W)
        sel = [ws(W // 2 * P) for _ in range(2)]
        recs = [ws(W * RD) for _ in range(2)]
        eaT = [ws(W // 2 * P) for _ in range(2)]
        zn = [ws(W // 2 * HID) for _ in range(2)]
        sq = ws(W // 2 * HID)
        assert at[0] <= 11000
        idx_r = [small[:, 8 * k:8 * k + 8].bitcast(I32) for k in (0, 1)]
        ssq = [small[:, 16 + 4 * k:20 + 4 * k] for k in range(2)]
        rs_x, rs_t = small[:, 24:28], small[:, 28:32]
        rstd = [small[:, 32 + 4 * k:36 + 4 * k] for k in range(2)]
        at[0] = W * D + W // 2 * P * 2
        ring_128 = work[:, 0:W * D].rearrange("p (k f) -> p k f", k=W)
        sel_p = [work[:, W * D + k * (W // 2) * P:W * D + (k + 1) * (W // 2) * P] for k in range(2)]
        pairs = ws(2 * T)
        tile_sums = ws(2 * T)
        turned = pairs
        tile_block = ws(TC)
        assert at[0] <= 11000
        at[0] = 0
        X, H, HT, TMP, TM2 = (ws(BW) for _ in range(5))
        AG = ws(2 * BW)
        OUT = ws(B * HID)
        assert at[0] <= 11000
        st1, st2, st3 = small[:, 32:39], small[:, 40:47], small[:, 48:55]

        def cols(ap, k, n=P):
            return ap[:, k * n:(k + 1) * n]

        weights_in = sem("weights_in")
        edges_in = sem("edges_in")
        ea8_in = sem("ea8_in")
        fill_ready = sem("fill_ready")
        fills_done = sem("fills_done")
        dve_step = sem("dve_step")
        act_step = sem("act_step")
        tanh_dot = sem("tanh_dot")
        tanh_ready = sem("tanh_ready")
        onehots_ready = sem("onehots_ready")
        counted = sem("counted")
        cmp_ready = sem("cmp_ready")
        blocks_in_psum = sem("blocks_in_psum")
        blocks_read = sem("blocks_read")
        seeds_ready = sem("seeds_ready")
        rank_onehots = sem("rank_onehots")
        ranks_in_psum = sem("ranks_in_psum")
        ranks_read = sem("ranks_read")
        carried = sem("carried")
        payload_ready = sem("payload_ready")
        ea_in = [sem(f"ea_in{k}") for k in range(2)]
        scattered = [sem(f"scattered{k}") for k in range(2)]
        pool_turn = sem("pool_turn")
        sp_turn = sem("sp_turn")
        regrouped = sem("regrouped")
        pairs_ready = sem("pairs_ready")
        tile_sums_in_psum = sem("tile_sums_in_psum")
        tile_sums_ready = sem("tile_sums_ready")
        starts_ready = sem("starts_ready")
        turned_in_psum = sem("turned_in_psum")
        turned_ready = sem("turned_ready")
        node_sums_in_psum = sem("node_sums_in_psum")
        node_sums_read = sem("node_sums_read")
        z_free = sem("z_free")
        b2_spread = sem("b2_spread")
        rel_moved = sem("rel_moved")
        columns_ready = sem("columns_ready")
        w_psum = sem("w_psum")
        w_ready = sem("w_ready")
        beta_ready = sem("beta_ready")
        beta_exp = sem("beta_exp")
        idx_copied = sem("idx_copied")
        gathered = [sem(f"gathered{k}") for k in range(W)]
        sel_ready = sem("sel_ready")
        sums_in_psum = sem("sums_in_psum")
        sums_added = sem("sums_added")
        acc_ready = sem("acc_ready")
        recs_in = [sem(f"recs_in{k}") for k in range(2)]
        eaT_in_psum = sem("eaT_in_psum")
        eaT_ready = sem("eaT_ready")
        edge_part = sem("edge_part")
        squares = sem("squares")
        z_scaled = sem("z_scaled")
        gelu_ready = sem("gelu_ready")
        rows_loaded = sem("rows_loaded")
        h_ready = sem("h_ready")
        hT_in_psum = sem("hT_in_psum")
        hT_ready = sem("hT_ready")
        sums_copied = sem("sums_copied")
        product = sem("product")
        product2 = sem("product2")
        pre_gelu = sem("pre_gelu")
        post_gelu = sem("post_gelu")
        result_ready = sem("result_ready")
        rows_stored = sem("rows_stored")

        def wait(eng, s, value):
            if not (isinstance(value, int) and value <= 0):
                eng.wait_ge(s, value)

        class Chain:

            def __init__(self, eng, s):
                self.eng, self.s, self.done, self.k, self.at = eng, s, 0, 0, 0

            def step(self, ins):
                self.k += 1
                ins.then_inc(self.s, 1)
                return self.at + self.k

            def after(self, count):
                self.eng.wait_ge(self.s, count)

            def link(self, ins):
                self.after(self.step(ins))

            def straight(self, ins):
                self.done += 1
                ins.then_inc(self.s, 1)
                self.eng.wait_ge(self.s, self.done)

            def run(self, n, body, per, peel_first=False, peel_last=False):
                lo, hi = int(peel_first), n - int(peel_last)

                def once(i):
                    self.at, self.k = self.done, 0
                    body(i)
                    self.done += self.k
                if peel_first:
                    once(0)
                with self.eng.Fori(lo, hi) as i:
                    self.at, self.k = self.done + (i - lo) * per, 0
                    body(i)
                    assert self.k == per, (self.k, per)
                self.done += (hi - lo) * per
                if peel_last:
                    once(n - 1)

        def inside(q):
            return not isinstance(q, int) or 0 <= q < 2 * TT

        def loop(eng, n, body, peel_first=False, peel_last=False):
            lo, hi = int(peel_first), n - int(peel_last)
            if peel_first:
                body(0)
            with eng.Fori(lo, hi) as i:
                body(i)
            if peel_last:
                body(n - 1)

        TABLES = {0: (A["L1_gnn_rel_emb"], ety), 2: (h1, idx), 3: (h2, idx), 4: (h4, idx), 5: (g1t, idx), 6: (g2t, idx)}
        STORES = [2, 2, 1, 2, 2, 1, 1]
        LOADS = [1, 1, 1, 2, 1, 0, 1]

        def stored(n, j=0):
            extra = 16 * STORES[n] * j if not isinstance(j, int) or j else 0
            return 16 * NT * sum(STORES[:n]) + extra

        def loaded(n, j=0):
            return 16 * NT * sum(LOADS[:n]) + (NX if n > 0 else 0) + 16 * LOADS[n] * j
        NX = 16

        def table_done(n):
            return stored(n + 1)

        block = ctx.enter_context(nc.Block())

        @block.sync
        def _(sp):
            def row(name):
                return A[name].rearrange("(a f) -> a f", a=1)

            loads = [(consts[:, :], A["shape_consts"]), (w1a[:, :], A["L0_gnn_W1"][0:D, :]),
                     (w1b[:, :], A["L0_gnn_W1"][D:D + ED, :]),
                     (b2col[:, :], A["L0_gnn_b2"].rearrange("(f a) -> f a", a=1)),
                     (attn[:, :], A["L2_gnn_w_attn"].rearrange("k a -> a k").to_broadcast([P, W])),
                     (w2[:, :, :], A["L0_gnn_W2"].rearrange("(a p) f -> p a f", a=2)),
                     (wu[:, :, :], A["L0_gnn_Wu"].rearrange("(a p) f -> p a f", a=2)),
                     (wn[:, :, :], A["L1_gnn_w_neighbor"].rearrange("a p f -> p a f")),
                     (wl[:, :, :], A["L1_gnn_w_loop"].rearrange("a p f -> p a f")),
                     (trow, A["tile_numbers"].to_broadcast([P, T]))]
            loads += [(rows256[:, k, :], row(n).to_broadcast([P, HID]))
                      for k, n in enumerate(("L0_gnn_b1", "L0_gnn_g1", "L0_gnn_be1"))]
            loads += [(rows128[:, k, :], row(n).to_broadcast([P, D])) for k, n in enumerate(
                ("L0_gnn_bu", "L0_gnn_gu", "L0_gnn_beu", "L3_gnn_b1", "L3_gnn_b2", "L3_gnn_b3"))]
            loads += [(lin[:, k, :], A[n]) for k, n in enumerate(
                ("L2_gnn_W_lin", "L3_gnn_W1", "L3_gnn_W2", "L3_gnn_W3"))]
            for dst, src in loads:
                with nc.allow_non_contiguous_dma(reason="a column of 128 biases"):
                    sp.dma_start(dst, src).then_inc(weights_in, 16)
            assert len(loads) == 23
            sp.wait_ge(fill_ready, 1)
            for v, name in ((src_i, "src"), (dst_i, "dst"), (ety_i, "edge_type_460")):
                sp.dma_start(v[0:P - 1, :], A[name][0:(P - 1) * C].rearrange("(p c) -> p c", c=C)).then_inc(edges_in, 16)
                sp.dma_start(v[P - 1:P, 0:LAST], A[name][(P - 1) * C:E].rearrange("(a c) -> a c", a=1)).then_inc(edges_in, 16)
            sp.wait_ge(fill_ready, 2)
            fd = rec_d.rearrange("(p r) w -> p (r w)", p=P)
            fs = rec_s.rearrange("(p r) w -> p (r w)", p=P)
            for k in range(8):
                sp.dma_start(fd[:, k * FILL * RD:(k + 1) * FILL * RD], fill_d).then_inc(fills_done, 16)
                sp.dma_start(fs[:, k * FILL * RS:(k + 1) * FILL * RS], fill_s).then_inc(fills_done, 16)
            for q in range(NE8):
                if q:
                    sp.wait_ge(tanh_dot, q)
                n = CE8
                c0 = q * n
                sp.dma_start(chunk8[0:P - 1, 0:n * W], A["edge_attr_8"][0:(P - 1) * C, :].rearrange("(p c) k -> p (c k)", c=C)[:, c0 * W:(c0 + n) * W]).then_inc(ea8_in, 16)
                m = max(0, min(LAST - c0, n))
                if m:
                    a0 = (P - 1) * C + c0
                    sp.dma_start(chunk8[P - 1:P, 0:m * W], A["edge_attr_8"][a0:a0 + m, :].rearrange("(a c) k -> a (c k)", a=1)).then_inc(ea8_in, 16)
                else:
                    sp.dma_start(chunk8[P - 1:P, 0:W], A["edge_attr_8"][0:1, :]).then_inc(ea8_in, 16)

            ea = A["edge_attr_32"]
            top, mid = 112, P - 1
            ea_top = ea[0:top * C, :].rearrange("(p c) f -> p c f", c=C)
            ea_mid = ea[top * C:mid * C, :].rearrange("(p c) f -> p c f", c=C)
            ea_low = ea[mid * C:E, :].rearrange("(a c) f -> a c f", a=1)

            def feed(j, low):
                for k in range(2):
                    c0 = (2 * j + k) * W
                    wait(sp, scattered[k], 16 * W * j)
                    v = pay_d[k].rearrange("p (c w) -> p c w", c=W)
                    sp.dma_start(v[0:top, :, 4:RD], ea_top[:, bass.ds(c0, W), :]).then_inc(ea_in[k], 16)
                    sp.dma_start(v[top:mid, :, 4:RD], ea_mid[:, bass.ds(c0, W), :]).then_inc(ea_in[k], 16)
                    if low:
                        sp.dma_start(v[mid:P, :, 4:RD], ea_low[:, bass.ds(c0, W), :]).then_inc(ea_in[k], 16)
            feed(0, True)
            with sp.Fori(1, LAST // W // 2) as j:
                feed(j, True)
            with sp.Fori(LAST // W // 2, CT // 2) as j:
                feed(j, False)

            for k in range(2):
                sp.wait_ge(scattered[k], 16 * W * CT // 2)
            rd = rec_d.rearrange("(p r) w -> p (r w)", p=P)
            for q in range(NRB):
                if q:
                    sp.wait_ge(columns_ready, q)
                sp.dma_start(fill_d[:, 0:T // NRB * RD], rd[:, q * (T // NRB) * RD:(q + 1) * (T // NRB) * RD]).then_inc(regrouped, 16)
            sp.wait_ge(sums_added, 2 * TT)
            sp.dma_start(rel_sums[:, :], acc[:, ACCW:2 * ACCW]).then_inc(rel_moved, 16)

            def node_rows(t, j):
                return t[bass.ds(j * B * P, B * P), :].rearrange("(b p) f -> p b f", p=P)

            def seven(v):
                return v.rearrange("p (b f) -> p b f", b=B)

            FULL = B - 1
            NR = N - (NB - 1) * P

            def stage(n, load, store):
                def body(j):
                    if n > 0 or not (isinstance(j, int) and j == 0):
                        wait(sp, rows_stored, stored(n, j))
                        sp.sem_inc(sp_turn)
                    load(j)
                    store(j)
                loop(sp, NT, body, peel_first=n == 0, peel_last=n in (0, 6))

            def load_x(src):
                return lambda j: sp.dma_start(seven(X), node_rows(src, j)).then_inc(rows_loaded, 16)

            def load0(j):
                if isinstance(j, int) and j == NT - 1:
                    r0 = j * B * P
                    sp.dma_start(seven(X)[:, 0:FULL, :], A["x"][r0:r0 + FULL * P, :].rearrange("(b p) f -> p b f", p=P)).then_inc(rows_loaded, 16)
                    sp.dma_start(seven(X)[0:NR, FULL, :], A["x"][r0 + FULL * P:N, :]).then_inc(rows_loaded, 16)
                else:
                    sp.dma_start(seven(X), node_rows(A["x"], j)).then_inc(rows_loaded, 16)

            def store0(j):
                sp.wait_ge(rows_loaded, (16 + 16 * j) if not (isinstance(j, int) and j == NT - 1) else 16 * NT + NX)
                sp.dma_start(node_rows(x_pad, j), seven(X)).then_inc(rows_stored, 16)
                sp.wait_ge(result_ready, 1 + j)
                sp.dma_start(node_rows(tab_p, j), seven(OUT)).then_inc(rows_stored, 16)
            sp.wait_ge(node_sums_read, 1)
            sp.wait_ge(w_ready, 4)
            stage(0, load0, store0)

            rdt = rec_d.rearrange("(p r) w -> p (r w)", p=P)

            def edge_recs(j):
                for k in range(2):
                    t = 2 * j + k
                    wait(sp, eaT_in_psum, 2 * t - 2)
                    sp.dma_start(recs[k], rdt[:, bass.ds(t * (W * RD), W * RD)]).then_inc(recs_in[k], 16)
            sp.wait_ge(rows_stored, stored(1))
            loop(sp, TT // 2, edge_recs, peel_first=True)

            def results(n, first, second=None):
                m = 2 if second is not None else 1

                def body(j):
                    base_r = RES[n]
                    sp.wait_ge(result_ready, base_r + 1 + m * j)
                    sp.dma_start(node_rows(first[0], j), seven(first[1])).then_inc(rows_stored, 16)
                    if second is not None:
                        sp.wait_ge(result_ready, base_r + 2 + m * j)
                        sp.dma_start(node_rows(second[0], j), seven(second[1])).then_inc(rows_stored, 16)
                return body

            sp.wait_ge(sums_added, 4 * TT)
            stage(1, load_x(x_pad), results(1, (x1, TM2), (h1, H)))

            def rel_back(n):
                sp.wait_ge(sums_copied, n * NT)
                sp.dma_start(acc[:, ACCW:2 * ACCW], rel_sums[:, :]).then_inc(rel_moved, 16)
            sp.wait_ge(rel_moved, 16)
            rel_back(1)
            for k in range(2):
                sp.wait_ge(scattered[k], 16 * W * CT)
            sp.dma_start(acc[:, 0:T * RS], rec_s.rearrange("(p r) w -> p (r w)", p=P)[:, 0:T * RS]).then_inc(regrouped, 16)

            def load_h(src, second=None):
                def body(j):
                    sp.dma_start(seven(H), node_rows(src, j)).then_inc(rows_loaded, 16)
                    if second is not None:
                        sp.dma_start(seven(X), node_rows(second, j)).then_inc(rows_loaded, 16)
                return body
            sp.wait_ge(sums_added, 6 * TT)
            stage(2, load_h(h1), results(2, (h2, TM2)))
            rel_back(2)
            sp.wait_ge(sums_added, 8 * TT)
            stage(3, load_h(h2, x1), results(3, (x2, TM2), (h4, HT)))
            sp.wait_ge(sums_added, 10 * TT)
            stage(4, load_x(x2), results(4, (x3, TM2), (g1t, TMP)))
            sp.wait_ge(sums_added, 12 * TT)
            stage(5, lambda j: None, results(5, (g2t, TM2)))
            sp.wait_ge(sums_added, 14 * TT)

            def last_rows(j):
                sp.wait_ge(result_ready, RES[6] + 1 + j)
                if isinstance(j, int):
                    r0 = j * B * P
                    sp.dma_start(out[r0:r0 + FULL * P, :].rearrange("(b p) f -> p b f", p=P), seven(TM2)[:, 0:FULL, :]).then_inc(rows_stored, 16)
                    sp.dma_start(out[r0 + FULL * P:N, :], seven(TM2)[0:NR, FULL, :]).then_inc(rows_stored, 16)
                else:
                    sp.dma_start(node_rows(out, j), seven(TM2)).then_inc(rows_stored, 16)
            stage(6, load_x(x3), last_rows)
            sp.wait_ge(rows_stored, stored(7) + 16)

        @block.gpsimd
        def _(pool):
            def admitted():
                pool.sem_inc(pool_turn)

            pool.wait_ge(fills_done, 16 * 16)

            def scatter(j, rec, pay, words, first, dst):
                for k in range(2):
                    wait(pool, payload_ready, first + 2 * j + k + 1)
                    if dst:
                        wait(pool, ea_in[k], dst(j))
                    admitted()
                    v = pay[k].rearrange("p (c w) -> p c w", c=W)
                    for c in range(W):
                        pool.indirect_dma_start(
                            out=rec[:, :], out_offset=bass.IndirectOffsetOnAxis(ap=row_i[k][:, c:c + 1], axis=0),
                            in_=v[:, c, :], in_offset=None).then_inc(scattered[k], 16)
            lowj = LAST // W // 2
            loop(pool, lowj, lambda j: scatter(j, rec_d, pay_d, RD, 0, lambda j: 48 * (j + 1)))
            with pool.Fori(lowj, CT // 2) as j:
                scatter(j, rec_d, pay_d, RD, 0, lambda j: 48 * lowj + 32 * (j - lowj + 1))
            loop(pool, CT // 2, lambda j: scatter(j, rec_s, pay_s, RS, CT, None))

            def gathers(n, table, nodes, dst, used, g0):
                def copy(i, k):
                    pool.tensor_copy(idx_r[k], nodes[:, bass.ds(i * W, W)]).then_inc(idx_copied, 1)
                wait(pool, idx_copied, n * (TT + 1))
                copy(0, 0)

                def turn2(j):
                    for k in range(2):
                        i = 2 * j + k
                        for h in range(2):
                            wait(pool, used, g0 + 2 * i + h - 1)
                            if h == 1:
                                admitted()
                                copy(i + 1, 1 - k)
                            else:
                                wait(pool, idx_copied, n * (TT + 1) + i + 1)
                                admitted()
                            for c in range(4 * h, 4 * h + 4):
                                pool.indirect_dma_start(
                                    out=dst[:, c, :], out_offset=None, in_=table[:, :],
                                    in_offset=bass.IndirectOffsetOnAxis(ap=idx_r[k][:, c:c + 1], axis=0)).then_inc(gathered[c], 16)
                loop(pool, TT // 2, turn2, peel_first=True)
            pool.wait_ge(columns_ready, NRB)
            pool.wait_ge(carried, 4 * CT)
            for n in range(7):
                if n == 1:
                    pool.wait_ge(rows_stored, table_done(0))
                    gathers(1, tab_p, idx, ring3, edge_part, 0)
                    continue
                if n > 1:
                    pool.wait_ge(rows_stored, table_done(n - 1))
                if n == 5:
                    pool.wait_ge(columns_ready, NRB + 1)
                table, nodes = TABLES[n]
                gathers(n, table, nodes, ring_128, sums_in_psum, 2 * TT * n)

        @block.scalar
        def _(act):
            act.wait_ge(tanh_dot, NE8)
            nc.scalar.activation(tanh_c, tanh_c, ACT.Tanh).then_inc(tanh_ready, 1)

            def tile_sum_copies(g):
                def turn(i):
                    for h in range(2):
                        act.wait_ge(tile_sums_in_psum, 2 * TT * g + 2 * i + h + 1)
                        nc.scalar.copy(tile_sums[:, bass.ds((i * W + 4 * h) * 2, W)], pair[2 + h][:, 0:W]).then_inc(tile_sums_ready, 1)
                loop(act, TT, turn)
                for k in range(2):
                    act.wait_ge(turned_in_psum, 3 * g + k + 2)
                    nc.scalar.copy(turned[:, k * T:k * T + 1024], pair[2][:, :])
                    nc.scalar.copy(turned[:, k * T + 1024:(k + 1) * T], pair[3][:, 0:T - 1024]).then_inc(turned_ready, 1)
                act.wait_ge(turned_ready, 2 * g + 2)
            tile_sum_copies(0)
            act.wait_ge(beta_ready, 1)
            nc.scalar.activation(beta[:, 0:NB], beta[:, 0:NB], ACT.Exp).then_inc(beta_exp, 1)
            act.wait_ge(w_psum, 1)
            nc.scalar.copy(linT[:, :, :].rearrange("p a f -> p (a f)"), pair[3][:, 0:4 * D]).then_inc(w_ready, 1)
            nc.scalar.copy(TMP[:, 0:2 * D], pair[3][:, 512:512 + 2 * D]).then_inc(w_ready, 1)
            act.wait_ge(w_psum, 2)
            nc.scalar.copy(w2u[:, :, :].rearrange("p a f -> p (a f)"), pair[2][:, 0:2 * D]).then_inc(w_ready, 1)
            nc.scalar.copy(vrow[:, :], pair[2][:, 2 * D:3 * D]).then_inc(w_ready, 1)

            def transposed(at, j):
                act.wait_ge(hT_in_psum, at + 1 + j)
                nc.scalar.copy(HT, pair[0][:, 0:BW]).then_inc(hT_ready, 1)

            def sums(at, j, halves, func=ACT.Copy):
                v = acc2[:, 2 - halves:2, bass.ds(j * BW, BW)]
                nc.scalar.activation(AG[:, 0:halves * BW].rearrange("p (a n) -> p a n", a=halves), v, func).then_inc(sums_copied, 1)

            loop(act, NT, lambda j: transposed(0, j), peel_first=True)

            def copy_eaT(q, b):
                act.wait_ge(eaT_in_psum, q + 1)
                wait(act, edge_part, q - 1)
                nc.scalar.copy(eaT[b][0:ED, :], pair[3][0:ED, 512 * b:512 * b + 4 * P]).then_inc(eaT_ready, 1)

            def square(q, b):
                act.wait_ge(edge_part, q + 1)
                wait(act, squares, q)
                for c in range(4):
                    last = nc.scalar.activation(cols(sq, c, HID), cols(pair[1 + b], c, HID), ACT.Square, accum_out=ssq[b][:, c:c + 1])
                last.then_inc(squares, 1)

            def tile16(j):
                for s in range(4):
                    q = 4 * j + s
                    if inside(q + 3):
                        copy_eaT(q + 3, (s + 1) % 2)
                    act.wait_ge(z_scaled, q + 1)
                    nc.scalar.activation(zn[s % 2], zn[s % 2], ACT.Gelu).then_inc(gelu_ready, 1)
                    if inside(q + 2):
                        square(q + 2, s % 2)
            act.wait_ge(rows_stored, stored(1))
            copy_eaT(0, 0)
            copy_eaT(1, 1)
            square(0, 0)
            copy_eaT(2, 0)
            square(1, 1)
            loop(act, TT // 2, tile16, peel_first=True, peel_last=True)

            def stage1(j):
                wait(act, rows_stored, stored(1, j))
                sums(1, j, 2)
                transposed(NT, j)
                act.wait_ge(pre_gelu, 1 + j)
                nc.scalar.activation(TMP, TMP, ACT.Gelu).then_inc(post_gelu, 1)
            act.wait_ge(sums_added, 4 * TT)
            loop(act, NT, stage1)
            for n, at_h in ((2, 2 * NT), (3, 3 * NT)):
                act.wait_ge(sums_added, (2 + 2 * n) * TT)

                def stage23(j):
                    wait(act, rows_stored, stored(n, j))
                    sums(n, j, 1)
                    transposed(at_h, j)
                loop(act, NT, stage23)
            act.wait_ge(sums_added, 10 * TT)

            def stage4(j):
                wait(act, rows_stored, stored(4, j))
                sums(4, j, 1)
                transposed(4 * NT, j)
            loop(act, NT, stage4)
            tile_sum_copies(1)
            act.wait_ge(node_sums_read, 2)
            for n in (5, 6):
                act.wait_ge(sums_added, (2 + 2 * n) * TT)

                def stage56(j):
                    wait(act, rows_stored, stored(n, j))
                    sums(n, j, 1, ACT.Relu)
                loop(act, NT, stage56)

        @block.tensor
        def _(pe):
            mm = nc.tensor.matmul

            def count(g):
                g0 = 2 * CT * g

                def body(i):
                    for h in range(2):
                        pe.wait_ge(onehots_ready, g0 + 2 * i + h + 1)
                        mm(pair[0][:, 512 * h:512 * h + 512], ones_b[:, :], oh[h], start=isinstance(i, int), stop=False, skip_group_check=True).then_inc(counted, 1)
                loop(pe, CT, body, peel_first=True)

            def block_numbers(g):
                pe.wait_ge(cmp_ready, g + 1)
                n = T // 4
                for q in range(4):
                    last = mm(pair[2 + q // 2][0:32, 512 * (q % 2):512 * (q % 2) + n], mask_b[:, 0:32], cmp_b[:, q * n:(q + 1) * n], start=True, stop=True)
                last.then_inc(blocks_in_psum, 1)

            def ranks(g):
                g0 = 2 * CT * g
                pe.wait_ge(seeds_ready, g + 1)
                for h in range(2):
                    for s in range(3):
                        mm(pair[0][:, 512 * h:512 * h + 512], ident_b, part[s][:, 512 * h:512 * h + 512], start=s == 0, stop=False, skip_group_check=True)

                def body(i):
                    for h in range(2):
                        pe.wait_ge(rank_onehots, g0 + 2 * i + h + 1)
                        mm(pair[0][:, 512 * h:512 * h + 512], lower_b, oh[h], start=False, stop=False, skip_group_check=True).then_inc(ranks_in_psum, 1)
                    for h in range(2):
                        pe.wait_ge(ranks_read, g0 + 2 * i + h + 1)
                        mm(pair[0][:, 512 * h:512 * h + 512], rest_b, oh[h], start=False, stop=False, skip_group_check=True).then_inc(carried, 1)
                loop(pe, CT, body)

            for g in range(2):
                count(g)
                block_numbers(g)
                ranks(g)

            def passes(n, g=None):
                g0 = 2 * TT * n

                def turn(i):
                    for h in range(2):
                        pe.wait_ge(sel_ready, g0 + 2 * i + h + 1)
                        if g is not None:
                            wait(pe, tile_sums_ready, 2 * TT * g + 2 * i + h - 1)
                            for c in range(4):
                                last = mm(pair[2 + h][:, 2 * c:2 * c + 2], cols(sel_p[h], c), pairs[:, bass.ds((i * W + 4 * h + c) * 2, 2)], start=True, stop=True)
                            last.then_inc(tile_sums_in_psum, 1)
                        for c in range(4 * h, 4 * h + 4):
                            pe.wait_ge(gathered[c], 16 * (TT * n + i + 1))
                        wait(pe, sums_added, g0 + 2 * i + h - 1)
                        for c in range(4):
                            last = mm(pair[h][:, c * P:(c + 1) * P], ring_128[:, 4 * h + c, :], cols(sel_p[h], c), start=True, stop=True)
                        last.then_inc(sums_in_psum, 1)
                loop(pe, TT, turn, peel_first=True)

            def node_totals(g):
                pe.wait_ge(starts_ready, 2 * g + 1)
                for c in range(TC):
                    last = mm(pair[1][:, c:c + 1], pairs[0:1, c * P:(c + 1) * P], ident[0:1, 0:1], start=True, stop=True)
                last.then_inc(turned_in_psum, 1)
                pe.wait_ge(tile_sums_ready, 2 * TT * (g + 1))
                both = tile_sums.rearrange("p (t k) -> p t k", k=2)
                for k in range(2):
                    if k:
                        pe.wait_ge(turned_ready, 2 * g + 1)
                    for c in range(TC):
                        last = nc.tensor.transpose(pair[2 + c // 8][:, (c % 8) * P:(c % 8 + 1) * P], both[:, c * P:(c + 1) * P, k], ident)
                    last.then_inc(turned_in_psum, 1)
                pe.wait_ge(turned_ready, 2 * g + 2)
                pe.wait_ge(starts_ready, 2 * g + 2)
                for k in range(2):
                    for c in range(TC):
                        last = mm(pair[0][:, 512 * k:512 * k + P], cols(turned[:, k * T:(k + 1) * T], c), cols(work, c), start=c == 0, stop=c == TC - 1)
                last.then_inc(node_sums_in_psum, 1)

            pe.wait_ge(weights_in, 16 * 23)
            pe.wait_ge(blocks_read, 2)
            pe.wait_ge(pairs_ready, 1)
            passes(0, 0)
            node_totals(0)

            pe.wait_ge(node_sums_read, 1)
            for k in range(4):
                nc.tensor.transpose(pair[3][:, k * D:(k + 1) * D], lin[:, k, :], ident)
            for k in range(2):
                last = nc.tensor.transpose(pair[3][:, 512 + k * D:512 + (k + 1) * D], w2[:, k, :], ident)
            last.then_inc(w_psum, 1)
            pe.wait_ge(w_ready, 2)
            for k in range(2):
                mm(pair[2][:, k * D:(k + 1) * D], TMP[:, k * D:(k + 1) * D], wu[:, 1, :], start=True, stop=True)
            pe.wait_ge(b2_spread, 1)
            mm(pair[2][:, 2 * D:3 * D], TMP[:, 2 * D:3 * D], wu[:, 1, :], start=True, stop=True).then_inc(w_psum, 1)

            def transposes(at, j, src=H):
                pe.wait_ge(h_ready, at + 1 + j)
                for b in range(B):
                    last = nc.tensor.transpose(pair[0][:, b * D:(b + 1) * D], cols(src, b), ident)
                last.then_inc(hT_in_psum, 1)

            def times(dst, terms, done, width=D):
                for b in range(B):
                    o = dst(b)
                    for t, (lhs, rhs) in enumerate(terms):
                        last = mm(o, cols(lhs, b), rhs, start=t == 0, stop=t == len(terms) - 1)
                last.then_inc(done, 1)

            def wide(b):
                return pair[1 + b // 4][:, (b % 4) * HID:(b % 4 + 1) * HID]

            def narrow(k):
                return lambda b: pair[k][:, b * D:(b + 1) * D]

            def stage0(j):
                transposes(0, j)
                pe.wait_ge(hT_ready, 1 + j)
                times(wide, [(HT, w1a[:, :])], product)
            pe.wait_ge(w_ready, 4)
            loop(pe, NT, stage0, peel_first=True)

            G1 = 2 * TT

            def sum_edges(q, b):
                pe.wait_ge(gelu_ready, q + 1)
                pe.wait_ge(sel_ready, G1 + q + 1)
                pe.wait_ge(sums_added, G1 + q)
                for a in range(2):
                    for c in range(4):
                        last = mm(pair[0][:, a * 512 + c * P:a * 512 + (c + 1) * P], zn[b][:, c * HID + a * P:c * HID + (a + 1) * P],
                                  cols(sel[b], c), start=True, stop=True)
                last.then_inc(sums_in_psum, 1)

            def turn_features(q, b, t, k):
                pe.wait_ge(recs_in[k], 16 * (t + 1))
                wait(pe, eaT_ready, q - 1)
                r = recs[k].rearrange("p (c w) -> p c w", c=W)
                for c in range(4):
                    last = nc.tensor.transpose(pair[3][0:ED, 512 * b + c * P:512 * b + (c + 1) * P], r[:, 4 * b + c, 4:RD], ident)
                last.then_inc(eaT_in_psum, 1)

            def hidden(q, b, t):
                pe.wait_ge(eaT_ready, q + 1)
                wait(pe, z_free, q - 1)
                for c in range(4 * b, 4 * b + 4):
                    pe.wait_ge(gathered[c], 16 * (TT + t + 1))
                for c in range(4):
                    o = cols(pair[1 + b], c, HID)
                    mm(o, eaT[b][0:ED, c * P:(c + 1) * P], w1b[:, :], start=True, stop=False)
                    last = mm(o, ident, ring3[:, 4 * b + c, :], start=False, stop=True)
                last.then_inc(edge_part, 1)

            def tile16(j):
                for s in range(4):
                    q = 4 * j + s
                    if inside(q - 1):
                        sum_edges(q - 1, (s + 1) % 2)
                    if inside(q + 3):
                        m = (s + 3) // 2
                        turn_features(q + 3, (s + 1) % 2, j + m // 2, m % 2)
                    if inside(q + 2):
                        hidden(q + 2, s % 2, 2 * j + s // 2 + 1)
            pe.wait_ge(rows_stored, stored(1))
            turn_features(0, 0, 0, 0)
            turn_features(1, 1, 0, 0)
            hidden(0, 0, 0)
            turn_features(2, 0, 0, 1)
            hidden(1, 1, 0)
            loop(pe, TT // 2, tile16, peel_first=True, peel_last=True)
            sum_edges(2 * TT - 1, 1)

            def stage1(j):
                transposes(NT, j)
                pe.wait_ge(hT_ready, NT + 1 + j)
                pe.wait_ge(sums_copied, 1 + j)
                times(narrow(1), [(HT, wu[:, 0, :]), (AG[:, 0:BW], w2u[:, 0, :]), (AG[:, BW:2 * BW], w2u[:, 1, :])], product)
            loop(pe, NT, stage1)
            passes(2)
            for n in (2, 3):
                def stage23(j):
                    pe.wait_ge(rows_loaded, loaded(n, j + 1))
                    pe.wait_ge(sums_copied, (n - 1) * NT + 1 + j)
                    times(narrow(1), [(AG[:, 0:BW], wn[:, n - 2, :])], product)
                    for b in range(B):
                        last = nc.tensor.transpose(pair[0][:, b * D:(b + 1) * D], cols(H, b), ident)
                    last.then_inc(hT_in_psum, 1)
                    pe.wait_ge(hT_ready, n * NT + 1 + j)
                    times(narrow(2), [(HT, wl[:, n - 2, :])], product2)
                loop(pe, NT, stage23)
                passes(n + 1)

            def stage4(j):
                pe.wait_ge(sums_copied, 3 * NT + 1 + j)
                times(narrow(1), [(AG[:, 0:BW], linT[:, 0, :])], product)
                transposes(2 * NT, j)
                pe.wait_ge(hT_ready, 4 * NT + 1 + j)
                times(narrow(2), [(HT, linT[:, 1, :])], product2)
            loop(pe, NT, stage4)
            pe.wait_ge(pairs_ready, 2)
            passes(5, 1)
            node_totals(1)
            for n in (5, 6):
                def stage56(j):
                    pe.wait_ge(sums_copied, (n - 1) * NT + 1 + j)
                    times(narrow(1), [(AG[:, 0:BW], linT[:, n - 3, :])], product)
                loop(pe, NT, stage56)
                if n == 5:
                    passes(6)

        @block.vector
        def _(dve):
            v = nc.vector
            ch = Chain(dve, dve_step)
            link, straight = ch.link, ch.straight

            v.memset(src_i, TRASH * P)
            v.memset(dst_i, TRASH * P)
            v.memset(ety_i, 0)
            v.memset(chunk8, 0.0)
            v.memset(ones_b[:, :], 1.0)
            v.memset(idx[:, T:T + W], 0)
            v.memset(ety[:, T:T + W], 0)
            v.memset(pay_d[0], 0.0)
            v.memset(pay_d[1], 0.0).then_inc(fill_ready, 1)
            straight(v.memset(fill_d, 0.0))
            straight(v.memset(fill_s, 0.0))
            v.memset(fill_d.rearrange("p (r w) -> p r w", w=RD)[:, :, 1], -1.0)
            v.memset(fill_s.rearrange("p (r w) -> p r w", w=RS)[:, :, 1], -1.0).then_inc(fill_ready, 1)
            dve.wait_ge(weights_in, 16 * 23)
            v.tensor_copy(cbf[:, 0:4 * P], consts[:, :])
            straight(v.tensor_scalar(rest_b, lower, -1.0, 1.0, ALU.mult, ALU.add))
            for w in (w1a[:, :], w1b[:, :], rows256[:, 0, :]):
                s = small[0:w.shape[0], 0:1]
                straight(v.tensor_reduce(s, w, AX, ALU.add))
                straight(v.tensor_scalar(s, s, -1.0 / HID, None, ALU.mult))
                straight(v.tensor_scalar(w, w, s, None, ALU.add))
            dve.wait_ge(edges_in, 16 * 6)
            dve.wait_ge(fills_done, 16 * 16)
            for ids, blk, place in ((dst_i, blk_d, lod), (src_i, blk_s, los)):
                straight(v.tensor_scalar(tcol_i, ids, 7, None, ALU.arith_shift_right))
                straight(v.tensor_copy(blk, tcol_i))
                straight(v.tensor_scalar(tcol_i, ids, P - 1, None, ALU.bitwise_and))
                straight(v.tensor_copy(place, tcol_i))
            attn_b = attn[:, :].rearrange("p (a k) -> p a k", a=1).to_broadcast([P, CE8, W])
            for q in range(NE8):
                dve.wait_ge(ea8_in, 32 * (q + 1))
                m3 = chunk8[:, 0:CE8 * W].rearrange("p (c k) -> p c k", k=W)
                straight(v.tensor_tensor(m3, m3, attn_b, ALU.mult))
                v.tensor_reduce(tanh_c[:, q * CE8:(q + 1) * CE8], m3, AX, ALU.add).then_inc(tanh_dot, 1)

            def onehot(h, i, blk):
                for c in range(4):
                    last = v.tensor_scalar(cols(oh[h], c), iota_b, blk[:, bass.ds(i * W + 4 * h + c, 1)], None, ALU.is_equal)
                return last

            def count(g, blk):
                g0 = 2 * CT * g
                wait(dve, carried, g0)

                def body(i):
                    for h in range(2):
                        wait(dve, counted, g0 + 2 * (i - 1) + h + 1)
                        onehot(h, i, blk).then_inc(onehots_ready, 1)
                loop(dve, CT, body, peel_first=True)

            def plan(g, off):
                dve.wait_ge(counted, 2 * CT * (g + 1))
                straight(v.tensor_copy(cnt, pair[0][:, :]))
                total = ping[0]
                straight(v.tensor_reduce(total, cnt.rearrange("p (k b) -> p b k", k=W), AX, ALU.add))
                ti = base_i[:, 0:P]
                straight(v.tensor_copy(ti, total))
                straight(v.tensor_scalar(ti, ti, P - 1, None, ALU.add))
                straight(v.tensor_scalar(ti, ti, 7, None, ALU.arith_shift_right))
                tiles = cols(base, 1)
                straight(v.tensor_copy(tiles, ti))
                straight(v.memset(tiles[:, NB:P], 0.0))
                straight(v.tensor_copy(ping[0], tiles))
                a = 0
                for s in (1, 2, 4, 8, 16, 32, 64):
                    straight(v.tensor_copy(ping[1 - a][:, 0:s], ping[a][:, 0:s]))
                    straight(v.tensor_tensor(ping[1 - a][:, s:P], ping[a][:, s:P], ping[a][:, 0:P - s], ALU.add))
                    a = 1 - a
                ends, spare = ping[a], ping[1 - a]
                straight(v.tensor_tensor(spare, ends, ident, ALU.mult))
                straight(v.tensor_reduce(small[:, 0:1], spare, AX, ALU.add))
                v.tensor_scalar(cmp_b, trow, small[:, 0:1], None, ALU.is_ge).then_inc(cmp_ready, 1)
                straight(v.tensor_tensor(spare, ends, tiles, ALU.subtract))
                straight(v.tensor_scalar(cols(base, 0), spare, float(P), None, ALU.mult))
                straight(v.memset(cols(base, 0)[:, TRASH:P], float(T * P)))
                for k in range(1, W):
                    straight(v.tensor_tensor(cols(base, k), cols(base, k - 1), cols(cnt, k - 1), ALU.add))
                straight(v.tensor_copy(base_i, base))
                ci = cnt.bitcast(I32)
                for s, bits in enumerate((0xFF, 0xFF00, 0xFF0000)):
                    straight(v.tensor_scalar(ci, base_i, bits, None, ALU.bitwise_and))
                    straight(v.tensor_copy(part[s], ci))
                dve.sem_inc(seeds_ready)
                dve.wait_ge(blocks_in_psum, g + 1)
                n = T // 4
                for q in range(4):
                    last = v.tensor_scalar(off[:, q * n:(q + 1) * n], pair[2 + q // 2][0:32, 512 * (q % 2):512 * (q % 2) + n], float(P), None, ALU.mult)
                last.then_inc(blocks_read, 1)

            def ranks(g, blk, pay, fields, words):
                g0 = 2 * CT * g

                def body(j):
                    for k in range(2):
                        i = 2 * j + k
                        for h in range(2):
                            wait(dve, carried, g0 + 2 * (i - 1) + h + 1)
                            onehot(h, i, blk).then_inc(rank_onehots, 1)
                        for h in range(2):
                            dve.wait_ge(ranks_in_psum, g0 + 2 * i + h + 1)
                            v.tensor_tensor(prod[h], oh[h], pair[0][:, 512 * h:512 * h + 512], ALU.mult).then_inc(ranks_read, 1)
                        for h in range(2):
                            dve.wait_ge(ranks_read, g0 + 2 * i + h + 1)
                            link(v.tensor_reduce(pos[:, 4 * h:4 * h + 4], prod[h].rearrange("p (c b) -> p c b", c=4), AX, ALU.add))
                        link(v.tensor_copy(pos_i[0], pos))
                        link(v.tensor_scalar(pos_i[1], pos_i[0], P - 1, None, ALU.bitwise_and))
                        link(v.tensor_scalar(pos_i[2], pos_i[0], 7, None, ALU.arith_shift_right))
                        wait(dve, scattered[k], 16 * W * (CT // 2 * g + j))
                        link(v.scalar_tensor_tensor(out=row_i[k], in0=pos_i[1], scalar=float(ROWS), in1=pos_i[2], op0=ALU.mult, op1=ALU.add))
                        pv = pay[k].rearrange("p (c w) -> p c w", c=W)
                        for w, field in fields:
                            last = v.tensor_copy(pv[:, :, w].bitcast(field.dtype), field[:, bass.ds(i * W, W)])
                        link(last)
                        dve.sem_inc(payload_ready)
                ch.run(CT // 2, body, 14, peel_first=True)

            dve.wait_ge(tanh_ready, 1)
            count(0, blk_d)
            plan(0, off)
            ranks(0, blk_d, pay_d, [(0, src_i), (1, lod), (2, ety_i), (3, tanh_c)], RD)
            count(1, blk_s)
            plan(1, off_s)
            ranks(1, blk_s, pay_s, [(0, dst_i), (1, los)], RS)

            dve.wait_ge(carried, 4 * CT)
            dve.wait_ge(scattered[0], 16 * W * CT)
            dve.wait_ge(scattered[1], 16 * W * CT)
            n = T // NRB
            pt = pairs.rearrange("p (t k) -> p t k", k=2)
            straight(v.memset(pairs, 1.0))
            for q in range(NRB):
                dve.wait_ge(regrouped, 16 * (q + 1))
                r = fill_d[:, 0:n * RD].rearrange("p (t w) -> p t w", w=RD)
                at = slice(q * n, (q + 1) * n)
                v.tensor_copy(idx[:, at], r[:, :, 0].bitcast(I32))
                v.tensor_copy(loc[:, at], r[:, :, 1])
                v.tensor_copy(pt[:, at, 0], r[:, :, 3])
                v.tensor_copy(ety[:, at], r[:, :, 2].bitcast(I32)).then_inc(columns_ready, 1)
            dve.wait_ge(columns_ready, NRB)
            dve.sem_inc(pairs_ready)
            offs = [dve.alloc_register(f"off{k}") for k in range(W)]

            def choose(dst, i, h):
                for c in range(4):
                    last = v.tensor_scalar(cols(dst, c), iota, loc[:, bass.ds(i * W + 4 * h + c, 1)], None, ALU.is_equal)
                last.then_inc(sel_ready, 1)

            def add_sum(h, c, psum, halves):
                o = dve.snap(offs[4 * h + c], min_val=0, max_val=NB * P)
                if halves == 2:
                    dst = acc2[:, :, bass.ds(o, P)]
                    srcv = psum.rearrange("p (a c n) -> p a c n", a=2, c=4)[:, :, c, :]
                else:
                    dst = acc[:, bass.ds(ACCW + o, P)]
                    srcv = cols(psum, c)
                return v.tensor_tensor(dst, dst, srcv, ALU.add)

            def tiles(n, offset, start):
                g0 = 2 * TT * n
                if start is None:
                    straight(v.memset(acc[:, ACCW:2 * ACCW], 0.0))
                else:
                    dve.wait_ge(rel_moved, start)

                def turn(i):
                    dve.load(offs, offset[0:1, bass.ds(i * W, W)])
                    for h in range(2):
                        wait(dve, sums_in_psum, g0 + 2 * i + h - 1)
                        choose(sel_p[h], i, h)
                    for h in range(2):
                        dve.wait_ge(sums_in_psum, g0 + 2 * i + h + 1)
                        for c in range(4):
                            link(add_sum(h, c, pair[h][:, 0:512], 1))
                        dve.sem_inc(sums_added)
                ch.run(TT, turn, 8, peel_first=True)

            def node_totals(g, offset):
                dve.wait_ge(tile_sums_in_psum, 2 * TT * (g + 1))
                v.tensor_copy(pairs[0:1, 0:T], offset[0:1, :]).then_inc(starts_ready, 1)
                dve.wait_ge(turned_in_psum, 3 * g + 1)
                dve.wait_ge(sums_in_psum, 2 * TT * (1 if g == 0 else 6))
                straight(v.tensor_scalar(tile_block, pair[1][:, 0:TC], 1.0 / P, None, ALU.mult))
                for c in range(TC):
                    last = v.tensor_scalar(cols(work, c), iota, tile_block[:, c:c + 1], None, ALU.is_equal)
                last.then_inc(starts_ready, 1)
                dve.wait_ge(node_sums_in_psum, g + 1)
                both = node_sums[:, :].rearrange("p (k n) -> p k n", k=2)
                straight(v.tensor_copy(both, pair[0][:, :].rearrange("p (k n) -> p k n", k=2)[:, :, 0:P]))
                dve.sem_inc(node_sums_read)

            tiles(0, off, None)
            node_totals(0, off)
            straight(v.memset(beta[:, NB:P], 0.0))
            straight(v.tensor_scalar(beta[:, 0:NB], node_sums[:, 0:NB], 1.0 / N, None, ALU.mult))
            one = beta[:, 0:NB].rearrange("p (b a) -> p b a", a=1)
            straight(v.tensor_reduce(norm_d[:, 0:NB], one, AX, ALU.max))
            v.tensor_tensor(beta[:, 0:NB], beta[:, 0:NB], norm_d[:, 0:NB], ALU.subtract).then_inc(beta_ready, 1)
            dve.wait_ge(beta_exp, 1)
            straight(v.tensor_reduce(norm_d[:, 0:NB], one, AX, ALU.add))
            straight(v.reciprocal(norm_d[:, 0:NB], norm_d[:, 0:NB]))
            straight(v.tensor_tensor(beta[:, 0:NB], beta[:, 0:NB], norm_d[:, 0:NB], ALU.mult))
            straight(v.tensor_copy(deg[:, :], node_sums[:, P:2 * P]))
            straight(v.tensor_scalar(norm_d[:, :], deg[:, :], 1.0, None, ALU.max))
            straight(v.reciprocal(norm_d[:, :], norm_d[:, :]))
            straight(v.tensor_scalar(node_sums[:, 0:P], deg[:, :], 0.0, None, ALU.is_gt))
            straight(v.tensor_tensor(norm_d[:, :], norm_d[:, :], node_sums[:, 0:P], ALU.mult))

            dve.wait_ge(w_ready, 2)
            v.tensor_scalar(TMP[:, 2 * D:3 * D], ident, 0.0, b2col[:, 0:1], ALU.mult, ALU.add).then_inc(b2_spread, 1)
            dve.wait_ge(w_ready, 4)

            def three(x):
                return x.rearrange("p (b f) -> p b f", b=B)

            def per_block(s):
                return s.rearrange("p (b a) -> p b a", a=1).to_broadcast([P, B, D])

            def every(row, width=D):
                return row.rearrange("p (a f) -> p a f", a=1).to_broadcast([P, B, width])

            def rsqrt_steps(y, x, t):
                yield lambda: v.tensor_scalar(t.bitcast(I32), x.bitcast(I32), 1, None, ALU.arith_shift_right)
                yield lambda: v.tensor_scalar(y.bitcast(I32), t.bitcast(I32), -1.0, float(0x5F3759DF), ALU.mult, ALU.add)
                for _ in range(3):
                    yield lambda: v.scalar_tensor_tensor(out=t, in0=y, scalar=-0.5, in1=y, op0=ALU.mult, op1=ALU.mult)
                    yield lambda: v.tensor_tensor(t, t, x, ALU.mult)
                    yield lambda: v.scalar_tensor_tensor(out=y, in0=t, scalar=1.5, in1=y, op0=ALU.add, op1=ALU.mult)
            RSQ = 11
            LN = 7 + RSQ

            def normalise(src, dst, tmp):
                link(v.tensor_reduce(st1, three(src), AX, ALU.add))
                link(v.tensor_scalar(st1, st1, 1.0 / D, None, ALU.mult))
                link(v.tensor_tensor(three(dst), three(src), per_block(st1), ALU.subtract))
                link(v.tensor_tensor(tmp, dst, dst, ALU.mult))
                link(v.tensor_reduce(st2, three(tmp), AX, ALU.add))
                link(v.tensor_scalar(st2, st2, 1.0 / D, EPS, ALU.mult, ALU.add))
                for make in rsqrt_steps(st3, st2, st1):
                    link(make())
                link(v.tensor_tensor(three(dst), three(dst), per_block(st3), ALU.mult))

            def stage0(j):
                dve.wait_ge(rows_loaded, 16 + 16 * j if not (isinstance(j, int) and j == NT - 1) else 16 * NT + NX)
                normalise(X, H, TMP)
                v.tensor_scalar(H, H, 0.0, None, ALU.max).then_inc(h_ready, 1)
                dve.wait_ge(product, 1 + j)
                o = OUT.rearrange("p (b f) -> p b f", b=B)
                b1 = rows256[:, 0:1, :]
                v.tensor_tensor(o[:, 0:4, :], pair[1][:, :].rearrange("p (b f) -> p b f", b=4), b1.to_broadcast([P, 4, HID]), ALU.add)
                v.tensor_tensor(o[:, 4:7, :], pair[2][:, 0:3 * HID].rearrange("p (b f) -> p b f", b=3), b1.to_broadcast([P, 3, HID]), ALU.add).then_inc(result_ready, 1)
            ch.run(NT, stage0, LN, peel_first=True, peel_last=True)

            dve.wait_ge(rel_moved, 16)
            straight(v.memset(acc[:, :], 0.0))
            dve.wait_ge(rows_stored, stored(1))
            G1 = 2 * TT

            def deviations(b):
                yield lambda: v.tensor_scalar(rs_x, ssq[b], 1.0 / HID, EPS, ALU.mult, ALU.add)
                yield from rsqrt_steps(rstd[b], rs_x, rs_t)

            def sums_of(h):
                for c in range(4):
                    yield lambda c=c: add_sum(h, c, pair[0][:, :], 2)

            def in_turn(*chains):
                chains = [[c, None] for c in chains]
                while chains:
                    for item in list(chains):
                        make = next(item[0], None)
                        if make is None:
                            chains.remove(item)
                            continue
                        if item[1] is not None:
                            ch.after(item[1])
                        item[1] = ch.step(make())
                ch.after(ch.at + ch.k)

            def tile16(j):
                for s in range(4):
                    q, b = 4 * j + s, s % 2
                    dve.wait_ge(sums_in_psum, G1 + q - 1)
                    for c in range(4):
                        last = v.scalar_tensor_tensor(out=cols(zn[b], c, HID), in0=cols(pair[1 + b], c, HID), scalar=rstd[b][:, c:c + 1], in1=rows256[:, 1, :], op0=ALU.mult, op1=ALU.mult)
                    last.then_inc(z_free, 1)
                    choose(sel[b], 2 * j + s // 2, b)
                    dve.wait_ge(z_free, q + 1)
                    z4 = zn[b].rearrange("p (c f) -> p c f", c=4)
                    v.tensor_tensor(z4, z4, rows256[:, 2:3, :].to_broadcast([P, 4, HID]), ALU.add).then_inc(z_scaled, 1)
                    chains = []
                    if inside(q - 1):
                        dve.wait_ge(sums_in_psum, G1 + q)
                        chains.append(sums_of(1 - b))
                    if inside(q + 1):
                        dve.wait_ge(squares, q + 2)
                        chains.append(deviations(1 - b))
                    in_turn(*chains)
                    if inside(q - 1):
                        dve.sem_inc(sums_added)
                    if b == 0:
                        dve.load(offs, off[0:1, bass.ds((2 * j + s // 2) * W, W)])
            dve.wait_ge(squares, 1)
            ch.at, ch.k = ch.done, 0
            in_turn(deviations(0))
            ch.done += ch.k
            ch.run(TT // 2, tile16, 4 * (4 + 1 + RSQ), peel_first=True, peel_last=True)
            dve.wait_ge(sums_in_psum, G1 + 2 * TT)
            ch.at, ch.k = ch.done, 0
            in_turn(sums_of(1))
            ch.done += ch.k
            dve.sem_inc(sums_added)

            def stage1(j):
                dve.wait_ge(rows_loaded, loaded(1, j + 1))
                normalise(X, H, TMP)
                v.tensor_scalar(H, H, 0.0, None, ALU.max).then_inc(h_ready, 1)
                dve.wait_ge(product, NT + 1 + j)
                dve.wait_ge(h_ready, NT + 1 + j)
                for b in range(B):
                    last = v.scalar_tensor_tensor(out=cols(TM2, b), in0=vrow[:, :], scalar=deg[:, bass.ds(j * B + b, 1)], in1=pair[1][:, b * D:(b + 1) * D], op0=ALU.mult, op1=ALU.add)
                link(last)
                link(v.tensor_tensor(three(TM2), three(TM2), every(rows128[:, 0, :]), ALU.add))
                normalise(TM2, TMP, TM2)
                link(v.tensor_tensor(three(TMP), three(TMP), every(rows128[:, 1, :]), ALU.mult))
                link(v.tensor_tensor(three(TMP), three(TMP), every(rows128[:, 2, :]), ALU.add))
                dve.sem_inc(pre_gelu)
                dve.wait_ge(post_gelu, 1 + j)
                link(v.tensor_tensor(TM2, TMP, H, ALU.add))
                link(v.tensor_tensor(TM2, TM2, X, ALU.add))
                dve.sem_inc(result_ready)
                normalise(TM2, H, TMP)
                v.tensor_scalar(H, H, 0.0, None, ALU.max).then_inc(result_ready, 1)
            ch.run(NT, stage1, 3 * LN + 6)
            tiles(2, off, 32)

            for n in (2, 3):
                def stage23(j):
                    dve.wait_ge(product, n * NT + 1 + j)
                    dve.wait_ge(product2, (n - 2) * NT + 1 + j)
                    link(v.tensor_copy(TMP, pair[2][:, 0:BW]))
                    for b in range(B):
                        last = v.scalar_tensor_tensor(out=cols(TMP, b), in0=pair[1][:, b * D:(b + 1) * D], scalar=norm_d[:, bass.ds(j * B + b, 1)], in1=cols(TMP, b), op0=ALU.mult, op1=ALU.add)
                    link(last)
                    if n == 2:
                        v.scalar_tensor_tensor(out=TM2, in0=TMP, scalar=SLOPE, in1=TMP, op0=ALU.mult, op1=ALU.max).then_inc(result_ready, 1)
                    else:
                        link(v.scalar_tensor_tensor(out=TM2, in0=TMP, scalar=SLOPE, in1=TMP, op0=ALU.mult, op1=ALU.max))
                        v.tensor_tensor(TM2, TM2, X, ALU.add).then_inc(result_ready, 1)
                        dve.wait_ge(result_ready, RES[3] + 1 + 2 * j)
                        normalise(TM2, HT, TMP)
                        v.tensor_scalar(HT, HT, 0.0, None, ALU.max).then_inc(result_ready, 1)
                if n == 3:
                    dve.wait_ge(rows_loaded, loaded(2, NT))
                ch.run(NT, stage23, 2 if n == 2 else 3 + LN)
                dve.wait_ge(rows_stored, stored(n + 1))
                if n == 2:
                    tiles(3, off, 48)
                else:
                    dve.wait_ge(sums_copied, n * NT)
                    tiles(4, off, None)

            def stage4(j):
                dve.wait_ge(rows_loaded, loaded(4, j + 1))
                dve.wait_ge(product, 4 * NT + 1 + j)
                for b in range(B):
                    last = v.scalar_tensor_tensor(out=cols(TM2, b), in0=pair[1][:, b * D:(b + 1) * D], scalar=beta[:, bass.ds(j * B + b, 1)], in1=cols(X, b), op0=ALU.mult, op1=ALU.add)
                last.then_inc(result_ready, 1)
                dve.wait_ge(result_ready, RES[4] + 1 + 2 * j)
                normalise(TM2, H, TMP)
                v.tensor_scalar(H, H, 0.0, None, ALU.max).then_inc(h_ready, 1)
                dve.wait_ge(product2, 2 * NT + 1 + j)
                v.tensor_tensor(three(TMP), pair[2][:, 0:BW].rearrange("p (b f) -> p b f", b=B), every(rows128[:, 3, :]), ALU.add).then_inc(result_ready, 1)
            ch.run(NT, stage4, LN)
            dve.wait_ge(rows_stored, stored(5))
            dve.wait_ge(regrouped, 16 * (NRB + 1))
            dve.wait_ge(idx_copied, 5 * (TT + 1))
            r = acc[:, 0:T * RS].rearrange("p (t w) -> p t w", w=RS)
            v.tensor_copy(idx[:, 0:T], r[:, :, 0].bitcast(I32))
            straight(v.tensor_copy(loc[:, :], r[:, :, 1]))
            straight(v.memset(pairs, 1.0))
            dve.sem_inc(columns_ready)
            dve.sem_inc(pairs_ready)
            dve.wait_ge(sums_copied, 4 * NT)
            tiles(5, off_s, None)
            node_totals(1, off_s)
            straight(v.tensor_scalar(deg[:, :], node_sums[:, P:2 * P], 1.0, None, ALU.max))
            straight(v.reciprocal(deg[:, :], deg[:, :]))
            for n in (5, 6):
                def stage56(j):
                    if n == 6:
                        dve.wait_ge(rows_loaded, loaded(6, j + 1))
                    dve.wait_ge(product, n * NT + 1 + j)
                    for b in range(B):
                        last = v.scalar_tensor_tensor(out=cols(TM2, b), in0=pair[1][:, b * D:(b + 1) * D], scalar=deg[:, bass.ds(j * B + b, 1)], in1=rows128[:, n - 1, :], op0=ALU.mult, op1=ALU.add)
                    if n == 6:
                        link(last)
                        last = v.tensor_tensor(TM2, TM2, X, ALU.add)
                    last.then_inc(result_ready, 1)
                ch.run(NT, stage56, n - 5, peel_last=n == 6)
                if n == 5:
                    dve.wait_ge(rows_stored, stored(6))
                    dve.wait_ge(sums_copied, 5 * NT)
                    tiles(6, off_s, None)


TC = T // P
CE8 = 112
NE8 = C // CE8
NRB = 8
RES = [0, NT, 3 * NT, 4 * NT, 6 * NT, 8 * NT, 9 * NT]
assert C % CE8 == 0 and T % NRB == 0 and CE8 * W <= W * P

_INS = ['x', 'src', 'dst', 'edge_attr_32', 'edge_attr_8', 'edge_type_460', 'L0_gnn_W1', 'L0_gnn_b1', 'L0_gnn_g1',
        'L0_gnn_be1', 'L0_gnn_W2', 'L0_gnn_b2', 'L0_gnn_Wu', 'L0_gnn_bu', 'L0_gnn_gu', 'L0_gnn_beu',
        'L1_gnn_rel_emb', 'L1_gnn_w_neighbor', 'L1_gnn_w_loop', 'L2_gnn_w_attn', 'L2_gnn_W_lin', 'L3_gnn_W1',
        'L3_gnn_b1', 'L3_gnn_W2', 'L3_gnn_b2', 'L3_gnn_W3', 'L3_gnn_b3']


def kernel(**inputs):
    import numpy as _np
    import concourse.bacc as _bacc
    from concourse import mybir as _mybir
    from concourse.bass_utils import run_bass_kernel_spmd as _run

    nc = _bacc.Bacc("TRN2", target_bir_lowering=False, num_devices=1)
    arrays, aps = {}, {}
    given = {name: _np.ascontiguousarray(inputs[name]) for name in _INS}
    k = _np.arange(P)
    given["shape_consts"] = _np.concatenate(
        [k[:, None] == k, _np.broadcast_to(k, (P, P)), k[:, None] < k, _np.broadcast_to(k[:, None] < NB, (P, P))],
        axis=1).astype(_np.float32)
    given["tile_numbers"] = _np.arange(T, dtype=_np.float32)[None, :]
    for name, a in given.items():
        arrays[f"in_{name}_dram"] = a
        aps[name] = nc.dram_tensor(f"in_{name}_dram", a.shape, _mybir.dt.from_np(a.dtype), kind="ExternalInput").ap()
    out = nc.dram_tensor("out_0_dram", (N, D), F32, kind="ExternalOutput").ap()
    build(nc, aps, out)
    r = _run(nc, [arrays], core_ids=[0])
    return r.results[0]["out_0_dram"]
```

```python
from contextlib import ExitStack

import concourse.bass as bass
from concourse import mybir

P = 128
N = 12500
E = 200000
D = 128
HID = 256
ED = 32
NB = -(-N // P)
NPAD = NB * P
W = 8
C = -(-E // (P * W)) * W
CT = C // W
LAST = E - (P - 1) * C
T = -(-(E // P + NB) // (2 * W)) * 2 * W
TT = T // W
ROWS = T + W
RD = 4 + ED
RS = 2
ACCW = (NB + 1) * P
B = 7
NT = NB // B
BW = B * D
HALF = NT // 2
WORK = 13 * BW
TRASH = P - 1
EPS = 1e-5
SLOPE = 11.0 / 48.0

assert NB % B == 0 and NT % 2 == 0 and LAST % W == 0 and LAST > 0 and CT % 2 == 0 and TT % 2 == 0
assert T >= (E + NB * (P - 1)) // P + 1 and ROWS - T >= (P * C - E) // P + 2

F32 = mybir.dt.float32
BF16 = mybir.dt.bfloat16
I32 = mybir.dt.int32
ALU = mybir.AluOpType
ACT = mybir.ActivationFunctionType
AX = mybir.AxisListType.X


def build(nc, A, out):
    ctx = ExitStack()
    with ctx:
        def sb(name, shape, dt=F32):
            return ctx.enter_context(nc.sbuf_tensor(name, shape, dt))

        def sem(name):
            return ctx.enter_context(nc.semaphore(name))

        def dram(name, shape, dt=F32):
            return nc.dram_tensor(name, shape, dt).ap()

        rec_d = dram("rec_d", [P * ROWS, RD])
        rec_s = dram("rec_s", [P * ROWS, RS])
        rel_sums = dram("rel_sums", [P, ACCW])
        tab_p = dram("tab_p", [NPAD, HID])
        x1, x2, x3 = (dram(f"x{k}_rows", [NPAD, D]) for k in (1, 2, 3))
        h1, h2, h4, g1t, g2t = (dram(n, [NPAD, D]) for n in ("h1_rows", "h2_rows", "h4_rows", "l3a_rows", "l3b_rows"))

        acc = sb("acc", [P, 2 * ACCW])
        acc2 = acc[:, :].rearrange("p (a n) -> p a n", a=2)
        idx = sb("idx", [P, T + W], I32)
        ety = sb("ety", [P, T + W], I32)
        loc = sb("loc", [P, T])
        off = sb("off", [32, T], I32)
        off_s = sb("off_s", [32, T], I32)
        work = sb("work", [P, WORK])

        consts = sb("consts", [P, 4 * P])
        ident, iota, lower, mask = (consts[:, k * P:(k + 1) * P] for k in range(4))
        cbf = sb("cbf", [P, 5 * P], BF16)
        ident_b, iota_b, lower_b, mask_b, rest_b = (cbf[:, k * P:(k + 1) * P] for k in range(5))
        ones_b = sb("ones_b", [P, P], BF16)
        w1a = sb("w1a", [P, HID])
        w1b_two = [sb(f"w1b_{k}", [P, HID]) for k in range(2)]
        rows256 = sb("rows256", [P, 3, HID])
        rows128 = sb("rows128", [P, 6, D])
        b2col = sb("b2col", [P, 1])
        attn = sb("attn", [P, W])
        w2 = sb("w2", [P, 2, D])
        wu = sb("wu", [P, 2, D])
        wn = sb("wn", [P, 2, D])
        wl = sb("wl", [P, 2, D])
        lin = sb("lin", [P, 4, D])
        linT = sb("linT", [P, 4, D])
        w2u = sb("w2u", [P, 2, D])
        vrow = sb("vrow", [P, D])
        deg = sb("deg", [P, P])
        node_sums = sb("node_sums", [P, 2 * P])
        beta = sb("beta", [P, P])
        norm_d = sb("norm_d", [P, P])
        small = sb("small", [P, 64])

        pair = [ctx.enter_context(nc.psum_tensor(f"pair{k}", [P, 1024], F32)) for k in range(4)]

        def acc_view(at, n):
            return acc[:, at:at + n]
        src_i, dst_i, ety_i, blk_d, lod, blk_s, los, tanh_c = (acc_view(k * C, C) for k in range(8))
        src_i, dst_i, ety_i = (v.bitcast(I32) for v in (src_i, dst_i, ety_i))
        FILL = ROWS // 8
        fill_d = acc_view(8 * C, FILL * RD)
        fill_s = acc_view(8 * C + FILL * RD, FILL * RS)
        trow = acc_view(8 * C + FILL * (RD + RS), T)
        tcol_i = fill_d[:, 0:C].bitcast(I32)

        at = [0]

        def ws(n, dt=F32):
            v = work[:, at[0]:at[0] + n]
            at[0] += n
            return v if dt == F32 else v.bitcast(dt)

        oh = [ws(W // 2 * P // 2, BF16) for _ in range(2)]
        oh_s = [ws(W // 2 * P // 2, BF16) for _ in range(2)]
        prod = [ws(W // 2 * P) for _ in range(2)]
        pay_d = [ws(W * RD) for _ in range(2)]
        pay_s = [ws(W * RS) for _ in range(2)]
        cnt = ws(W * P)
        base = ws(W * P)
        base_i = ws(W * P, I32)
        part = [ws(W * P // 2, BF16) for _ in range(3)]
        cmp_b = ws(T // 2, BF16)
        ping = [ws(P) for _ in range(2)]
        assert at[0] <= WORK
        pos = small[:, 0:8]
        pos_i = [small[:, 8 * k:8 * k + 8].bitcast(I32) for k in (1, 2, 3)]
        row_i = [small[:, 8 * k:8 * k + 8].bitcast(I32) for k in (4, 5)]
        chunk8 = cnt
        at[0] = 0
        ring = ws(W * HID)
        ring3 = ring.rearrange("p (k f) -> p k f", k=W)
        sel = [ws(W // 2 * P) for _ in range(2)]
        recs = [ws((W - 2) * RD + P) for _ in range(2)]
        eaT = [ws(2 * P) for _ in range(2)]
        zn = [ws(W // 2 * HID) for _ in range(2)]
        sq = ws(W // 2 * HID)
        assert at[0] <= WORK
        idx_r = [small[:, 8 * k:8 * k + 8].bitcast(I32) for k in (0, 1)]
        ssq = [small[:, 16 + 4 * k:20 + 4 * k] for k in range(2)]
        rs_x, rs_t = small[:, 24:28], small[:, 28:32]
        rstd = [small[:, 32 + 4 * k:36 + 4 * k] for k in range(2)]
        at[0] = W * D + W // 2 * P * 2
        ring_128 = work[:, 0:W * D].rearrange("p (k f) -> p k f", k=W)
        sel_p = [work[:, W * D + k * (W // 2) * P:W * D + (k + 1) * (W // 2) * P] for k in range(2)]
        pairs = ws(2 * T)
        tile_sums = ws(2 * T)
        turned = pairs
        tile_block = ws(TC)
        assert at[0] <= WORK
        at[0] = 0
        X, H, HT, TM2, G = ([ws(BW) for _ in range(2)] for _ in range(5))
        TMP = ws(BW)
        AG2 = ws(2 * BW)
        AG = [AG2[:, 0:BW], AG2[:, BW:2 * BW]]
        WIDE = [work[:, 6 * BW:8 * BW], AG2]
        assert at[0] <= WORK
        st1, st2, st3 = small[:, 32:39], small[:, 40:47], small[:, 48:55]

        def cols(ap, k, n=P):
            return ap[:, k * n:(k + 1) * n]

        weights_in = sem("weights_in")
        edges_in = sem("edges_in")
        ea8_in = sem("ea8_in")
        fill_ready = sem("fill_ready")
        fills_done = sem("fills_done")
        dve_step = sem("dve_step")
        tanh_dot = sem("tanh_dot")
        tanh_ready = sem("tanh_ready")
        onehots_ready = sem("onehots_ready")
        counted = sem("counted")
        cmp_ready = sem("cmp_ready")
        blocks_in_psum = sem("blocks_in_psum")
        blocks_read = sem("blocks_read")
        seeds_ready = sem("seeds_ready")
        rank_onehots = sem("rank_onehots")
        ranks_in_psum = sem("ranks_in_psum")
        ranks_read = sem("ranks_read")
        carried = sem("carried")
        payload_ready = sem("payload_ready")
        ea_in = [sem(f"ea_in{k}") for k in range(2)]
        scattered = [sem(f"scattered{k}") for k in range(2)]
        pool_turn = sem("pool_turn")
        sp_turn = sem("sp_turn")
        regrouped = sem("regrouped")
        pairs_ready = sem("pairs_ready")
        tile_sums_in_psum = sem("tile_sums_in_psum")
        tile_sums_ready = sem("tile_sums_ready")
        starts_ready = sem("starts_ready")
        turned_in_psum = sem("turned_in_psum")
        turned_ready = sem("turned_ready")
        node_sums_in_psum = sem("node_sums_in_psum")
        node_sums_read = sem("node_sums_read")
        z_free = sem("z_free")
        rec_ends_clear = sem("rec_ends_clear")
        b2_spread = sem("b2_spread")
        rel_moved = sem("rel_moved")
        columns_ready = sem("columns_ready")
        w_psum = sem("w_psum")
        w_ready = sem("w_ready")
        beta_ready = sem("beta_ready")
        beta_exp = sem("beta_exp")
        idx_copied = sem("idx_copied")
        gathered = [sem(f"gathered{k}") for k in range(W)]
        sel_ready = sem("sel_ready")
        sums_in_psum = sem("sums_in_psum")
        sums_added = sem("sums_added")
        recs_in = [sem(f"recs_in{k}") for k in range(2)]
        eaT_in_psum = sem("eaT_in_psum")
        eaT_ready = sem("eaT_ready")
        edge_part = sem("edge_part")
        squares = sem("squares")
        z_scaled = sem("z_scaled")
        gelu_ready = sem("gelu_ready")
        rows_loaded = [sem(f"rows_loaded{k}") for k in range(2)]
        h_ready = sem("h_ready")
        hT_in_psum = sem("hT_in_psum")
        hT_ready = sem("hT_ready")
        sums_copied = sem("sums_copied")
        product = sem("product")
        product2 = sem("product2")
        pre_gelu = sem("pre_gelu")
        post_gelu = sem("post_gelu")
        result_ready = sem("result_ready")
        rows_stored = [sem(f"rows_stored{k}") for k in range(2)]
        result2_ready = sem("result2_ready")
        product2_read = sem("product2_read")

        def wait(eng, s, value):
            if not (isinstance(value, int) and value <= 0):
                eng.wait_ge(s, value)

        class Chain:

            def __init__(self, eng, s):
                self.eng, self.s, self.done, self.k, self.at = eng, s, 0, 0, 0

            def step(self, ins):
                self.k += 1
                ins.then_inc(self.s, 1)
                return self.at + self.k

            def after(self, count):
                self.eng.wait_ge(self.s, count)

            def link(self, ins):
                self.after(self.step(ins))

            def straight(self, ins):
                self.done += 1
                ins.then_inc(self.s, 1)
                self.eng.wait_ge(self.s, self.done)

            def part(self, body):
                self.at, self.k = self.done, 0
                body()
                self.done += self.k

            def run(self, n, body, per, peel_first=False, peel_last=False):
                lo, hi = int(peel_first), n - int(peel_last)

                if peel_first:
                    self.part(lambda: body(0))
                with self.eng.Fori(lo, hi) as i:
                    self.at, self.k = self.done + (i - lo) * per, 0
                    body(i)
                    assert self.k == per, (self.k, per)
                self.done += (hi - lo) * per
                if peel_last:
                    self.part(lambda: body(n - 1))

        def inside(q):
            return not isinstance(q, int) or 0 <= q < 2 * TT

        def loop(eng, n, body, peel_first=False, peel_last=False):
            lo, hi = int(peel_first), n - int(peel_last)
            if peel_first:
                body(0)
            with eng.Fori(lo, hi) as i:
                body(i)
            if peel_last:
                body(n - 1)

        TABLES = {0: (A["L1_gnn_rel_emb"], ety), 2: (h1, idx), 3: (h2, idx), 4: (h4, idx), 5: (g1t, idx), 6: (g2t, idx)}
        STORES = [1, 2, 1, 2, 2, 1, 1]
        LOADS = [1, 1, 1, 2, 1, 0, 1]

        def stored(n, m=0):
            return 16 * HALF * sum(STORES[:n]) + (16 * STORES[n] * m if not isinstance(m, int) or m else 0)

        def loaded(n, k, m):
            parts = k * min(n, 2)
            if n < 2 and k == 1 and isinstance(m, int) and m == HALF - 1:
                parts += 1
            return 16 * HALF * sum(LOADS[:n]) + 16 * parts + 16 * LOADS[n] * (m + 1)

        def all_stored(eng, n):
            for k in range(2):
                eng.wait_ge(rows_stored[k], stored(n))

        def more(j):
            return not isinstance(j, int) or j < NT

        block = ctx.enter_context(nc.Block())

        @block.sync
        def _(sp):
            def row(name):
                return A[name].rearrange("(a f) -> a f", a=1)

            loads = [(consts[:, :], A["shape_consts"]), (w1a[:, :], A["L0_gnn_W1"][0:D, :]),
                     (b2col[:, :], A["L0_gnn_b2"].rearrange("(f a) -> f a", a=1)),
                     (attn[:, :], A["L2_gnn_w_attn"].rearrange("k a -> a k").to_broadcast([P, W])),
                     (w2[:, :, :], A["L0_gnn_W2"].rearrange("(a p) f -> p a f", a=2)),
                     (wu[:, :, :], A["L0_gnn_Wu"].rearrange("(a p) f -> p a f", a=2)),
                     (wn[:, :, :], A["L1_gnn_w_neighbor"].rearrange("a p f -> p a f")),
                     (wl[:, :, :], A["L1_gnn_w_loop"].rearrange("a p f -> p a f")),
                     (trow, A["tile_numbers"].to_broadcast([P, T]))]
            loads += [(rows256[:, k, :], row(n).to_broadcast([P, HID]))
                      for k, n in enumerate(("L0_gnn_b1", "L0_gnn_g1", "L0_gnn_be1"))]
            loads += [(rows128[:, k, :], row(n).to_broadcast([P, D])) for k, n in enumerate(
                ("L0_gnn_bu", "L0_gnn_gu", "L0_gnn_beu", "L3_gnn_b1", "L3_gnn_b2", "L3_gnn_b3"))]
            loads += [(lin[:, k, :], A[n]) for k, n in enumerate(
                ("L2_gnn_W_lin", "L3_gnn_W1", "L3_gnn_W2", "L3_gnn_W3"))]
            for dst, src in loads:
                with nc.allow_non_contiguous_dma(reason="a column of 128 biases"):
                    sp.dma_start(dst, src).then_inc(weights_in, 16)
            assert len(loads) + 2 == NLOADS
            sp.wait_ge(fill_ready, 1)
            for k in range(2):
                r0 = (k + 1) * RD - ED
                sp.dma_start(w1b_two[k][r0:r0 + ED, :], A["L0_gnn_W1"][D:D + ED, :]).then_inc(weights_in, 16)
            for v, name in ((src_i, "src"), (dst_i, "dst"), (ety_i, "edge_type_460")):
                sp.dma_start(v[0:P - 1, :], A[name][0:(P - 1) * C].rearrange("(p c) -> p c", c=C)).then_inc(edges_in, 16)
                sp.dma_start(v[P - 1:P, 0:LAST], A[name][(P - 1) * C:E].rearrange("(a c) -> a c", a=1)).then_inc(edges_in, 16)
            sp.wait_ge(fill_ready, 2)
            fd = rec_d.rearrange("(p r) w -> p (r w)", p=P)
            fs = rec_s.rearrange("(p r) w -> p (r w)", p=P)
            for k in range(8):
                sp.dma_start(fd[:, k * FILL * RD:(k + 1) * FILL * RD], fill_d).then_inc(fills_done, 16)
                sp.dma_start(fs[:, k * FILL * RS:(k + 1) * FILL * RS], fill_s).then_inc(fills_done, 16)
            for q in range(NE8):
                if q:
                    sp.wait_ge(tanh_dot, q)
                n = CE8
                c0 = q * n
                sp.dma_start(chunk8[0:P - 1, 0:n * W], A["edge_attr_8"][0:(P - 1) * C, :].rearrange("(p c) k -> p (c k)", c=C)[:, c0 * W:(c0 + n) * W]).then_inc(ea8_in, 16)
                m = max(0, min(LAST - c0, n))
                if m:
                    a0 = (P - 1) * C + c0
                    sp.dma_start(chunk8[P - 1:P, 0:m * W], A["edge_attr_8"][a0:a0 + m, :].rearrange("(a c) k -> a (c k)", a=1)).then_inc(ea8_in, 16)
                else:
                    sp.dma_start(chunk8[P - 1:P, 0:W], A["edge_attr_8"][0:1, :]).then_inc(ea8_in, 16)

            ea = A["edge_attr_32"]
            top, mid = 112, P - 1
            ea_top = ea[0:top * C, :].rearrange("(p c) f -> p c f", c=C)
            ea_mid = ea[top * C:mid * C, :].rearrange("(p c) f -> p c f", c=C)
            ea_low = ea[mid * C:E, :].rearrange("(a c) f -> a c f", a=1)

            def feed(j, low):
                for k in range(2):
                    c0 = (2 * j + k) * W
                    wait(sp, scattered[k], 16 * W * j)
                    v = pay_d[k].rearrange("p (c w) -> p c w", c=W)
                    sp.dma_start(v[0:top, :, 4:RD], ea_top[:, bass.ds(c0, W), :]).then_inc(ea_in[k], 16)
                    sp.dma_start(v[top:mid, :, 4:RD], ea_mid[:, bass.ds(c0, W), :]).then_inc(ea_in[k], 16)
                    if low:
                        sp.dma_start(v[mid:P, :, 4:RD], ea_low[:, bass.ds(c0, W), :]).then_inc(ea_in[k], 16)
            feed(0, True)
            with sp.Fori(1, LAST // W // 2) as j:
                feed(j, True)
            with sp.Fori(LAST // W // 2, CT // 2) as j:
                feed(j, False)

            for k in range(2):
                sp.wait_ge(scattered[k], 16 * W * CT // 2)
            rd = rec_d.rearrange("(p r) w -> p (r w)", p=P)
            for q in range(NRB):
                if q:
                    sp.wait_ge(columns_ready, q)
                sp.dma_start(fill_d[:, 0:T // NRB * RD], rd[:, q * (T // NRB) * RD:(q + 1) * (T // NRB) * RD]).then_inc(regrouped, 16)
            sp.wait_ge(sums_added, 2 * TT)
            sp.dma_start(rel_sums[:, :], acc[:, ACCW:2 * ACCW]).then_inc(rel_moved, 16)

            def node_rows(t, j):
                return t[bass.ds(j * B * P, B * P), :].rearrange("(b p) f -> p b f", p=P)

            def seven(v):
                return v.rearrange("p (b f) -> p b f", b=B)

            FULL = B - 1
            NR = N - (NB - 1) * P

            def loads_of(*pairs_):
                def load(j, k):
                    for buf, src in pairs_:
                        sp.dma_start(seven(buf[k]), node_rows(src, j)).then_inc(rows_loaded[k], 16)
                return load

            def load_input(j, k):
                if isinstance(j, int) and j == NT - 1:
                    r0 = j * B * P
                    sp.dma_start(seven(X[k])[:, 0:FULL, :], A["x"][r0:r0 + FULL * P, :].rearrange("(b p) f -> p b f", p=P)).then_inc(rows_loaded[k], 16)
                    sp.dma_start(seven(X[k])[0:NR, FULL, :], A["x"][r0 + FULL * P:N, :]).then_inc(rows_loaded[k], 16)
                else:
                    sp.dma_start(seven(X[k]), node_rows(A["x"], j)).then_inc(rows_loaded[k], 16)

            def to_rows(table, buf):
                return lambda j, k: sp.dma_start(node_rows(table, j), seven(buf[k])).then_inc(rows_stored[k], 16)

            SECOND = {1: 0, 3: 1, 4: 2}

            def stage(n, load, first, second=None):
                def body(m):
                    for k in range(2):
                        j = 2 * m + k
                        sp.wait_ge(result_ready, n * NT + 1 + j)
                        sp.sem_inc(sp_turn)
                        first(j, k)
                        if load is not None and more(j + 2):
                            load(j + 2, k)
                        if second is not None:
                            sp.wait_ge(result2_ready, SECOND[n] * NT + 1 + j)
                            sp.sem_inc(sp_turn)
                            second(j, k)
                if load is not None:
                    load(0, 0)
                    load(1, 1)
                with sp.Fori(0, HALF - 2) as m:
                    body(m)
                body(HALF - 2)
                body(HALF - 1)

            sp.wait_ge(node_sums_read, 1)
            sp.wait_ge(w_ready, 4)
            stage(0, load_input, to_rows(tab_p, WIDE))

            rdt = rec_d.rearrange("(p r) w -> p (r w)", p=P)

            def edge_recs(j):
                for k in range(2):
                    t = 2 * j + k
                    wait(sp, eaT_in_psum, 2 * t - 2)
                    sp.dma_start(recs[k][:, 0:W * RD], rdt[:, bass.ds(t * (W * RD), W * RD)]).then_inc(recs_in[k], 16)
            all_stored(sp, 1)
            loop(sp, TT // 2, edge_recs, peel_first=True)

            sp.wait_ge(sums_added, 4 * TT)
            stage(1, load_input, to_rows(x1, TM2), to_rows(h1, G))

            def rel_back(n):
                sp.wait_ge(sums_copied, n * NT)
                sp.dma_start(acc[:, ACCW:2 * ACCW], rel_sums[:, :]).then_inc(rel_moved, 16)
            sp.wait_ge(rel_moved, 16)
            rel_back(1)
            for k in range(2):
                sp.wait_ge(scattered[k], 16 * W * CT)
            sp.dma_start(acc[:, 0:T * RS], rec_s.rearrange("(p r) w -> p (r w)", p=P)[:, 0:T * RS]).then_inc(regrouped, 16)

            sp.wait_ge(sums_added, 6 * TT)
            stage(2, loads_of((H, h1)), to_rows(h2, TM2))
            rel_back(2)
            sp.wait_ge(sums_added, 8 * TT)
            stage(3, loads_of((H, h2), (X, x1)), to_rows(x2, TM2), to_rows(h4, G))
            sp.wait_ge(sums_added, 10 * TT)
            stage(4, loads_of((X, x2)), to_rows(x3, TM2), to_rows(g1t, G))
            sp.wait_ge(sums_added, 12 * TT)
            stage(5, None, to_rows(g2t, TM2))
            sp.wait_ge(sums_added, 14 * TT)

            def last_rows(j, k):
                if isinstance(j, int) and j == NT - 1:
                    r0 = j * B * P
                    sp.dma_start(out[r0:r0 + FULL * P, :].rearrange("(b p) f -> p b f", p=P), seven(TM2[k])[:, 0:FULL, :]).then_inc(rows_stored[k], 16)
                    sp.dma_start(out[r0 + FULL * P:N, :], seven(TM2[k])[0:NR, FULL, :]).then_inc(rows_stored[k], 16)
                else:
                    sp.dma_start(node_rows(out, j), seven(TM2[k])).then_inc(rows_stored[k], 16)
            stage(6, loads_of((X, x3)), last_rows)
            sp.wait_ge(rows_stored[0], stored(7))
            sp.wait_ge(rows_stored[1], stored(7) + 16)

        @block.gpsimd
        def _(pool):
            def admitted():
                pool.sem_inc(pool_turn)

            pool.wait_ge(fills_done, 16 * 16)

            def scatter(j, rec, pay, words, first, dst):
                for k in range(2):
                    wait(pool, payload_ready, first + 2 * j + k + 1)
                    if dst:
                        wait(pool, ea_in[k], dst(j))
                    admitted()
                    v = pay[k].rearrange("p (c w) -> p c w", c=W)
                    for c in range(W):
                        pool.indirect_dma_start(
                            out=rec[:, :], out_offset=bass.IndirectOffsetOnAxis(ap=row_i[k][:, c:c + 1], axis=0),
                            in_=v[:, c, :], in_offset=None).then_inc(scattered[k], 16)
            lowj = LAST // W // 2
            loop(pool, lowj, lambda j: scatter(j, rec_d, pay_d, RD, 0, lambda j: 48 * (j + 1)))
            with pool.Fori(lowj, CT // 2) as j:
                scatter(j, rec_d, pay_d, RD, 0, lambda j: 48 * lowj + 32 * (j - lowj + 1))
            loop(pool, CT // 2, lambda j: scatter(j, rec_s, pay_s, RS, CT, None))

            def gathers(n, table, nodes, dst, used, g0):
                def copy(i, k):
                    pool.tensor_copy(idx_r[k], nodes[:, bass.ds(i * W, W)]).then_inc(idx_copied, 1)
                wait(pool, idx_copied, n * (TT + 1))
                copy(0, 0)

                def turn2(j):
                    for k in range(2):
                        i = 2 * j + k
                        for h in range(2):
                            wait(pool, used, g0 + 2 * i + h - 1)
                            if h == 1:
                                admitted()
                                copy(i + 1, 1 - k)
                            else:
                                wait(pool, idx_copied, n * (TT + 1) + i + 1)
                                admitted()
                            for c in range(4 * h, 4 * h + 4):
                                pool.indirect_dma_start(
                                    out=dst[:, c, :], out_offset=None, in_=table[:, :],
                                    in_offset=bass.IndirectOffsetOnAxis(ap=idx_r[k][:, c:c + 1], axis=0)).then_inc(gathered[c], 16)
                loop(pool, TT // 2, turn2, peel_first=True)
            pool.wait_ge(columns_ready, NRB)
            pool.wait_ge(carried, 4 * CT)
            for n in range(7):
                if n == 1:
                    all_stored(pool, 1)
                    gathers(1, tab_p, idx, ring3, edge_part, 0)
                    continue
                if n > 1:
                    all_stored(pool, n)
                if n == 5:
                    pool.wait_ge(columns_ready, NRB + 1)
                table, nodes = TABLES[n]
                gathers(n, table, nodes, ring_128, sums_in_psum, 2 * TT * n)

        @block.scalar
        def _(act):
            act.wait_ge(tanh_dot, NE8)
            nc.scalar.activation(tanh_c, tanh_c, ACT.Tanh).then_inc(tanh_ready, 1)

            def tile_sum_copies(g):
                def turn(i):
                    for h in range(2):
                        act.wait_ge(tile_sums_in_psum, 2 * TT * g + 2 * i + h + 1)
                        nc.scalar.copy(tile_sums[:, bass.ds((i * W + 4 * h) * 2, W)], pair[2 + h][:, 0:W]).then_inc(tile_sums_ready, 1)
                loop(act, TT, turn)
                for k in range(2):
                    act.wait_ge(turned_in_psum, 3 * g + k + 2)
                    nc.scalar.copy(turned[:, k * T:k * T + 1024], pair[2][:, :])
                    nc.scalar.copy(turned[:, k * T + 1024:(k + 1) * T], pair[3][:, 0:T - 1024]).then_inc(turned_ready, 1)
                act.wait_ge(turned_ready, 2 * g + 2)
            tile_sum_copies(0)
            act.wait_ge(beta_ready, 1)
            nc.scalar.activation(beta[:, 0:NB], beta[:, 0:NB], ACT.Exp).then_inc(beta_exp, 1)
            act.wait_ge(w_psum, 1)
            nc.scalar.copy(linT[:, :, :].rearrange("p a f -> p (a f)"), pair[3][:, 0:4 * D]).then_inc(w_ready, 1)
            nc.scalar.copy(TMP[:, 0:2 * D], pair[3][:, 512:512 + 2 * D]).then_inc(w_ready, 1)
            act.wait_ge(w_psum, 2)
            nc.scalar.copy(w2u[:, :, :].rearrange("p a f -> p (a f)"), pair[2][:, 0:2 * D]).then_inc(w_ready, 1)
            nc.scalar.copy(vrow[:, :], pair[2][:, 2 * D:3 * D]).then_inc(w_ready, 1)

            def transposed(n, j, k):
                act.wait_ge(hT_in_psum, n * NT + 1 + j)
                nc.scalar.copy(HT[k], pair[0][:, 0:BW]).then_inc(hT_ready, 1)

            def sums(n, j, k, halves, func=ACT.Copy):
                act.wait_ge(product, n * NT + j - 1)
                v = acc2[:, 2 - halves:2, bass.ds(j * BW, BW)]
                to = AG2 if halves == 2 else AG[k]
                nc.scalar.activation(to.rearrange("p (a n) -> p a n", a=halves), v, func).then_inc(sums_copied, 1)

            def stage0(m):
                for k in range(2):
                    wait(act, product, 2 * m + k - 1)
                    transposed(0, 2 * m + k, k)
            loop(act, HALF, stage0, peel_first=True)

            def copy_eaT(q, b):
                act.wait_ge(eaT_in_psum, q + 1)
                wait(act, edge_part, q - 1)
                nc.scalar.copy(eaT[b], pair[3][:, 512 * b:512 * b + 2 * P]).then_inc(eaT_ready, 1)

            def square(q, b):
                act.wait_ge(edge_part, q + 1)
                wait(act, squares, q)
                for c in range(4):
                    last = nc.scalar.activation(cols(sq, c, HID), cols(pair[1 + b], c, HID), ACT.Square, accum_out=ssq[b][:, c:c + 1])
                last.then_inc(squares, 1)

            def tile16(j):
                for s in range(4):
                    q = 4 * j + s
                    if inside(q + 3):
                        copy_eaT(q + 3, (s + 1) % 2)
                    act.wait_ge(z_scaled, q + 1)
                    nc.scalar.activation(zn[s % 2], zn[s % 2], ACT.Gelu).then_inc(gelu_ready, 1)
                    if inside(q + 2):
                        square(q + 2, s % 2)
            all_stored(act, 1)
            copy_eaT(0, 0)
            copy_eaT(1, 1)
            square(0, 0)
            copy_eaT(2, 0)
            square(1, 1)
            loop(act, TT // 2, tile16, peel_first=True, peel_last=True)

            def stage1(m):
                for k in range(2):
                    j = 2 * m + k
                    if more(j + 1):
                        act.wait_ge(product, NT + j)
                        transposed(1, j + 1, 1 - k)
                        act.wait_ge(product, NT + j + 1)
                        sums(1, j + 1, 1 - k, 2)
                    act.wait_ge(pre_gelu, 1 + j)
                    nc.scalar.activation(TMP, TMP, ACT.Gelu).then_inc(post_gelu, 1)
            act.wait_ge(sums_added, 4 * TT)
            sums(1, 0, 0, 2)
            transposed(1, 0, 0)
            loop(act, HALF, stage1, peel_last=True)
            for n in (2, 3):
                act.wait_ge(sums_added, (2 + 2 * n) * TT)

                def stage23(m):
                    for k in range(2):
                        j = 2 * m + k
                        sums(n, j, k, 1)
                        wait(act, product2, (n - 2) * NT + j - 1)
                        transposed(n, j, k)
                loop(act, HALF, stage23, peel_first=True)
            act.wait_ge(sums_added, 10 * TT)

            def stage4(m):
                for k in range(2):
                    j = 2 * m + k
                    if more(j + 1):
                        sums(4, j + 1, 1 - k, 1)
                    act.wait_ge(product2, 2 * NT + j - 1)
                    transposed(4, j, k)
            sums(4, 0, 0, 1)
            loop(act, HALF, stage4, peel_last=True)
            tile_sum_copies(1)
            act.wait_ge(node_sums_read, 2)
            for n in (5, 6):
                act.wait_ge(sums_added, (2 + 2 * n) * TT)

                def stage56(m):
                    for k in range(2):
                        sums(n, 2 * m + k, k, 1, ACT.Relu)
                loop(act, HALF, stage56)

        @block.tensor
        def _(pe):
            mm = nc.tensor.matmul

            def counts(g, i, rows):
                for h in range(2):
                    pe.wait_ge(onehots_ready, 2 * CT * g + 2 * i + h + 1)
                    mm(pair[g][:, 512 * h:512 * h + 512], ones_b[:, :], rows[h], start=isinstance(i, int), stop=False, skip_group_check=True).then_inc(counted, 1)

            def block_numbers(g):
                pe.wait_ge(cmp_ready, g + 1)
                n = T // 4
                for q in range(4):
                    last = mm(pair[2 + q // 2][0:32, 512 * (q % 2):512 * (q % 2) + n], mask_b[:, 0:32], cmp_b[:, q * n:(q + 1) * n], start=True, stop=True)
                last.then_inc(blocks_in_psum, 1)

            def ranks(g):
                g0 = 2 * CT * g
                pe.wait_ge(seeds_ready, g + 1)
                for h in range(2):
                    for s in range(3):
                        mm(pair[0][:, 512 * h:512 * h + 512], ident_b, part[s][:, 512 * h:512 * h + 512], start=s == 0, stop=False, skip_group_check=True)

                def body(i):
                    for h in range(2):
                        pe.wait_ge(rank_onehots, g0 + 2 * i + h + 1)
                        mm(pair[0][:, 512 * h:512 * h + 512], lower_b, oh[h], start=False, stop=False, skip_group_check=True).then_inc(ranks_in_psum, 1)
                    for h in range(2):
                        pe.wait_ge(ranks_read, g0 + 2 * i + h + 1)
                        mm(pair[0][:, 512 * h:512 * h + 512], rest_b, oh[h], start=False, stop=False, skip_group_check=True).then_inc(carried, 1)
                    if g == 0:
                        counts(1, i, oh_s)
                loop(pe, CT, body, peel_first=g == 0)

            loop(pe, CT, lambda i: counts(0, i, oh), peel_first=True)
            for g in range(2):
                block_numbers(g)
                ranks(g)

            def passes(n, g=None):
                g0 = 2 * TT * n

                def turn(i):
                    for h in range(2):
                        pe.wait_ge(sel_ready, g0 + 2 * i + h + 1)
                        if g is not None:
                            wait(pe, tile_sums_ready, 2 * TT * g + 2 * i + h - 1)
                            for c in range(4):
                                last = mm(pair[2 + h][:, 2 * c:2 * c + 2], cols(sel_p[h], c), pairs[:, bass.ds((i * W + 4 * h + c) * 2, 2)], start=True, stop=True)
                            last.then_inc(tile_sums_in_psum, 1)
                        for c in range(4 * h, 4 * h + 4):
                            pe.wait_ge(gathered[c], 16 * (TT * n + i + 1))
                        wait(pe, sums_added, g0 + 2 * i + h - 1)
                        for c in range(4):
                            last = mm(pair[h][:, c * P:(c + 1) * P], ring_128[:, 4 * h + c, :], cols(sel_p[h], c), start=True, stop=True)
                        last.then_inc(sums_in_psum, 1)
                loop(pe, TT, turn, peel_first=True)

            def node_totals(g):
                pe.wait_ge(starts_ready, 2 * g + 1)
                for c in range(TC):
                    last = mm(pair[1][:, c:c + 1], pairs[0:1, c * P:(c + 1) * P], ident[0:1, 0:1], start=True, stop=True)
                last.then_inc(turned_in_psum, 1)
                pe.wait_ge(tile_sums_ready, 2 * TT * (g + 1))
                both = tile_sums.rearrange("p (t k) -> p t k", k=2)
                for k in range(2):
                    if k:
                        pe.wait_ge(turned_ready, 2 * g + 1)
                    for c in range(TC):
                        last = nc.tensor.transpose(pair[2 + c // 8][:, (c % 8) * P:(c % 8 + 1) * P], both[:, c * P:(c + 1) * P, k], ident)
                    last.then_inc(turned_in_psum, 1)
                pe.wait_ge(turned_ready, 2 * g + 2)
                pe.wait_ge(starts_ready, 2 * g + 2)
                for k in range(2):
                    for c in range(TC):
                        last = mm(pair[0][:, 512 * k:512 * k + P], cols(turned[:, k * T:(k + 1) * T], c), cols(work, c), start=c == 0, stop=c == TC - 1)
                last.then_inc(node_sums_in_psum, 1)

            pe.wait_ge(weights_in, 16 * NLOADS)
            pe.wait_ge(blocks_read, 2)
            pe.wait_ge(pairs_ready, 1)
            passes(0, 0)
            node_totals(0)

            pe.wait_ge(node_sums_read, 1)
            for k in range(4):
                nc.tensor.transpose(pair[3][:, k * D:(k + 1) * D], lin[:, k, :], ident)
            for k in range(2):
                last = nc.tensor.transpose(pair[3][:, 512 + k * D:512 + (k + 1) * D], w2[:, k, :], ident)
            last.then_inc(w_psum, 1)
            pe.wait_ge(w_ready, 2)
            for k in range(2):
                mm(pair[2][:, k * D:(k + 1) * D], TMP[:, k * D:(k + 1) * D], wu[:, 1, :], start=True, stop=True)
            pe.wait_ge(b2_spread, 1)
            mm(pair[2][:, 2 * D:3 * D], TMP[:, 2 * D:3 * D], wu[:, 1, :], start=True, stop=True).then_inc(w_psum, 1)

            def transposes(n, j, k):
                wait(pe, hT_ready, n * NT + j)
                for b in range(B):
                    last = nc.tensor.transpose(pair[0][:, b * D:(b + 1) * D], cols(H[k], b), ident)
                last.then_inc(hT_in_psum, 1)

            def times(dst, terms, done):
                for b in range(B):
                    o = dst(b)
                    for t, (lhs, rhs) in enumerate(terms):
                        last = mm(o, cols(lhs, b), rhs, start=t == 0, stop=t == len(terms) - 1)
                last.then_inc(done, 1)

            def wide(b):
                return pair[1 + b // 4][:, (b % 4) * HID:(b % 4 + 1) * HID]

            def narrow(p):
                return lambda b: pair[p][:, b * D:(b + 1) * D]

            def main_product(n, j, k, terms):
                pe.wait_ge(sums_copied, (n - 1) * NT + 1 + j)
                pe.wait_ge(result_ready, n * NT + j - 1)
                times(narrow(1 + 2 * k), terms, product)

            def turn_h(n, at, j, k):
                pe.wait_ge(h_ready, at + 1 + j)
                transposes(n, j, k)

            def stage0(m):
                for k in range(2):
                    j = 2 * m + k
                    if more(j + 1):
                        turn_h(0, 0, j + 1, 1 - k)
                    pe.wait_ge(hT_ready, 1 + j)
                    wait(pe, result_ready, j)
                    times(wide, [(HT[k], w1a[:, :])], product)
            pe.wait_ge(w_ready, 4)
            turn_h(0, 0, 0, 0)
            loop(pe, HALF, stage0, peel_first=True, peel_last=True)

            G1 = 2 * TT

            def sum_edges(q, b):
                pe.wait_ge(gelu_ready, q + 1)
                pe.wait_ge(sel_ready, G1 + q + 1)
                pe.wait_ge(sums_added, G1 + q)
                for a in range(2):
                    for c in range(4):
                        last = mm(pair[0][:, a * 512 + c * P:a * 512 + (c + 1) * P], zn[b][:, c * HID + a * P:c * HID + (a + 1) * P],
                                  cols(sel[b], c), start=True, stop=True)
                last.then_inc(sums_in_psum, 1)

            def turn_features(q, b, t, k):
                pe.wait_ge(recs_in[k], 16 * (t + 1))
                wait(pe, eaT_ready, q - 1)
                for c in range(2):
                    w0 = (4 * b + 2 * c) * RD
                    last = nc.tensor.transpose(pair[3][:, 512 * b + c * P:512 * b + (c + 1) * P], recs[k][:, w0:w0 + P], ident)
                last.then_inc(eaT_in_psum, 1)

            def hidden(q, b, t):
                pe.wait_ge(eaT_ready, q + 1)
                wait(pe, z_free, q - 1)
                for c in range(4 * b, 4 * b + 4):
                    pe.wait_ge(gathered[c], 16 * (TT + t + 1))
                for c in range(4):
                    o = cols(pair[1 + b], c, HID)
                    mm(o, cols(eaT[b], c // 2), w1b_two[c % 2][:, :], start=True, stop=False)
                    last = mm(o, ident, ring3[:, 4 * b + c, :], start=False, stop=True)
                last.then_inc(edge_part, 1)

            def tile16(j):
                for s in range(4):
                    q = 4 * j + s
                    if inside(q - 1):
                        sum_edges(q - 1, (s + 1) % 2)
                    if inside(q + 3):
                        m = (s + 3) // 2
                        turn_features(q + 3, (s + 1) % 2, j + m // 2, m % 2)
                    if inside(q + 2):
                        hidden(q + 2, s % 2, 2 * j + s // 2 + 1)
            pe.wait_ge(rec_ends_clear, 1)
            turn_features(0, 0, 0, 0)
            turn_features(1, 1, 0, 0)
            hidden(0, 0, 0)
            turn_features(2, 0, 0, 1)
            hidden(1, 1, 0)
            loop(pe, TT // 2, tile16, peel_first=True, peel_last=True)
            sum_edges(2 * TT - 1, 1)

            def stage1(m):
                for k in range(2):
                    j = 2 * m + k
                    if more(j + 1):
                        turn_h(1, NT, j + 1, 1 - k)
                    pe.wait_ge(hT_ready, NT + 1 + j)
                    main_product(1, j, k, [(HT[k], wu[:, 0, :]), (AG[0], w2u[:, 0, :]), (AG[1], w2u[:, 1, :])])
            turn_h(1, NT, 0, 0)
            loop(pe, HALF, stage1, peel_last=True)
            passes(2)
            for n in (2, 3):
                def stage23(m):
                    for k in range(2):
                        j = 2 * m + k
                        pe.wait_ge(rows_loaded[k], loaded(n, k, m))
                        transposes(n, j, k)
                        main_product(n, j, k, [(AG[k], wn[:, n - 2, :])])
                        pe.wait_ge(hT_ready, n * NT + 1 + j)
                        wait(pe, product2_read, (n - 2) * NT + j)
                        times(narrow(2), [(HT[k], wl[:, n - 2, :])], product2)
                loop(pe, HALF, stage23, peel_first=True)
                passes(n + 1)

            def stage4(m):
                for k in range(2):
                    j = 2 * m + k
                    if more(j + 1):
                        main_product(4, j + 1, 1 - k, [(AG[1 - k], linT[:, 0, :])])
                    turn_h(4, 2 * NT, j, k)
                    pe.wait_ge(hT_ready, 4 * NT + 1 + j)
                    pe.wait_ge(result2_ready, 2 * NT + j)
                    times(narrow(2), [(HT[k], linT[:, 1, :])], product2)
            main_product(4, 0, 0, [(AG[0], linT[:, 0, :])])
            loop(pe, HALF, stage4, peel_last=True)
            pe.wait_ge(pairs_ready, 2)
            passes(5, 1)
            node_totals(1)
            for n in (5, 6):
                def stage56(m):
                    for k in range(2):
                        main_product(n, 2 * m + k, k, [(AG[k], linT[:, n - 3, :])])
                loop(pe, HALF, stage56)
                if n == 5:
                    passes(6)

        @block.vector
        def _(dve):
            v = nc.vector
            ch = Chain(dve, dve_step)
            link, straight = ch.link, ch.straight

            v.memset(src_i, TRASH * P)
            v.memset(dst_i, TRASH * P)
            v.memset(ety_i, 0)
            v.memset(chunk8, 0.0)
            v.memset(w1b_two[0][:, :], 0.0)
            v.memset(w1b_two[1][:, :], 0.0)
            v.memset(ones_b[:, :], 1.0)
            v.memset(idx[:, T:T + W], 0)
            v.memset(ety[:, T:T + W], 0)
            v.memset(pay_d[0], 0.0)
            v.memset(pay_d[1], 0.0).then_inc(fill_ready, 1)
            straight(v.memset(fill_d, 0.0))
            straight(v.memset(fill_s, 0.0))
            v.memset(fill_d.rearrange("p (r w) -> p r w", w=RD)[:, :, 1], -1.0)
            v.memset(fill_s.rearrange("p (r w) -> p r w", w=RS)[:, :, 1], -1.0).then_inc(fill_ready, 1)
            dve.wait_ge(weights_in, 16 * NLOADS)
            v.tensor_copy(cbf[:, 0:4 * P], consts[:, :])
            straight(v.tensor_scalar(rest_b, lower, -1.0, 1.0, ALU.mult, ALU.add))
            for w in (w1a[:, :], w1b_two[0][:, :], w1b_two[1][:, :], rows256[:, 0, :]):
                s = small[0:w.shape[0], 0:1]
                straight(v.tensor_reduce(s, w, AX, ALU.add))
                straight(v.tensor_scalar(s, s, -1.0 / HID, None, ALU.mult))
                straight(v.tensor_scalar(w, w, s, None, ALU.add))
            dve.wait_ge(edges_in, 16 * 6)
            dve.wait_ge(fills_done, 16 * 16)
            for ids, blk, place in ((dst_i, blk_d, lod), (src_i, blk_s, los)):
                straight(v.tensor_scalar(tcol_i, ids, 7, None, ALU.arith_shift_right))
                straight(v.tensor_copy(blk, tcol_i))
                straight(v.tensor_scalar(tcol_i, ids, P - 1, None, ALU.bitwise_and))
                straight(v.tensor_copy(place, tcol_i))
            attn_b = attn[:, :].rearrange("p (a k) -> p a k", a=1).to_broadcast([P, CE8, W])
            for q in range(NE8):
                dve.wait_ge(ea8_in, 32 * (q + 1))
                m3 = chunk8[:, 0:CE8 * W].rearrange("p (c k) -> p c k", k=W)
                straight(v.tensor_tensor(m3, m3, attn_b, ALU.mult))
                v.tensor_reduce(tanh_c[:, q * CE8:(q + 1) * CE8], m3, AX, ALU.add).then_inc(tanh_dot, 1)

            def onehot(to, h, i, blk):
                for c in range(4):
                    last = v.tensor_scalar(cols(to, c), iota_b, blk[:, bass.ds(i * W + 4 * h + c, 1)], None, ALU.is_equal)
                return last

            def count(g, i, blk, rows):
                for h in range(2):
                    if not (isinstance(i, int) and i == 0):
                        dve.wait_ge(counted, 2 * CT * g + 2 * (i - 1) + h + 1)
                    onehot(rows[h], h, i, blk).then_inc(onehots_ready, 1)

            def plan(g, off):
                dve.wait_ge(counted, 2 * CT * (g + 1))
                straight(v.tensor_copy(cnt, pair[g][:, :]))
                total = ping[0]
                straight(v.tensor_reduce(total, cnt.rearrange("p (k b) -> p b k", k=W), AX, ALU.add))
                ti = base_i[:, 0:P]
                straight(v.tensor_copy(ti, total))
                straight(v.tensor_scalar(ti, ti, P - 1, None, ALU.add))
                straight(v.tensor_scalar(ti, ti, 7, None, ALU.arith_shift_right))
                tiles = cols(base, 1)
                straight(v.tensor_copy(tiles, ti))
                straight(v.memset(tiles[:, NB:P], 0.0))
                straight(v.tensor_copy(ping[0], tiles))
                a = 0
                for s in (1, 2, 4, 8, 16, 32, 64):
                    straight(v.tensor_copy(ping[1 - a][:, 0:s], ping[a][:, 0:s]))
                    straight(v.tensor_tensor(ping[1 - a][:, s:P], ping[a][:, s:P], ping[a][:, 0:P - s], ALU.add))
                    a = 1 - a
                ends, spare = ping[a], ping[1 - a]
                straight(v.tensor_tensor(spare, ends, ident, ALU.mult))
                straight(v.tensor_reduce(small[:, 0:1], spare, AX, ALU.add))
                v.tensor_scalar(cmp_b, trow, small[:, 0:1], None, ALU.is_ge).then_inc(cmp_ready, 1)
                straight(v.tensor_tensor(spare, ends, tiles, ALU.subtract))
                straight(v.tensor_scalar(cols(base, 0), spare, float(P), None, ALU.mult))
                straight(v.memset(cols(base, 0)[:, TRASH:P], float(T * P)))
                for k in range(1, W):
                    straight(v.tensor_tensor(cols(base, k), cols(base, k - 1), cols(cnt, k - 1), ALU.add))
                straight(v.tensor_copy(base_i, base))
                ci = cnt.bitcast(I32)
                for s, bits in enumerate((0xFF, 0xFF00, 0xFF0000)):
                    straight(v.tensor_scalar(ci, base_i, bits, None, ALU.bitwise_and))
                    straight(v.tensor_copy(part[s], ci))
                dve.sem_inc(seeds_ready)
                dve.wait_ge(blocks_in_psum, g + 1)
                n = T // 4
                for q in range(4):
                    last = v.tensor_scalar(off[:, q * n:(q + 1) * n], pair[2 + q // 2][0:32, 512 * (q % 2):512 * (q % 2) + n], float(P), None, ALU.mult)
                last.then_inc(blocks_read, 1)

            def ranks(g, blk, pay, fields, words):
                g0 = 2 * CT * g

                def body(j):
                    for k in range(2):
                        i = 2 * j + k
                        for h in range(2):
                            wait(dve, carried, g0 + 2 * (i - 1) + h + 1)
                            onehot(oh[h], h, i, blk).then_inc(rank_onehots, 1)
                        for h in range(2):
                            dve.wait_ge(ranks_in_psum, g0 + 2 * i + h + 1)
                            v.tensor_tensor(prod[h], oh[h], pair[0][:, 512 * h:512 * h + 512], ALU.mult).then_inc(ranks_read, 1)
                        for h in range(2):
                            dve.wait_ge(ranks_read, g0 + 2 * i + h + 1)
                            link(v.tensor_reduce(pos[:, 4 * h:4 * h + 4], prod[h].rearrange("p (c b) -> p c b", c=4), AX, ALU.add))
                        link(v.tensor_copy(pos_i[0], pos))
                        link(v.tensor_scalar(pos_i[1], pos_i[0], P - 1, None, ALU.bitwise_and))
                        link(v.tensor_scalar(pos_i[2], pos_i[0], 7, None, ALU.arith_shift_right))
                        wait(dve, scattered[k], 16 * W * (CT // 2 * g + j))
                        link(v.scalar_tensor_tensor(out=row_i[k], in0=pos_i[1], scalar=float(ROWS), in1=pos_i[2], op0=ALU.mult, op1=ALU.add))
                        pv = pay[k].rearrange("p (c w) -> p c w", c=W)
                        for w, field in fields:
                            last = v.tensor_copy(pv[:, :, w].bitcast(field.dtype), field[:, bass.ds(i * W, W)])
                        link(last)
                        dve.sem_inc(payload_ready)
                        if g == 0:
                            count(1, i, blk_s, oh_s)
                ch.run(CT // 2, body, 14, peel_first=True)

            dve.wait_ge(tanh_ready, 1)
            loop(dve, CT, lambda i: count(0, i, blk_d, oh), peel_first=True)
            plan(0, off)
            ranks(0, blk_d, pay_d, [(0, src_i), (1, lod), (2, ety_i), (3, tanh_c)], RD)
            plan(1, off_s)
            ranks(1, blk_s, pay_s, [(0, dst_i), (1, los)], RS)

            dve.wait_ge(carried, 4 * CT)
            dve.wait_ge(scattered[0], 16 * W * CT)
            dve.wait_ge(scattered[1], 16 * W * CT)
            n = T // NRB
            pt = pairs.rearrange("p (t k) -> p t k", k=2)
            straight(v.memset(pairs, 1.0))
            for q in range(NRB):
                dve.wait_ge(regrouped, 16 * (q + 1))
                r = fill_d[:, 0:n * RD].rearrange("p (t w) -> p t w", w=RD)
                at = slice(q * n, (q + 1) * n)
                v.tensor_copy(idx[:, at], r[:, :, 0].bitcast(I32))
                v.tensor_copy(loc[:, at], r[:, :, 1])
                v.tensor_copy(pt[:, at, 0], r[:, :, 3])
                v.tensor_copy(ety[:, at], r[:, :, 2].bitcast(I32)).then_inc(columns_ready, 1)
            dve.wait_ge(columns_ready, NRB)
            dve.sem_inc(pairs_ready)
            offs = [dve.alloc_register(f"off{k}") for k in range(W)]

            def choose(dst, i, h):
                for c in range(4):
                    last = v.tensor_scalar(cols(dst, c), iota, loc[:, bass.ds(i * W + 4 * h + c, 1)], None, ALU.is_equal)
                last.then_inc(sel_ready, 1)

            def add_sum(h, c, psum, halves):
                o = dve.snap(offs[4 * h + c], min_val=0, max_val=NB * P)
                if halves == 2:
                    dst = acc2[:, :, bass.ds(o, P)]
                    srcv = psum.rearrange("p (a c n) -> p a c n", a=2, c=4)[:, :, c, :]
                else:
                    dst = acc[:, bass.ds(ACCW + o, P)]
                    srcv = cols(psum, c)
                return v.tensor_tensor(dst, dst, srcv, ALU.add)

            def tiles(n, offset, start):
                g0 = 2 * TT * n
                if start is None:
                    straight(v.memset(acc[:, ACCW:2 * ACCW], 0.0))
                else:
                    dve.wait_ge(rel_moved, start)

                def turn(i):
                    dve.load(offs, offset[0:1, bass.ds(i * W, W)])
                    for h in range(2):
                        wait(dve, sums_in_psum, g0 + 2 * i + h - 1)
                        choose(sel_p[h], i, h)
                    for h in range(2):
                        dve.wait_ge(sums_in_psum, g0 + 2 * i + h + 1)
                        for c in range(4):
                            link(add_sum(h, c, pair[h][:, 0:512], 1))
                        dve.sem_inc(sums_added)
                ch.run(TT, turn, 8, peel_first=True)

            def node_totals(g, offset):
                dve.wait_ge(tile_sums_in_psum, 2 * TT * (g + 1))
                v.tensor_copy(pairs[0:1, 0:T], offset[0:1, :]).then_inc(starts_ready, 1)
                dve.wait_ge(turned_in_psum, 3 * g + 1)
                dve.wait_ge(sums_in_psum, 2 * TT * (1 if g == 0 else 6))
                straight(v.tensor_scalar(tile_block, pair[1][:, 0:TC], 1.0 / P, None, ALU.mult))
                for c in range(TC):
                    last = v.tensor_scalar(cols(work, c), iota, tile_block[:, c:c + 1], None, ALU.is_equal)
                last.then_inc(starts_ready, 1)
                dve.wait_ge(node_sums_in_psum, g + 1)
                both = node_sums[:, :].rearrange("p (k n) -> p k n", k=2)
                straight(v.tensor_copy(both, pair[0][:, :].rearrange("p (k n) -> p k n", k=2)[:, :, 0:P]))
                dve.sem_inc(node_sums_read)

            tiles(0, off, None)
            node_totals(0, off)
            straight(v.memset(beta[:, NB:P], 0.0))
            straight(v.tensor_scalar(beta[:, 0:NB], node_sums[:, 0:NB], 1.0 / N, None, ALU.mult))
            one = beta[:, 0:NB].rearrange("p (b a) -> p b a", a=1)
            straight(v.tensor_reduce(norm_d[:, 0:NB], one, AX, ALU.max))
            v.tensor_tensor(beta[:, 0:NB], beta[:, 0:NB], norm_d[:, 0:NB], ALU.subtract).then_inc(beta_ready, 1)
            dve.wait_ge(beta_exp, 1)
            straight(v.tensor_reduce(norm_d[:, 0:NB], one, AX, ALU.add))
            straight(v.reciprocal(norm_d[:, 0:NB], norm_d[:, 0:NB]))
            straight(v.tensor_tensor(beta[:, 0:NB], beta[:, 0:NB], norm_d[:, 0:NB], ALU.mult))
            straight(v.tensor_copy(deg[:, :], node_sums[:, P:2 * P]))
            straight(v.tensor_scalar(norm_d[:, :], deg[:, :], 1.0, None, ALU.max))
            straight(v.reciprocal(norm_d[:, :], norm_d[:, :]))
            straight(v.tensor_scalar(node_sums[:, 0:P], deg[:, :], 0.0, None, ALU.is_gt))
            straight(v.tensor_tensor(norm_d[:, :], norm_d[:, :], node_sums[:, 0:P], ALU.mult))

            dve.wait_ge(w_ready, 2)
            v.tensor_scalar(TMP[:, 2 * D:3 * D], ident, 0.0, b2col[:, 0:1], ALU.mult, ALU.add).then_inc(b2_spread, 1)
            dve.wait_ge(w_ready, 4)

            def three(x):
                return x.rearrange("p (b f) -> p b f", b=B)

            def per_block(s):
                return s.rearrange("p (b a) -> p b a", a=1).to_broadcast([P, B, D])

            def every(row, width=D):
                return row.rearrange("p (a f) -> p a f", a=1).to_broadcast([P, B, width])

            def rsqrt_steps(y, x, t):
                yield lambda: v.tensor_scalar(t.bitcast(I32), x.bitcast(I32), 1, None, ALU.arith_shift_right)
                yield lambda: v.tensor_scalar(y.bitcast(I32), t.bitcast(I32), -1.0, float(0x5F3759DF), ALU.mult, ALU.add)
                for _ in range(3):
                    yield lambda: v.scalar_tensor_tensor(out=t, in0=y, scalar=-0.5, in1=y, op0=ALU.mult, op1=ALU.mult)
                    yield lambda: v.tensor_tensor(t, t, x, ALU.mult)
                    yield lambda: v.scalar_tensor_tensor(out=y, in0=t, scalar=1.5, in1=y, op0=ALU.add, op1=ALU.mult)
            RSQ = 11
            LN = 7 + RSQ

            def normalise(src, dst, tmp):
                link(v.tensor_reduce(st1, three(src), AX, ALU.add))
                link(v.tensor_scalar(st1, st1, 1.0 / D, None, ALU.mult))
                link(v.tensor_tensor(three(dst), three(src), per_block(st1), ALU.subtract))
                link(v.tensor_tensor(tmp, dst, dst, ALU.mult))
                link(v.tensor_reduce(st2, three(tmp), AX, ALU.add))
                link(v.tensor_scalar(st2, st2, 1.0 / D, EPS, ALU.mult, ALU.add))
                for make in rsqrt_steps(st3, st2, st1):
                    link(make())
                link(v.tensor_tensor(three(dst), three(dst), per_block(st3), ALU.mult))

            def relu_norm(n, j, k, m):
                dve.wait_ge(rows_loaded[k], loaded(n, k, m))
                normalise(X[k], H[k], TMP)
                v.tensor_scalar(H[k], H[k], 0.0, None, ALU.max).then_inc(h_ready, 1)

            def stage0(m):
                for k in range(2):
                    j = 2 * m + k
                    if more(j + 1):
                        relu_norm(0, j + 1, 1 - k, m + k)
                    dve.wait_ge(product, 1 + j)
                    wait(dve, rows_stored[k], stored(0, m))
                    o = WIDE[k].rearrange("p (b f) -> p b f", b=B)
                    b1 = rows256[:, 0:1, :]
                    v.tensor_tensor(o[:, 0:4, :], pair[1][:, :].rearrange("p (b f) -> p b f", b=4), b1.to_broadcast([P, 4, HID]), ALU.add)
                    v.tensor_tensor(o[:, 4:7, :], pair[2][:, 0:3 * HID].rearrange("p (b f) -> p b f", b=3), b1.to_broadcast([P, 3, HID]), ALU.add).then_inc(result_ready, 1)
            ch.part(lambda: relu_norm(0, 0, 0, 0))
            ch.run(HALF, stage0, 2 * LN, peel_first=True, peel_last=True)

            dve.wait_ge(rel_moved, 16)
            straight(v.memset(acc[:, :], 0.0))
            all_stored(dve, 1)
            for k in range(2):
                last = v.memset(recs[k][:, W * RD:], 0.0)
            last.then_inc(rec_ends_clear, 1)
            G1 = 2 * TT

            def deviations(b):
                yield lambda: v.tensor_scalar(rs_x, ssq[b], 1.0 / HID, EPS, ALU.mult, ALU.add)
                yield from rsqrt_steps(rstd[b], rs_x, rs_t)

            def sums_of(h):
                for c in range(4):
                    yield lambda c=c: add_sum(h, c, pair[0][:, :], 2)
                yield sums_added

            def in_turn(*chains):
                chains = [[c, None] for c in chains]
                while chains:
                    for item in list(chains):
                        make = next(item[0], None)
                        if make is None:
                            chains.remove(item)
                            continue
                        if item[1] is not None:
                            ch.after(item[1])
                        if callable(make):
                            item[1] = ch.step(make())
                        else:
                            dve.sem_inc(make)
                ch.after(ch.at + ch.k)

            def shift_and_sum(q, b):
                for c in range(4):
                    o = cols(zn[b], c, HID)
                    yield lambda o=o: v.tensor_tensor(o, o, rows256[:, 2, :], ALU.add)
                yield z_scaled
                if inside(q - 1):
                    dve.wait_ge(sums_in_psum, G1 + q)
                    yield from sums_of(1 - b)

            def tile16(j):
                for s in range(4):
                    q, b = 4 * j + s, s % 2
                    dve.wait_ge(sums_in_psum, G1 + q - 1)
                    for c in range(4):
                        last = v.scalar_tensor_tensor(out=cols(zn[b], c, HID), in0=cols(pair[1 + b], c, HID), scalar=rstd[b][:, c:c + 1], in1=rows256[:, 1, :], op0=ALU.mult, op1=ALU.mult)
                    last.then_inc(z_free, 1)
                    choose(sel[b], 2 * j + s // 2, b)
                    chains = [shift_and_sum(q, b)]
                    if inside(q + 1):
                        dve.wait_ge(squares, q + 2)
                        chains.append(deviations(1 - b))
                    dve.wait_ge(z_free, q + 1)
                    in_turn(*chains)
                    if b == 0:
                        dve.load(offs, off[0:1, bass.ds((2 * j + s // 2) * W, W)])
            dve.wait_ge(squares, 1)
            ch.part(lambda: in_turn(deviations(0)))
            ch.run(TT // 2, tile16, 4 * (4 + 4 + 1 + RSQ), peel_first=True, peel_last=True)
            dve.wait_ge(sums_in_psum, G1 + 2 * TT)
            ch.part(lambda: in_turn(sums_of(1)))

            def stage1(m):
                for k in range(2):
                    j = 2 * m + k
                    if more(j + 1):
                        relu_norm(1, j + 1, 1 - k, m + k)
                    dve.wait_ge(product, NT + 1 + j)
                    dve.wait_ge(h_ready, NT + 1 + j)
                    dve.wait_ge(rows_stored[k], stored(1, m))
                    for b in range(B):
                        last = v.scalar_tensor_tensor(out=cols(TM2[k], b), in0=vrow[:, :], scalar=deg[:, bass.ds(j * B + b, 1)], in1=pair[1 + 2 * k][:, b * D:(b + 1) * D], op0=ALU.mult, op1=ALU.add)
                    link(last)
                    link(v.tensor_tensor(three(TM2[k]), three(TM2[k]), every(rows128[:, 0, :]), ALU.add))
                    normalise(TM2[k], TMP, TM2[k])
                    link(v.tensor_tensor(three(TMP), three(TMP), every(rows128[:, 1, :]), ALU.mult))
                    link(v.tensor_tensor(three(TMP), three(TMP), every(rows128[:, 2, :]), ALU.add))
                    dve.sem_inc(pre_gelu)
                    dve.wait_ge(post_gelu, 1 + j)
                    link(v.tensor_tensor(TM2[k], TMP, H[k], ALU.add))
                    link(v.tensor_tensor(TM2[k], TM2[k], X[k], ALU.add))
                    dve.sem_inc(result_ready)
                    normalise(TM2[k], G[k], TMP)
                    v.tensor_scalar(G[k], G[k], 0.0, None, ALU.max).then_inc(result2_ready, 1)
            ch.part(lambda: relu_norm(1, 0, 0, 0))
            ch.run(HALF, stage1, 2 * (4 * LN - LN + 6), peel_last=True)
            tiles(2, off, 32)

            for n in (2, 3):
                def stage23(m):
                    for k in range(2):
                        j = 2 * m + k
                        dve.wait_ge(product2, (n - 2) * NT + 1 + j)
                        link(v.tensor_copy(TMP, pair[2][:, 0:BW]))
                        dve.sem_inc(product2_read)
                        dve.wait_ge(product, n * NT + 1 + j)
                        for b in range(B):
                            last = v.scalar_tensor_tensor(out=cols(TMP, b), in0=pair[1 + 2 * k][:, b * D:(b + 1) * D], scalar=norm_d[:, bass.ds(j * B + b, 1)], in1=cols(TMP, b), op0=ALU.mult, op1=ALU.add)
                        link(last)
                        dve.wait_ge(rows_stored[k], stored(n, m))
                        if n == 2:
                            link(v.scalar_tensor_tensor(out=TM2[k], in0=TMP, scalar=SLOPE, in1=TMP, op0=ALU.mult, op1=ALU.max))
                            dve.sem_inc(result_ready)
                        else:
                            link(v.scalar_tensor_tensor(out=TM2[k], in0=TMP, scalar=SLOPE, in1=TMP, op0=ALU.mult, op1=ALU.max))
                            dve.wait_ge(rows_loaded[k], loaded(3, k, m))
                            link(v.tensor_tensor(TM2[k], TM2[k], X[k], ALU.add))
                            dve.sem_inc(result_ready)
                            normalise(TM2[k], G[k], TMP)
                            v.tensor_scalar(G[k], G[k], 0.0, None, ALU.max).then_inc(result2_ready, 1)
                ch.run(HALF, stage23, 6 if n == 2 else 8 + 2 * LN)
                all_stored(dve, n + 1)
                if n == 2:
                    tiles(3, off, 48)
                else:
                    dve.wait_ge(sums_copied, n * NT)
                    tiles(4, off, None)

            def mixed(j, k, m):
                dve.wait_ge(rows_loaded[k], loaded(4, k, m))
                dve.wait_ge(product, 4 * NT + 1 + j)
                dve.wait_ge(rows_stored[k], stored(4, m))
                for b in range(B):
                    last = v.scalar_tensor_tensor(out=cols(TM2[k], b), in0=pair[1 + 2 * k][:, b * D:(b + 1) * D], scalar=beta[:, bass.ds(j * B + b, 1)], in1=cols(X[k], b), op0=ALU.mult, op1=ALU.add)
                last.then_inc(result_ready, 1)
                dve.wait_ge(result_ready, 4 * NT + 1 + j)
                normalise(TM2[k], H[k], TMP)
                v.tensor_scalar(H[k], H[k], 0.0, None, ALU.max).then_inc(h_ready, 1)

            def table_rows(j, k):
                dve.wait_ge(product2, 2 * NT + 1 + j)
                v.tensor_tensor(three(G[k]), pair[2][:, 0:BW].rearrange("p (b f) -> p b f", b=B), every(rows128[:, 3, :]), ALU.add).then_inc(result2_ready, 1)

            def stage4(m):
                for k in range(2):
                    j = 2 * m + k
                    mixed(j, k, m)
                    if not (isinstance(j, int) and j == 0):
                        table_rows(j - 1, 1 - k)
            ch.run(HALF, stage4, 2 * LN, peel_first=True)
            table_rows(NT - 1, 1)
            all_stored(dve, 5)
            dve.wait_ge(regrouped, 16 * (NRB + 1))
            dve.wait_ge(idx_copied, 5 * (TT + 1))
            r = acc[:, 0:T * RS].rearrange("p (t w) -> p t w", w=RS)
            v.tensor_copy(idx[:, 0:T], r[:, :, 0].bitcast(I32))
            straight(v.tensor_copy(loc[:, :], r[:, :, 1]))
            straight(v.memset(pairs, 1.0))
            dve.sem_inc(columns_ready)
            dve.sem_inc(pairs_ready)
            dve.wait_ge(sums_copied, 4 * NT)
            tiles(5, off_s, None)
            node_totals(1, off_s)
            straight(v.tensor_scalar(deg[:, :], node_sums[:, P:2 * P], 1.0, None, ALU.max))
            straight(v.reciprocal(deg[:, :], deg[:, :]))
            for n in (5, 6):
                def stage56(m):
                    for k in range(2):
                        j = 2 * m + k
                        if n == 6:
                            dve.wait_ge(rows_loaded[k], loaded(6, k, m))
                        dve.wait_ge(product, n * NT + 1 + j)
                        dve.wait_ge(rows_stored[k], stored(n, m))
                        for b in range(B):
                            last = v.scalar_tensor_tensor(out=cols(TM2[k], b), in0=pair[1 + 2 * k][:, b * D:(b + 1) * D], scalar=deg[:, bass.ds(j * B + b, 1)], in1=rows128[:, n - 1, :], op0=ALU.mult, op1=ALU.add)
                        if n == 6:
                            link(last)
                            last = v.tensor_tensor(TM2[k], TM2[k], X[k], ALU.add)
                        last.then_inc(result_ready, 1)
                ch.run(HALF, stage56, 2 * (n - 5))
                if n == 5:
                    all_stored(dve, 6)
                    dve.wait_ge(sums_copied, 5 * NT)
                    tiles(6, off_s, None)


TC = T // P
CE8 = 112
NE8 = C // CE8
NLOADS = 24
NRB = 8
assert C % CE8 == 0 and T % NRB == 0 and CE8 * W <= W * P

_INS = ['x', 'src', 'dst', 'edge_attr_32', 'edge_attr_8', 'edge_type_460', 'L0_gnn_W1', 'L0_gnn_b1', 'L0_gnn_g1',
        'L0_gnn_be1', 'L0_gnn_W2', 'L0_gnn_b2', 'L0_gnn_Wu', 'L0_gnn_bu', 'L0_gnn_gu', 'L0_gnn_beu',
        'L1_gnn_rel_emb', 'L1_gnn_w_neighbor', 'L1_gnn_w_loop', 'L2_gnn_w_attn', 'L2_gnn_W_lin', 'L3_gnn_W1',
        'L3_gnn_b1', 'L3_gnn_W2', 'L3_gnn_b2', 'L3_gnn_W3', 'L3_gnn_b3']


def kernel(**inputs):
    import numpy as _np
    import concourse.bacc as _bacc
    from concourse import mybir as _mybir
    from concourse.bass_utils import run_bass_kernel_spmd as _run

    nc = _bacc.Bacc("TRN2", target_bir_lowering=False, num_devices=1)
    arrays, aps = {}, {}
    given = {name: _np.ascontiguousarray(inputs[name]) for name in _INS}
    k = _np.arange(P)
    given["shape_consts"] = _np.concatenate(
        [k[:, None] == k, _np.broadcast_to(k, (P, P)), k[:, None] < k, _np.broadcast_to(k[:, None] < NB, (P, P))],
        axis=1).astype(_np.float32)
    given["tile_numbers"] = _np.arange(T, dtype=_np.float32)[None, :]
    for name, a in given.items():
        arrays[f"in_{name}_dram"] = a
        aps[name] = nc.dram_tensor(f"in_{name}_dram", a.shape, _mybir.dt.from_np(a.dtype), kind="ExternalInput").ap()
    out = nc.dram_tensor("out_0_dram", (N, D), F32, kind="ExternalOutput").ap()
    build(nc, aps, out)
    r = _run(nc, [arrays], core_ids=[0])
    return r.results[0]["out_0_dram"]
```
